# Optimizing a Trainium2 kernel written in Bass

```python
import numpy as np
import jax
import jax.numpy as jnp

def _softmax(x, axis=-1):
    return jax.nn.softmax(x, axis=axis)

def _gelu(x):
    return jax.nn.gelu(x, approximate=True)

def _silu(x):
    return jax.nn.silu(x)

def _sigmoid(x):
    return jax.nn.sigmoid(x)

def _layernorm(x, axis=-1, eps=1e-05):
    m = jnp.mean(x, axis=axis, keepdims=True)
    v = jnp.var(x, axis=axis, keepdims=True)
    return (x - m) / jnp.sqrt(v + eps)

def _scatter_add(tgt, idx, src, axis=0):
    return tgt.at[idx].add(src)

def _segment_sum(src, seg, n):
    return jax.ops.segment_sum(src, seg, n)
kernel_name = 'mk_sandwich_d2_jaxref_r8_024935'

def setup_inputs(seed: int=0):
    np.random.seed(seed)
    _w = jnp.asarray

    def _L0_attn_setup():
        import jax, jax.numpy as jnp
        import numpy as np
        import math
        B, L, D, H = (32, 64, 512, 32)
        HD = D // H
        key = jax.random.key(seed)
        ks = jax.random.split(key, 9)
        s = 1.0 / math.sqrt(D)
        return {'x': jax.random.normal(ks[0], (B, L, D), jnp.float32), 'Wq': jax.random.normal(ks[1], (D, D), jnp.float32) * s, 'bq': jax.random.normal(ks[2], (D,), jnp.float32) * s, 'Wk': jax.random.normal(ks[3], (D, D), jnp.float32) * s, 'bk': jax.random.normal(ks[4], (D,), jnp.float32) * s, 'Wv': jax.random.normal(ks[5], (D, D), jnp.float32) * s, 'bv': jax.random.normal(ks[6], (D,), jnp.float32) * s, 'Wo': jax.random.normal(ks[7], (D, D), jnp.float32) * s, 'bo': jax.random.normal(ks[8], (D,), jnp.float32) * s}
    _L0_attn_in = _L0_attn_setup()

    def _L0_ffn_setup():
        import jax, jax.numpy as jnp
        import numpy as np
        B, S, H, I, R = (4, 32, 512, 1792, 4)

        def _anemll_linear(x, w, su, sv):
            w_eff = w * (su @ sv)
            return jnp.einsum('bsh,oh->bso', x, w_eff)
        key = jax.random.key(seed)
        ks = jax.random.split(key, 10)
        sd = 0.02
        return {'x': jax.random.normal(ks[0], (B, S, H), dtype=jnp.float32), 'gate_w': jax.random.normal(ks[1], (I, H), dtype=jnp.float32) * sd, 'gate_su': jax.random.normal(ks[2], (I, R), dtype=jnp.float32) * 0.5, 'gate_sv': jax.random.normal(ks[3], (R, H), dtype=jnp.float32) * 0.5, 'up_w': jax.random.normal(ks[4], (I, H), dtype=jnp.float32) * sd, 'up_su': jax.random.normal(ks[5], (I, R), dtype=jnp.float32) * 0.5, 'up_sv': jax.random.normal(ks[6], (R, H), dtype=jnp.float32) * 0.5, 'down_w': jax.random.normal(ks[7], (H, I), dtype=jnp.float32) * sd, 'down_su': jax.random.normal(ks[8], (H, R), dtype=jnp.float32) * 0.5, 'down_sv': jax.random.normal(ks[9], (R, I), dtype=jnp.float32) * 0.5}
    _L0_ffn_in = _L0_ffn_setup()

    def _L1_attn_setup():
        import jax, jax.numpy as jnp
        import numpy as np
        from jax import lax
        H = 64
        P = 64
        N = 128
        G = 8
        K = 4
        D_MODEL = 512
        I = H * P
        GN = G * N
        CONV_DIM = I + 2 * GN
        PROJ = I + CONV_DIM + H
        EPS = 1e-05
        GROUP_SIZE = I // G

        def _reference_tuple_inner(hidden_states, in_proj_w, conv_weight, conv_bias, dt_bias, A_log, D, norm_weight, out_proj_w):
            B, L, _ = hidden_states.shape
            proj = jnp.einsum('bld,pd->blp', hidden_states, in_proj_w)
            gate = proj[..., :I]
            hbc = proj[..., I:I + CONV_DIM]
            dt = proj[..., -H:]
            pad = jnp.pad(hbc, ((0, 0), (K - 1, 0), (0, 0)))
            conv = conv_bias
            for k in range(K):
                conv = conv + pad[:, k:k + L, :] * conv_weight[:, k]
            xBC = jax.nn.silu(conv)
            x = xBC[..., :I].reshape(B, L, H, P)
            Bm = xBC[..., I:I + GN].reshape(B, L, G, N)
            Cm = xBC[..., I + GN:].reshape(B, L, G, N)
            hpg = H // G
            B_h = jnp.repeat(Bm, hpg, axis=2)
            C_h = jnp.repeat(Cm, hpg, axis=2)
            dt_p = jax.nn.softplus(dt + dt_bias)
            A = -jnp.exp(A_log)
            dA = jnp.exp(dt_p * A)
            dtx = dt_p[..., None] * x

            def step(state, inp):
                dA_t, dtx_t, B_t, C_t = inp
                state = state * dA_t[..., None, None] + dtx_t[..., None] * B_t[:, :, None, :]
                y_t = jnp.einsum('bhpn,bhn->bhp', state, C_t)
                return (state, y_t)
            xs = (jnp.moveaxis(dA, 1, 0), jnp.moveaxis(dtx, 1, 0), jnp.moveaxis(B_h, 1, 0), jnp.moveaxis(C_h, 1, 0))
            state0 = jnp.zeros((B, H, P, N), jnp.float32)
            final_state, ys = lax.scan(step, state0, xs)
            y = jnp.moveaxis(ys, 0, 1) + x * D[None, None, :, None]
            y = y.reshape(B, L, I)
            yg = y.reshape(B, L, G, GROUP_SIZE)
            var = jnp.mean(yg * yg, axis=-1, keepdims=True)
            yn = (yg * lax.rsqrt(var + EPS)).reshape(B, L, I) * norm_weight
            yn = yn * jax.nn.silu(gate)
            out = jnp.einsum('bli,di->bld', yn, out_proj_w)
            conv_state_new = jnp.moveaxis(hbc[:, L - (K - 1):, :], 1, 2)
            return (out, conv_state_new, final_state)
        key = jax.random.key(seed)
        ks = jax.random.split(key, 6)
        B, L = (2, 256)
        s = 0.02
        return {'hidden_states': jax.random.normal(ks[0], (B, L, D_MODEL), jnp.float32), 'in_proj_w': jax.random.normal(ks[1], (PROJ, D_MODEL), jnp.float32) * s, 'conv_weight': jax.random.normal(ks[2], (CONV_DIM, K), jnp.float32) * s, 'conv_bias': jnp.zeros((CONV_DIM,), jnp.float32), 'dt_bias': jnp.ones((H,), jnp.float32), 'A_log': jnp.log(jnp.arange(1, H + 1, dtype=jnp.float32)), 'D': jnp.ones((H,), jnp.float32), 'norm_weight': jnp.ones((I,), jnp.float32), 'out_proj_w': jax.random.normal(ks[3], (D_MODEL, I), jnp.float32) * s}
    _L1_attn_in = _L1_attn_setup()

    def _L1_ffn_setup():
        import jax, jax.numpy as jnp
        import numpy as np
        H = 512
        I = 1376
        B, S = (2, 256)
        key = jax.random.key(seed)
        k1, k2, k3 = jax.random.split(key, 3)
        x = jax.random.normal(k1, (B, S, H), dtype=jnp.float32)
        w_gate_up = jax.random.normal(k2, (2 * I, H), dtype=jnp.float32) * 0.02
        w_down = jax.random.normal(k3, (H, I), dtype=jnp.float32) * 0.02
        return {'x': x, 'w_gate_up': w_gate_up, 'w_down': w_down}
    _L1_ffn_in = _L1_ffn_setup()
    _d = {'L0_attn_x': _L0_attn_in['x'], 'L0_attn_Wq': _L0_attn_in['Wq'], 'L0_attn_bq': _L0_attn_in['bq'], 'L0_attn_Wk': _L0_attn_in['Wk'], 'L0_attn_bk': _L0_attn_in['bk'], 'L0_attn_Wv': _L0_attn_in['Wv'], 'L0_attn_bv': _L0_attn_in['bv'], 'L0_attn_Wo': _L0_attn_in['Wo'], 'L0_attn_bo': _L0_attn_in['bo'], 'L0_ffn_gate_w': _L0_ffn_in['gate_w'], 'L0_ffn_gate_su': _L0_ffn_in['gate_su'], 'L0_ffn_gate_sv': _L0_ffn_in['gate_sv'], 'L0_ffn_up_w': _L0_ffn_in['up_w'], 'L0_ffn_up_su': _L0_ffn_in['up_su'], 'L0_ffn_up_sv': _L0_ffn_in['up_sv'], 'L0_ffn_down_w': _L0_ffn_in['down_w'], 'L0_ffn_down_su': _L0_ffn_in['down_su'], 'L0_ffn_down_sv': _L0_ffn_in['down_sv'], 'L1_attn_in_proj_w': _L1_attn_in['in_proj_w'], 'L1_attn_conv_weight': _L1_attn_in['conv_weight'], 'L1_attn_conv_bias': _L1_attn_in['conv_bias'], 'L1_attn_dt_bias': _L1_attn_in['dt_bias'], 'L1_attn_A_log': _L1_attn_in['A_log'], 'L1_attn_D': _L1_attn_in['D'], 'L1_attn_norm_weight': _L1_attn_in['norm_weight'], 'L1_attn_out_proj_w': _L1_attn_in['out_proj_w'], 'L1_ffn_w_gate_up': _L1_ffn_in['w_gate_up'], 'L1_ffn_w_down': _L1_ffn_in['w_down']}
    _x0 = _d['L0_attn_x']
    _d['L0_attn_x'] = jax.random.normal(jax.random.fold_in(jax.random.key(seed), 1), (2, 1024, 512), dtype=_x0.dtype)
    del _x0
    return _d

def reference(L0_attn_x, L0_attn_Wq, L0_attn_bq, L0_attn_Wk, L0_attn_bk, L0_attn_Wv, L0_attn_bv, L0_attn_Wo, L0_attn_bo, L0_ffn_gate_w, L0_ffn_gate_su, L0_ffn_gate_sv, L0_ffn_up_w, L0_ffn_up_su, L0_ffn_up_sv, L0_ffn_down_w, L0_ffn_down_su, L0_ffn_down_sv, L1_attn_in_proj_w, L1_attn_conv_weight, L1_attn_conv_bias, L1_attn_dt_bias, L1_attn_A_log, L1_attn_D, L1_attn_norm_weight, L1_attn_out_proj_w, L1_ffn_w_gate_up, L1_ffn_w_down):

    def _L0_attn_ref(x, Wq, bq, Wk, bk, Wv, bv, Wo, bo):
        import jax, jax.numpy as jnp
        import numpy as np
        import math
        B, L, D, H = (32, 64, 512, 32)
        HD = D // H
        b, l, d = x.shape
        h, hd = (H, HD)
        q = (x @ Wq.T + bq).reshape(b, l, h, hd).transpose(0, 2, 1, 3)
        k = (x @ Wk.T + bk).reshape(b, l, h, hd).transpose(0, 2, 1, 3)
        v = (x @ Wv.T + bv).reshape(b, l, h, hd).transpose(0, 2, 1, 3)
        scores = jnp.einsum('bhqd,bhkd->bhqk', q, k) / math.sqrt(hd)
        causal = jnp.tril(jnp.ones((l, l), bool))
        scores = jnp.where(causal, scores, -jnp.inf)
        att = jax.nn.softmax(scores, axis=-1)
        out = jnp.einsum('bhqk,bhkd->bhqd', att, v)
        out = out.transpose(0, 2, 1, 3).reshape(b, l, d)
        return out @ Wo.T + bo

    def _L0_ffn_ref(x, gate_w, gate_su, gate_sv, up_w, up_su, up_sv, down_w, down_su, down_sv):
        import jax, jax.numpy as jnp
        import numpy as np
        B, S, H, I, R = (4, 32, 512, 1792, 4)

        def _anemll_linear(x, w, su, sv):
            w_eff = w * (su @ sv)
            return jnp.einsum('bsh,oh->bso', x, w_eff)
        a = _anemll_linear(x, gate_w, gate_su, gate_sv)
        b = _anemll_linear(x, up_w, up_su, up_sv)
        d = jax.nn.silu(a) * b
        return _anemll_linear(d, down_w, down_su, down_sv)

    def _L1_attn_ref(hidden_states, in_proj_w, conv_weight, conv_bias, dt_bias, A_log, D, norm_weight, out_proj_w):
        import jax, jax.numpy as jnp
        import numpy as np
        from jax import lax
        H = 64
        P = 64
        N = 128
        G = 8
        K = 4
        D_MODEL = 512
        I = H * P
        GN = G * N
        CONV_DIM = I + 2 * GN
        PROJ = I + CONV_DIM + H
        EPS = 1e-05
        GROUP_SIZE = I // G

        def _reference_tuple_inner(hidden_states, in_proj_w, conv_weight, conv_bias, dt_bias, A_log, D, norm_weight, out_proj_w):
            B, L, _ = hidden_states.shape
            proj = jnp.einsum('bld,pd->blp', hidden_states, in_proj_w)
            gate = proj[..., :I]
            hbc = proj[..., I:I + CONV_DIM]
            dt = proj[..., -H:]
            pad = jnp.pad(hbc, ((0, 0), (K - 1, 0), (0, 0)))
            conv = conv_bias
            for k in range(K):
                conv = conv + pad[:, k:k + L, :] * conv_weight[:, k]
            xBC = jax.nn.silu(conv)
            x = xBC[..., :I].reshape(B, L, H, P)
            Bm = xBC[..., I:I + GN].reshape(B, L, G, N)
            Cm = xBC[..., I + GN:].reshape(B, L, G, N)
            hpg = H // G
            B_h = jnp.repeat(Bm, hpg, axis=2)
            C_h = jnp.repeat(Cm, hpg, axis=2)
            dt_p = jax.nn.softplus(dt + dt_bias)
            A = -jnp.exp(A_log)
            dA = jnp.exp(dt_p * A)
            dtx = dt_p[..., None] * x

            def step(state, inp):
                dA_t, dtx_t, B_t, C_t = inp
                state = state * dA_t[..., None, None] + dtx_t[..., None] * B_t[:, :, None, :]
                y_t = jnp.einsum('bhpn,bhn->bhp', state, C_t)
                return (state, y_t)
            xs = (jnp.moveaxis(dA, 1, 0), jnp.moveaxis(dtx, 1, 0), jnp.moveaxis(B_h, 1, 0), jnp.moveaxis(C_h, 1, 0))
            state0 = jnp.zeros((B, H, P, N), jnp.float32)
            final_state, ys = lax.scan(step, state0, xs)
            y = jnp.moveaxis(ys, 0, 1) + x * D[None, None, :, None]
            y = y.reshape(B, L, I)
            yg = y.reshape(B, L, G, GROUP_SIZE)
            var = jnp.mean(yg * yg, axis=-1, keepdims=True)
            yn = (yg * lax.rsqrt(var + EPS)).reshape(B, L, I) * norm_weight
            yn = yn * jax.nn.silu(gate)
            out = jnp.einsum('bli,di->bld', yn, out_proj_w)
            conv_state_new = jnp.moveaxis(hbc[:, L - (K - 1):, :], 1, 2)
            return (out, conv_state_new, final_state)
        return _reference_tuple_inner(hidden_states, in_proj_w, conv_weight, conv_bias, dt_bias, A_log, D, norm_weight, out_proj_w)[0]

    def _L1_ffn_ref(x, w_gate_up, w_down):
        import jax, jax.numpy as jnp
        import numpy as np
        H = 512
        I = 1376
        B, S = (2, 256)
        gate_up = jnp.einsum('bsh,oh->bso', x, w_gate_up)
        d = gate_up.shape[-1] // 2
        h = jax.nn.silu(gate_up[..., :d]) * gate_up[..., d:]
        return jnp.einsum('bsi,hi->bsh', h, w_down)
    x = L0_attn_x
    x = x + _layernorm(_L0_attn_ref(_layernorm(x, axis=-1), L0_attn_Wq, L0_attn_bq, L0_attn_Wk, L0_attn_bk, L0_attn_Wv, L0_attn_bv, L0_attn_Wo, L0_attn_bo), axis=-1)
    x = x + _layernorm(_L0_ffn_ref(_layernorm(x, axis=-1), L0_ffn_gate_w, L0_ffn_gate_su, L0_ffn_gate_sv, L0_ffn_up_w, L0_ffn_up_su, L0_ffn_up_sv, L0_ffn_down_w, L0_ffn_down_su, L0_ffn_down_sv), axis=-1)
    x = x + _layernorm(_L1_attn_ref(_layernorm(x, axis=-1), L1_attn_in_proj_w, L1_attn_conv_weight, L1_attn_conv_bias, L1_attn_dt_bias, L1_attn_A_log, L1_attn_D, L1_attn_norm_weight, L1_attn_out_proj_w), axis=-1)
    x = x + _layernorm(_L1_ffn_ref(_layernorm(x, axis=-1), L1_ffn_w_gate_up, L1_ffn_w_down), axis=-1)
    return x

_drawn_inputs = setup_inputs


def setup_inputs(seed=0):
    import zlib

    import numpy as np

    out = dict(_drawn_inputs(seed))
    spreads = {'L1_attn_conv_bias': (0.0, 0.1),
     'L1_attn_dt_bias': (1.0, 0.2),
     'L1_attn_D': (1.0, 0.2),
     'L1_attn_norm_weight': (1.0, 0.2)}
    factors = {}
    for name, (base, spread) in spreads.items():
        noise = np.random.default_rng([zlib.crc32(name.encode()), seed]).standard_normal(out[name].shape)
        drawn = base * np.exp(spread * noise) if base else spread * noise
        out[name] = jnp.asarray(drawn.astype(out[name].dtype))
    for name, factor in factors.items():
        out[name] = (out[name] * factor).astype(out[name].dtype)
    return out
```

```python
from contextlib import ExitStack

import concourse.bass as bass
from concourse import mybir

ALU = mybir.AluOpType
ACT = mybir.ActivationFunctionType
AX = mybir.AxisListType
F32 = mybir.dt.float32
F32R = mybir.dt.float32r
BF16 = mybir.dt.bfloat16

B, L, D = 2, 1024, 512
P = 128
TT = L // P
KT = D // P
HALF = 512
EPS = 1e-5
NEG = -1e30

AH, HD = 32, 16
QUAD = 4
NQ = AH // QUAD
VW = HD + 1
ROWS = 3 * HD

NF0 = 1792 // P
NF1 = (1376 + P - 1) // P
RANK = 4

MH, MP, MN, MG, MK = 64, 64, 128, 8, 4
HPG = MH // MG
GI = HPG * MP
XT = GI // P
CT = XT + 2
UNITS = 2 * MG
CPH = HALF // P
PROJ_AT = [(0, 1), (2,), (3, 4), (5,)]
SPLIT_AT = {1: (0, 1), 2: (2,), 3: (3, 4), 4: (5,)}
W_PER_G = CT + KT + XT
PROJ_PER_B = 2 * CT * MG

START = 1
BARRIERS = 12


def build(nc, x, w_attn, qk_bias, bv, bo, w_ffn0, lr0, lr0_const, w_ffn1,
          w_mamba, w_dt, conv_par, dt_bias, a_log, d_skip, out):
    ctx = ExitStack()
    with ctx:
        def sb(name, shape, dt=F32, stack=ctx):
            return stack.enter_context(nc.sbuf_tensor(name, shape, dt))

        def sem(name):
            return ctx.enter_context(nc.semaphore(name))

        banks = ctx.enter_context(nc.psum_tensor("banks", [P, 8, HALF], F32))
        bank = [banks[:, i, :] for i in range(8)]

        X = sb("X", [P, TT, D])
        Y = sb("Y", [P, TT, D])
        xhi = sb("xhi", [P, KT, L], F32R)
        xlo = sb("xlo", [P, KT, L], F32R)
        ones = sb("ones", [P, P])
        ident = sb("ident", [P, P])
        ident_b = sb("ident_b", [P, P], BF16)
        mask_qk = sb("mask_qk", [P, P], BF16)
        mask_kq = sb("mask_kq", [P, P], BF16)
        upto = sb("upto", [P, P])
        after = sb("after", [P, P])
        after_r = sb("after_r", [P, P], F32R)
        quarter = sb("quarter", [P, P])
        zeros = sb("zeros", [P, MK])
        half_neg = sb("half_neg", [P, TT])
        stats = sb("stats", [P, TT, 6])
        mv = sb("mv", [P, TT, 2])
        var_eps = sb("var_eps", [P, TT])
        rstd = sb("rstd", [P, TT])

        with ExitStack() as s:
            xn = sb("xn", [P, 2, D], stack=s)
        with ExitStack() as s:
            V = sb("V", [P, TT, AH, VW], stack=s)
            with ExitStack() as s2:
                wv_raw = sb("wv_raw", [P, KT, D], stack=s2)
                wv_hi = sb("wv_hi", [P, KT, D], F32R, stack=s2)
                wv_lo = sb("wv_lo", [P, KT, D], F32R, stack=s2)
                bv_sb = sb("bv_sb", [P, D], stack=s2)
            with ExitStack() as s2:
                stack_q = [sb(f"stack_q{i}", [P, QUAD, L], F32R, stack=s2) for i in range(2)]
                stack_k = [sb(f"stack_k{i}", [P, QUAD, L], F32R, stack=s2) for i in range(2)]
                part_hi = sb("part_hi", [P, 2, L], F32R, stack=s2)
                part_lo = sb("part_lo", [P, 2, L], F32R, stack=s2)
                wqk_raw = sb("wqk_raw", [P, 2, D], stack=s2)
                wqk_hi = sb("wqk_hi", [P, 2, D], F32R, stack=s2)
                wqk_lo = sb("wqk_lo", [P, 2, D], F32R, stack=s2)
                qk_b = sb("qk_b", [P, 2], stack=s2)
                probs = [sb(f"probs{i}", [P, QUAD, HALF], stack=s2) for i in range(2)]
                ot = sb("ot", [P, HALF], stack=s2)
                mx = sb("mx", [P, 2, QUAD * TT], stack=s2)
                mt_hi = sb("mt_hi", [QUAD * TT, P], F32R, stack=s2)
                mt_lo = sb("mt_lo", [QUAD * TT, P], F32R, stack=s2)
                rsum = sb("rsum", [P, CPH, QUAD], stack=s2)
        with ExitStack() as s:
            wo_raw = sb("wo_raw", [P, KT, D], stack=s)
            wo_hi = sb("wo_hi", [P, KT, D], F32R, stack=s)
            wo_lo = sb("wo_lo", [P, KT, D], F32R, stack=s)
            bo_sb = sb("bo_sb", [P, D], stack=s)
        with ExitStack() as s:
            f_raw = [sb(f"f_raw{i}", [P, 3, D], stack=s) for i in range(2)]
            f_hi = [sb(f"f_hi{i}", [P, 3, D], F32R, stack=s) for i in range(2)]
            f_lo = [sb(f"f_lo{i}", [P, 3, D], F32R, stack=s) for i in range(2)]
            f_lr = [sb(f"f_lr{i}", [RANK, 3 * P], stack=s) for i in range(2)]
            f_lrc = sb("f_lrc", [RANK, 3 * D], stack=s)
            sg = sb("sg", [P, 2, HALF], stack=s)
            hf = sb("hf", [P, 2, HALF], stack=s)
            h_hi = [sb(f"h_hi{i}", [P, L], F32R, stack=s) for i in range(2)]
            h_lo = [sb(f"h_lo{i}", [P, L], F32R, stack=s) for i in range(2)]
        with ExitStack() as s:
            EC, WE, ED, DTH, AHI, ALO = range(6)
            tab = sb("tab", [P, 6, TT, MH], stack=s)
            d_half = sb("d_half", [P, MH], stack=s)
            with ExitStack() as s2:
                wdt_raw = sb("wdt_raw", [P, KT, MH], stack=s2)
                wdt_hi = sb("wdt_hi", [P, KT, MH], F32R, stack=s2)
                wdt_lo = sb("wdt_lo", [P, KT, MH], F32R, stack=s2)
                dtb = sb("dtb", [P, MH], stack=s2)
                alog = sb("alog", [P, MH], stack=s2)
                neg_a = sb("neg_a", [P, MH], stack=s2)
                dsk = sb("dsk", [P, MH], stack=s2)
                dt_in = sb("dt_in", [P, TT, MH], stack=s2)
                dt_abs = sb("dt_abs", [P, TT, MH], stack=s2)
                dt_sp = sb("dt_sp", [P, TT, MH], stack=s2)
                a_all = sb("a_all", [P, TT, MH], stack=s2)
                a_r = sb("a_r", [P, TT, MH], F32R, stack=s2)
            with ExitStack() as s2:
                m_raw = sb("m_raw", [P, 2, D], stack=s2)
                wx_hi = sb("wx_hi", [P, CT, D], F32R, stack=s2)
                wx_lo = sb("wx_lo", [P, CT, D], F32R, stack=s2)
                wg_hi = sb("wg_hi", [P, KT, D], F32R, stack=s2)
                wg_lo = sb("wg_lo", [P, KT, D], F32R, stack=s2)
                wy_hi = sb("wy_hi", [P, XT, D], F32R, stack=s2)
                wy_lo = sb("wy_lo", [P, XT, D], F32R, stack=s2)
                cpar = sb("cpar", [P, CT * (MK + 1) + XT], stack=s2)
                gt = sb("gt", [P, 6, TT, HPG], stack=s2)
                gd = sb("gd", [P, HPG], stack=s2)
                xbc = [sb(f"xbc{i}", [P, CT, HALF], stack=s2) for i in range(2)]
                pre = [sb(f"pre{i}", [P, MK - 1 + HALF], stack=s2) for i in range(2)]
                carry = sb("carry", [P, CT, MK - 1], stack=s2)
                conv = [sb(f"conv{i}", [P, HALF], stack=s2) for i in range(2)]
                x_tm = sb("x_tm", [P, GI], stack=s2)
                b_tm = sb("b_tm", [P, MN], stack=s2)
                cb = sb("cb", [P, P], stack=s2)
                au_hi = sb("au_hi", [P, HPG, P], F32R, stack=s2)
                au_lo = sb("au_lo", [P, HPG, P], F32R, stack=s2)
                decay = sb("decay", [P, HPG, P], stack=s2)
                xdt = sb("xdt", [P, GI], stack=s2)
                xw = sb("xw", [P, GI], stack=s2)
                xd = sb("xd", [P, GI], stack=s2)
                state = sb("state", [P, GI], stack=s2)
                g_th = sb("g_th", [P, GI], stack=s2)
                yv = sb("yv", [P, GI], stack=s2)
                ss = sb("ss", [P, 1], stack=s2)
                rg = sb("rg", [P, 1], stack=s2)
                yn = sb("yn", [P, GI], stack=s2)
                yt_hi = sb("yt_hi", [P, XT, P], F32R, stack=s2)
                yt_lo = sb("yt_lo", [P, XT, P], F32R, stack=s2)

        consts_ready = sem("consts_ready")
        phase_end = sem("phase_end")
        held_waits = sem("held_waits")
        x_in = sem("x_in")
        out_done = sem("out_done")
        post_var, post_rstd = sem("post_var"), sem("post_rstd")
        pre_var, pre_rstd = sem("pre_var"), sem("pre_rstd")
        xn_ready, xt_done, xt_hi, xt_free = (sem(n) for n in ("xn_ready", "xt_done", "xt_hi", "xt_free"))
        wv_in, wv_ready, v_done, v_free = (sem(n) for n in ("wv_in", "wv_ready", "v_done", "v_free"))
        wo_in, wo_ready, at_done, at_hi, at_free, o_done, o_free = (
            sem(n) for n in ("wo_in", "wo_ready", "at_done", "at_hi", "at_free", "o_done", "o_free"))
        wqk_in, wqk_ready, wqk_used = sem("wqk_in"), sem("wqk_ready"), sem("wqk_used")
        ring_done, ring_free = sem("ring_done"), sem("ring_free")
        part_hi_ready, part_lo_ready = sem("part_hi_ready"), sem("part_lo_ready")
        stacked = [sem("stacked0"), sem("stacked1")]
        ones_rows = sem("ones_rows")
        mx_ready, misc_done, misc_free = sem("mx_ready"), sem("misc_done"), sem("misc_free")
        mt_ready, mt_in = sem("mt_ready"), sem("mt_in")
        st_done = [sem("st_done0"), sem("st_done1")]
        exp_done = [sem("exp_done0"), sem("exp_done1")]
        pv_done, ot_ready, o_zero = sem("pv_done"), sem("ot_ready"), sem("o_zero")
        F = [{n: sem(f"{n}_{i}") for n in (
            "raw_in0", "raw_in1", "lr_const", "lr_done", "weff", "w_ready", "g_done", "u_done", "sg_done",
            "hf_done", "hi_done", "h_ready", "dn_done", "dn_used", "y_zero")}
            for i in range(2)]
        dt_w_in, dt_w_ready, dt_mm, dt_sum, dt_soft, dt_a, dt_cs, dt_exp = (
            sem(n) for n in ("dt_w_in", "dt_w_ready", "dt_mm", "dt_sum", "dt_soft", "dt_a", "dt_cs", "dt_exp"))
        m_raw_in = [sem("m_raw_in0"), sem("m_raw_in1")]
        m_split, cpar_in = sem("m_split"), sem("cpar_in")
        gt_ready, m_zero = sem("gt_ready"), sem("m_zero")
        proj_done, gate_done = sem("proj_done"), sem("gate_done")
        pre_ready, conv_ready, cth_ready, xbc_ready = (
            sem(n) for n in ("pre_ready", "conv_ready", "cth_ready", "xbc_ready"))
        gate_th, gate_used = sem("gate_th"), sem("gate_used")
        xtr_done, x_tm_ready = sem("xtr_done"), sem("x_tm_ready")
        bc_done, bc_ready = sem("bc_done"), sem("bc_ready")
        au_ready, d_done, decay_ready, m_ready = (sem(n) for n in ("au_ready", "d_done", "decay_ready", "m_ready"))
        pool_x = sem("pool_x")
        inter_done, inter_used, intra_done, y_ready = (
            sem(n) for n in ("inter_done", "inter_used", "intra_done", "y_ready"))
        ss_ready, rg_ready, yn_ready = sem("ss_ready"), sem("rg_ready"), sem("yn_ready")
        yt_done, yt_hi_ready, yt_ready, mo_done, mo_used = (
            sem(n) for n in ("yt_done", "yt_hi_ready", "yt_ready", "mo_done", "mo_used"))
        st_mm, state_ready, state_dec = sem("st_mm"), sem("state_ready"), sem("state_dec")

        started = [misc_free, *exp_done, ot_ready, mt_in, gate_used, gate_done, yn_ready, yt_ready, x_tm_ready,
                   bc_ready, d_done, decay_ready, pool_x, inter_done, inter_used, intra_done, y_ready, ss_ready,
                   mo_done, mo_used, st_mm]

        block = ctx.enter_context(nc.Block())

        def held(eng, semaphore, value):
            eng.wait_ge(semaphore, value)
            eng.sem_inc(held_waits, 1)

        def barrier(eng, b, k):
            eng.drain().then_inc(phase_end, 1)
            held(eng, phase_end, b * (5 * BARRIERS) + 5 * (k + 1))

        STEPS = [(s, j) for s in range(2) for j in range(CPH * (s + 1))]
        PIECES = [(h, i, s, min((i + 1) * P - s * HALF, HALF), s == i // CPH)
                  for h in range(QUAD) for i in range(TT) for s in range(i // CPH + 1)]
        NS, NP = len(STEPS), len(PIECES)
        RING = 4 * (NQ // 2) + NQ * NP
        STACKED = 16 * 6 * QUAD
        AHEAD = 12

        def attention_order():
            yield "proj", 0
            yield "proj", 1
            for n in range(NP):
                yield "piece", 0, n
            yield "maxima", 0
            for n in range(AHEAD):
                yield "piece", 1, n
            for t in range(NQ):
                if t in (1, 3):
                    yield "proj", (t + 3) // 2
                if t > 0 and t + 1 < NQ:
                    for n in range(AHEAD):
                        yield "piece", t + 1, n
                at = AHEAD
                for n in range(NS):
                    yield "scores", t, n
                    if t + 1 < NQ:
                        for _ in range(4):
                            if at < NP:
                                yield "piece", t + 1, at
                                at += 1
                    if n > 0:
                        yield "values", t, n - 1
                    if n == 1 and t > 0:
                        yield "turn", t - 1, 1
                    if n == 7:
                        yield "turn", t, 0
                    if n == 10 and t + 1 < NQ:
                        yield "maxima", t + 1
                yield "values", t, NS - 1
            yield "turn", NQ - 1, 1

        ORDER = list(attention_order())

        def m_uses(last):
            uses = []
            for c in range(TT):
                s = c // CPH
                if not (last and s == 1):
                    uses += [("proj", s * CT + ft) for ft in PROJ_AT[c % CPH]]
                uses.append(("gate", c))
            return uses

        @block.sync
        def _(sp):
            sp.wait_ge(consts_ready, 1)
            with sp.Fori(0, B) as b:
                sp.dma_start(X[:], x[b].rearrange("(t p) d -> p t d", p=P)).then_inc(x_in, 16)
                barrier(sp, b, 0)
                sp.dma_start(wv_raw[:], w_attn[0:KT].rearrange("n p c -> p n c")).then_inc(wv_in, 16)
                sp.dma_start(bv_sb[:], bv).then_inc(wv_in, 16)
                barrier(sp, b, 1)
                for i in range(2):
                    for row in (ROWS, ROWS + 1, 64 + ROWS, 64 + ROWS + 1):
                        sp.dma_start(stack_k[i][row:row + 1, :, :].bitcast(F32), ones[0:QUAD * TT, :]
                                     ).then_inc(ones_rows, 16)

                def load_qk(f):
                    if f > 0:
                        held(sp, wqk_ready, b * 8 + 2 * f)
                        held(sp, part_lo_ready, b * 16 + 4 * f)
                    sp.dma_start(wqk_raw[:], w_attn[KT + 2 * f:KT + 2 * f + 2].rearrange("n p c -> p n c")
                                 ).then_inc(wqk_in, 16)
                    sp.dma_start(qk_b[:], qk_bias[f]).then_inc(wqk_in, 16)

                def stack(t):
                    f, par = t // 2, t % 2
                    held(sp, part_hi_ready, b * 16 + 4 * f + 4)
                    held(sp, part_lo_ready, b * 16 + 4 * f + 4)
                    if t >= 4:
                        held(sp, pv_done, b * (NQ * NS) + (t - 3) * NS)
                    for h in range(QUAD):
                        src = slice(HD * (QUAD * par + h), HD * (QUAD * par + h + 1))
                        for dst, which, parts in ((stack_q[f % 2], 0, (part_hi, part_hi, part_lo)),
                                                  (stack_k[f % 2], 1, (part_hi, part_lo, part_hi))):
                            for r, part in enumerate(parts):
                                at = 64 * par + HD * r
                                sp.dma_start(dst[at:at + HD, h, :].bitcast(F32),
                                             part[src, which, :].bitcast(F32)).then_inc(stacked[par], 16)

                def put_maxima(t):
                    held(sp, mt_ready, b * NQ + t + 1)
                    for r, part in ((0, mt_hi), (1, mt_lo)):
                        at = 64 * (t % 2) + ROWS + r
                        sp.dma_start(stack_q[t // 2 % 2][at:at + 1, :, :].bitcast(F32),
                                     part[:].bitcast(F32)).then_inc(mt_in, 16)

                load_qk(0)
                stack(0)
                stack(1)
                load_qk(1)
                stack(2)
                stack(3)
                put_maxima(0)
                load_qk(2)
                put_maxima(1)
                stack(4)
                put_maxima(2)
                stack(5)
                load_qk(3)
                put_maxima(3)
                stack(6)
                put_maxima(4)
                stack(7)
                for t in range(5, NQ):
                    put_maxima(t)
                barrier(sp, b, 2)
                sp.dma_start(wo_raw[:], w_attn[3 * KT:4 * KT].rearrange("n p c -> p n c")).then_inc(wo_in, 16)
                sp.dma_start(bo_sb[:], bo).then_inc(wo_in, 16)
                barrier(sp, b, 3)
                barrier(sp, b, 4)

                def ffn_loads(i, w, n, lowrank):
                    f = F[i]

                    def load(p, par, first):
                        t = p * 2 + par
                        if not first:
                            held(sp, f["w_ready"], (b * n + t) * 3 - 3)
                        sp.dma_start(f_raw[par][:], w[t].rearrange("m p c -> p m c")).then_inc(f[f"raw_in{par}"], 16)
                        if lowrank:
                            sp.dma_start(f_lr[par][:], lr0[t]).then_inc(f[f"raw_in{par}"], 16)

                    load(0, 0, True)
                    load(0, 1, True)
                    with sp.Fori(1, n // 2) as p:
                        for par in range(2):
                            load(p, par, False)
                    if n % 2:
                        load(n // 2, 0, False)

                sp.dma_start(f_lrc[:], lr0_const).then_inc(F[0]["lr_const"], 16)
                ffn_loads(0, w_ffn0, NF0, True)
                barrier(sp, b, 5)
                barrier(sp, b, 6)
                for dst, src in ((wdt_raw[:], w_dt), (dtb[:], dt_bias), (alog[:], a_log), (dsk[:], d_skip)):
                    sp.dma_start(dst, src).then_inc(dt_w_in, 16)
                barrier(sp, b, 7)

                def m_load(g, at, use, first=False):
                    if not first:
                        held(sp, m_split, b * (MG * W_PER_G) + use - 1)
                    sp.dma_start(m_raw[:, at % 2, :], w_mamba[g, at]).then_inc(m_raw_in[at % 2], 16)

                sp.dma_start(cpar[:], conv_par[0]).then_inc(cpar_in, 16)
                for n in range(CT):
                    m_load(0, n, n, n < 2)

                def m_group(g, last):
                    for n in range(CT, W_PER_G):
                        m_load(g, n, g * W_PER_G + n)
                    if not last:
                        for n in range(CT - 1):
                            m_load(g + 1, n, g * W_PER_G + (W_PER_G + n))
                        held(sp, conv_ready, b * PROJ_PER_B + g * (2 * CT) + 2 * CT)
                        held(sp, m_split, b * (MG * W_PER_G) + g * W_PER_G + W_PER_G)
                        sp.dma_start(cpar[:], conv_par[g + 1]).then_inc(cpar_in, 16)
                        m_load(g + 1, CT - 1, g * W_PER_G + (W_PER_G + CT - 1))

                with sp.Fori(0, MG - 1) as g:
                    m_group(g, False)
                m_group(MG - 1, True)
                barrier(sp, b, 8)
                barrier(sp, b, 9)
                ffn_loads(1, w_ffn1, NF1, False)
                barrier(sp, b, 10)
                barrier(sp, b, 11)
                sp.dma_start(out[b].rearrange("(t p) d -> p t d", p=P), X[:]).then_inc(out_done, 16)
                held(sp, out_done, b * 16 + 16)

        @block.tensor
        def _(pe):
            pe.wait_ge(consts_ready, 1)

            def three(dst, a_hi, a_lo, w_hi, w_lo, kt, first, last):
                pe.matmul(dst, a_hi(kt), w_hi(kt), start=first, stop=False)
                pe.matmul(dst, a_lo(kt), w_hi(kt), start=False, stop=False)
                return pe.matmul(dst, a_hi(kt), w_lo(kt), start=False, stop=last)

            def tokens(dst, i, w_hi, w_lo, cols=None):
                tok = slice(i * P, (i + 1) * P)
                for kt in range(KT):
                    r = three(dst, lambda k: xhi[:, k, tok], lambda k: xlo[:, k, tok],
                              lambda k: w_hi[:, k, :], lambda k: w_lo[:, k, :], kt, kt == 0, kt == KT - 1)
                return r

            def features(dst, w_hi, w_lo, s):
                tok = slice(s * HALF, (s + 1) * HALF)
                for kt in range(KT):
                    r = three(dst, lambda k: w_hi[:, k * P:(k + 1) * P], lambda k: w_lo[:, k * P:(k + 1) * P],
                              lambda k: xhi[:, k, tok], lambda k: xlo[:, k, tok], kt, kt == 0, kt == KT - 1)
                return r

            def norm_turn(e):
                for i in range(TT):
                    pe.wait_ge(xn_ready, e * TT + i + 1)
                    if i >= 2:
                        pe.wait_ge(xt_free, e * TT + i - 1)
                    for k in range(KT):
                        r = pe.transpose(bank[i % 2][:, k * P:(k + 1) * P], xn[:, i % 2, k * P:(k + 1) * P],
                                         ident[:])
                    r.then_inc(xt_done, 1)

            def ffn(b, i, n, lowrank):
                f = F[i]

                def factors(p, par, first=False):
                    t = p * 2 + par
                    pe.wait_ge(f[f"raw_in{par}"], (b * ((n + 1 - par) // 2) + p) * 32 + 32)
                    for m in range(3):
                        dst = bank[4 + (3 * par + m) % 2]
                        if not (first and m < 2):
                            pe.wait_ge(f["weff"], (b * n + t) * 3 + m - 1)
                        if m < 2:
                            for k in range(KT):
                                r = pe.matmul(dst[:, k * P:(k + 1) * P],
                                              f_lrc[:, m * D + k * P:m * D + (k + 1) * P],
                                              f_lr[par][:, m * P:(m + 1) * P], start=True, stop=True,
                                              skip_group_check=True)
                        else:
                            r = pe.matmul(dst[:], f_lr[par][:, 2 * P:3 * P], f_lrc[:, 2 * D:3 * D],
                                          start=True, stop=True)
                        r.then_inc(f["lr_done"], 1)

                def gate_up(t, par, first=False):
                    pe.wait_ge(f["w_ready"], (b * n + t) * 3 + 2)
                    for s in range(2):
                        if not first:
                            pe.wait_ge(f["hf_done"], (b * n + t) * 2 + s - 1)
                        features(bank[2 * s][:], f_hi[par][:, 0, :], f_lo[par][:, 0, :], s).then_inc(f["g_done"], 1)
                        features(bank[2 * s + 1][:], f_hi[par][:, 1, :], f_lo[par][:, 1, :], s
                                 ).then_inc(f["u_done"], 1)

                def down(t, par, first=False):
                    pe.wait_ge(f["w_ready"], (b * n + t) * 3 + 3)
                    pe.wait_ge(f["h_ready"], (b * n + t) * 2 + 2)
                    for i in range(TT):
                        if not (first and i < 2):
                            pe.wait_ge(f["dn_used"], (b * n + t) * TT + i - 1)
                        tok = slice(i * P, (i + 1) * P)
                        three(bank[6 + i % 2][:], lambda k: h_hi[par][:, tok], lambda k: h_lo[par][:, tok],
                              lambda k: f_hi[par][:, 2, :], lambda k: f_lo[par][:, 2, :], 0, True, True
                              ).then_inc(f["dn_done"], 1)

                def step(p, par, more2, more1, first=False):
                    t = p * 2 + par
                    if more2 and lowrank:
                        factors(p + 1, par)
                    if more1:
                        gate_up(t + 1, 1 - par)
                    down(t, par, first)

                if lowrank:
                    pe.wait_ge(f["lr_const"], b * 16 + 16)
                    factors(0, 0, True)
                    factors(0, 1)
                gate_up(0, 0, True)
                step(0, 0, True, True, True)
                step(0, 1, True, True)
                with pe.Fori(1, (n - 2) // 2) as p:
                    for par in range(2):
                        step(p, par, True, True)
                for t in range((n - 2) // 2 * 2, n):
                    step(t // 2, t % 2, t + 2 < n, t + 1 < n)

            with pe.Fori(0, B) as b:
                norm_turn(b * 4)
                barrier(pe, b, 0)
                pe.wait_ge(wv_ready, b + 1)
                for i in range(TT):
                    if i >= 2:
                        pe.wait_ge(v_free, b * TT + i - 1)
                    tokens(bank[i % 2][:], i, wv_hi, wv_lo).then_inc(v_done, 1)
                barrier(pe, b, 1)
                pe.wait_ge(ones_rows, (b + 1) * (16 * 8))
                pe.wait_ge(o_zero, b + 1)
                ring = 0
                misc = 0
                for what, *arg in ORDER:
                    if what == "proj":
                        f, = arg
                        pe.wait_ge(wqk_ready, b * 8 + 2 * f + 2)
                        for which in range(2):
                            for s in range(2):
                                if ring >= 2:
                                    pe.wait_ge(ring_free, b * RING + ring - 1)
                                features(bank[4 + ring % 2][:], wqk_hi[:, which, :], wqk_lo[:, which, :], s
                                         ).then_inc(ring_done, 1)
                                ring += 1
                    elif what == "piece":
                        t, n = arg
                        h, i, s, cols, diag = PIECES[n]
                        base, buf = 64 * (t % 2), t // 2 % 2
                        if n == 0:
                            pe.wait_ge(stacked[t % 2], (b * (NQ // 2) + t // 2 + 1) * STACKED)
                        pe.wait_ge(ring_free, b * RING + ring - 1)
                        dst = bank[4 + ring % 2]
                        r = pe.matmul(dst[:, 0:cols], stack_q[buf][base:base + ROWS, h, i * P:(i + 1) * P],
                                      stack_k[buf][base:base + ROWS, h, s * HALF:s * HALF + cols],
                                      start=True, stop=True)
                        if diag:
                            r = pe.matmul(dst[:, cols - P:cols], ident_b[:], mask_qk[:], start=False, stop=True,
                                          skip_group_check=True)
                        r.then_inc(ring_done, 1)
                        ring += 1
                    elif what == "maxima":
                        t, = arg
                        pe.wait_ge(mx_ready, b * NQ + t + 1)
                        pe.wait_ge(misc_free, START + b * (3 * NQ) + misc)
                        pe.transpose(bank[7][0:QUAD * TT, 0:P], mx[:, 0, :], ident[:]).then_inc(misc_done, 1)
                        misc += 1
                    elif what == "scores":
                        t, n = arg
                        s, j = STEPS[n]
                        lo = max(j * P - s * HALF, 0)
                        base, buf = 64 * (t % 2), t // 2 % 2
                        it = b * (NQ * NS) + (t * NS + n)
                        if n == 0:
                            pe.wait_ge(mt_in, START + (b * NQ + t + 1) * 32)
                        diag = j * P >= s * HALF
                        for p in range(2):
                            pe.wait_ge(exp_done[p], START + it)
                            for hh in range(2):
                                h = 2 * p + hh
                                dst = bank[2 * p + hh]
                                r = pe.matmul(dst[:, 0:HALF - lo],
                                              stack_k[buf][base:base + ROWS + 2, h, j * P:(j + 1) * P],
                                              stack_q[buf][base:base + ROWS + 2, h, s * HALF + lo:(s + 1) * HALF],
                                              start=True, stop=True)
                                if diag:
                                    r = pe.matmul(dst[:, 0:P], ident_b[:], mask_kq[:], start=False, stop=True,
                                                  skip_group_check=True)
                            r.then_inc(st_done[p], 1)
                    elif what == "values":
                        t, n = arg
                        s, j = STEPS[n]
                        lo = max(j * P - s * HALF, 0)
                        it = b * (NQ * NS) + (t * NS + n)
                        if j == 0:
                            pe.wait_ge(ot_ready, START + b * (2 * NQ) + 2 * t + s)
                        for p in range(2):
                            pe.wait_ge(exp_done[p], START + it + 1)
                        for h in range(QUAD):
                            r = pe.matmul(bank[6][32 * h:32 * h + VW, lo:HALF], V[:, j, QUAD * t + h, :],
                                          probs[n % 2][:, h, 0:HALF - lo], start=j == 0,
                                          stop=j == CPH * (s + 1) - 1, skip_group_check=True,
                                          tile_position=(0, 32 * h))
                        r.then_inc(pv_done, 1)
                    elif what == "turn":
                        t, s = arg
                        pe.wait_ge(ot_ready, START + b * (2 * NQ) + 2 * t + s + 1)
                        pe.wait_ge(misc_free, START + b * (3 * NQ) + misc)
                        for k in range(CPH):
                            r = pe.transpose(bank[7][:, k * P:(k + 1) * P], ot[:, k * P:(k + 1) * P], ident[:])
                        r.then_inc(misc_done, 1)
                        misc += 1
                barrier(pe, b, 2)
                for i in range(TT + 1):
                    if i < TT:
                        if i >= 2:
                            pe.wait_ge(at_free, b * TT + i - 1)
                        for k in range(KT):
                            r = pe.transpose(bank[2 + i % 2][:, k * P:(k + 1) * P], Y[:, i, k * P:(k + 1) * P],
                                             ident[:])
                        r.then_inc(at_done, 1)
                    if i > 0:
                        if i == 1:
                            pe.wait_ge(wo_ready, b + 1)
                        pe.wait_ge(at_free, b * TT + i)
                        if i >= 3:
                            pe.wait_ge(o_free, b * TT + i - 2)
                        tokens(bank[(i - 1) % 2][:], i - 1, wo_hi, wo_lo).then_inc(o_done, 1)
                barrier(pe, b, 3)
                norm_turn(b * 4 + 1)
                barrier(pe, b, 4)
                ffn(b, 0, NF0, True)
                barrier(pe, b, 5)
                norm_turn(b * 4 + 2)
                barrier(pe, b, 6)
                pe.wait_ge(dt_w_ready, b + 1)
                for i in range(TT):
                    tokens(bank[0][:, i * MH:(i + 1) * MH], i, wdt_hi, wdt_lo).then_inc(dt_mm, 1)
                pe.wait_ge(dt_a, b + 1)
                for k, m in enumerate((upto, after, ones)):
                    pe.matmul(bank[1 + k][:], m[:], a_all[:].rearrange("p c h -> p (c h)"), start=True, stop=True
                              ).then_inc(dt_cs, 1)
                barrier(pe, b, 7)

                def project(g, s, ft):
                    pe.wait_ge(m_split, b * (MG * W_PER_G) + g * W_PER_G + (ft + 1))
                    features(bank[ft % 2][:], wx_hi[:, ft, :], wx_lo[:, ft, :], s).then_inc(proj_done, 1)

                def bank_read(g, at, uses):
                    if at < 2:
                        pe.wait_ge(pre_ready, b * PROJ_PER_B + CT + g * (2 * CT))
                        pe.wait_ge(gate_used, START + (b * MG + g) * TT)
                        return
                    kind, n = uses[at - 2]
                    if kind == "proj":
                        pe.wait_ge(pre_ready, b * PROJ_PER_B + CT + g * (2 * CT) + (n + 1))
                    else:
                        pe.wait_ge(gate_used, START + (b * MG + g) * TT + (n + 1))

                def turn_out(g, c):
                    pe.wait_ge(yn_ready, START + (b * MG + g) * TT + (c + 1))
                    for k in range(XT):
                        r = pe.transpose(bank[2][:, k * P:(k + 1) * P], yn[:, k * P:(k + 1) * P], ident[:])
                    r.then_inc(yt_done, 1)

                def project_out(g, c):
                    it = (b * MG + g) * TT + c
                    if c == 0:
                        pe.wait_ge(m_split, b * (MG * W_PER_G) + g * W_PER_G + W_PER_G)
                    pe.wait_ge(yt_ready, START + it + 1)
                    pe.wait_ge(bc_ready, START + ((it + 1) if c == TT - 1 else (it + 2)))
                    for k in range(XT):
                        r = three(bank[3][:], lambda q: yt_hi[:, q, :], lambda q: yt_lo[:, q, :],
                                  lambda q: wy_hi[:, q, :], lambda q: wy_lo[:, q, :], k, k == 0, k == XT - 1)
                    r.then_inc(mo_done, 1)

                def decays(it):
                    pe.wait_ge(au_ready, it + 1)
                    pe.wait_ge(decay_ready, START + it)
                    for q in range(2):
                        h4 = slice(q * HPG // 2, (q + 1) * HPG // 2)
                        dst = bank[4 + q][:].rearrange("p (h l) -> p h l", l=P)
                        pe.matmul(dst, after_r[:], au_hi[:, h4, :], start=True, stop=False)
                        r = pe.matmul(dst, after_r[:], au_lo[:, h4, :], start=False, stop=True)
                    r.then_inc(d_done, 1)

                def m_group(g, last):
                    uses = m_uses(last)
                    at = 0
                    for c in range(TT):
                        it = (b * MG + g) * TT + c
                        s, ck = c // CPH, slice(c % CPH * P, (c % CPH + 1) * P)
                        if c % CPH == 0:
                            pe.wait_ge(xbc_ready, b * PROJ_PER_B + g * (2 * CT) + (s * CT + CT))
                        pe.wait_ge(yt_ready, START + (it if c == 0 else it - 1))
                        pe.wait_ge(x_tm_ready, START + it)
                        for k in range(XT):
                            r = pe.transpose(bank[2][:, k * P:(k + 1) * P], xbc[s][:, k, ck], ident[:])
                        r.then_inc(xtr_done, 1)
                        pe.wait_ge(mo_used, START + (it if c == 0 else it - 1))
                        pe.wait_ge(bc_ready, START + it)
                        pe.transpose(bank[3][:, 0:P], xbc[s][:, XT, ck], ident[:])
                        pe.matmul(bank[3][:, P:2 * P], xbc[s][:, XT, ck], xbc[s][:, XT + 1, ck],
                                  start=True, stop=True, skip_group_check=True).then_inc(bc_done, 1)
                        if c > 0:
                            decays(it)
                        while uses[at][0] == "proj":
                            n = uses[at][1]
                            bank_read(g, at, uses)
                            ft = n % CT
                            if n < CT:
                                features(bank[at % 2][:], wx_hi[:, ft, :], wx_lo[:, ft, :], 1).then_inc(proj_done, 1)
                            else:
                                pe.wait_ge(m_split, b * (MG * W_PER_G) + (g + 1) * W_PER_G + (ft + 1))
                                features(bank[at % 2][:], wx_hi[:, ft, :], wx_lo[:, ft, :], 0).then_inc(proj_done, 1)
                            at += 1
                        bank_read(g, at, uses)
                        if c == 0:
                            pe.wait_ge(m_split, b * (MG * W_PER_G) + g * W_PER_G + (CT + KT))
                        tokens(bank[at % 2][:], c, wg_hi, wg_lo).then_inc(gate_done, 1)
                        at += 1
                        if c == 0:
                            decays(it)
                        pe.wait_ge(state_ready, it + 1)
                        if c == 0:
                            pe.wait_ge(inter_used, START + it)
                        pe.matmul(bank[6][:], xbc[s][:, XT + 1, ck], state[:], start=True, stop=True
                                  ).then_inc(inter_done, 1)
                        if c > 0:
                            pe.wait_ge(x_tm_ready, START + it + 1)
                            turn_out(g, c - 1)
                        pe.wait_ge(m_ready, it + 1)
                        pe.wait_ge(pool_x, START + it + 1)
                        pe.wait_ge(ss_ready, START + it)
                        for h in range(HPG):
                            r = pe.matmul(bank[7][:, h * MP:(h + 1) * MP], decay[:, h, :], xdt[:, h * MP:(h + 1) * MP],
                                          start=True, stop=True, skip_group_check=True)
                        r.then_inc(intra_done, 1)
                        if c > 0:
                            project_out(g, c - 1)
                        if c < TT - 1:
                            pe.wait_ge(inter_used, START + it + 1)
                            pe.matmul(bank[6][:], b_tm[:], xw[:], start=True, stop=True).then_inc(st_mm, 1)
                    turn_out(g, TT - 1)
                    project_out(g, TT - 1)

                for ft in range(CT):
                    if ft >= 2:
                        pe.wait_ge(pre_ready, b * PROJ_PER_B + ft - 1)
                    project(0, 0, ft)
                with pe.Fori(0, MG - 1) as g:
                    m_group(g, False)
                m_group(MG - 1, True)
                barrier(pe, b, 8)
                norm_turn(b * 4 + 3)
                barrier(pe, b, 9)
                ffn(b, 1, NF1, False)
                barrier(pe, b, 10)
                barrier(pe, b, 11)

        @block.scalar
        def _(act):
            act.wait_ge(consts_ready, 1)

            def turned(src):
                return src.rearrange("p (k t) -> p k t", t=P)

            def norm_hi(e):
                for i in range(TT):
                    act.wait_ge(xt_done, e * TT + i + 1)
                    act.copy(xhi[:, :, i * P:(i + 1) * P], turned(bank[i % 2])).then_inc(xt_hi, 1)

            def ffn(b, i, n):
                f = F[i]

                def hidden(p, par, first=False):
                    for s in range(2):
                        it = (b * n + p * 2 + par) * 2 + s
                        act.wait_ge(f["g_done"], it + 1)
                        act.activation(sg[:, s, :], bank[2 * s], ACT.Silu).then_inc(f["sg_done"], 1)
                        act.wait_ge(f["hf_done"], it + 1)
                        if not first:
                            act.wait_ge(f["dn_done"], (b * n + p * 2 + par) * TT - TT)
                        act.copy(h_hi[par][:, s * HALF:(s + 1) * HALF], hf[:, s, :]).then_inc(f["hi_done"], 1)

                hidden(0, 0, True)
                hidden(0, 1, True)
                with act.Fori(1, n // 2) as p:
                    for par in range(2):
                        hidden(p, par)
                if n % 2:
                    hidden(n // 2, 0)

            with act.Fori(0, B) as b:
                norm_hi(b * 4)
                barrier(act, b, 0)
                barrier(act, b, 1)
                ring = 0
                for what, *arg in ORDER:
                    if what == "proj":
                        f, = arg
                        act.wait_ge(wqk_in, (b * (NQ // 2) + f + 1) * 32)
                        if f > 0:
                            act.wait_ge(stacked[0], (b * (NQ // 2) + f) * STACKED)
                            act.wait_ge(stacked[1], (b * (NQ // 2) + f) * STACKED)
                        for which in range(2):
                            for s in range(2):
                                act.wait_ge(ring_done, b * RING + ring + 1)
                                act.activation(part_hi[:, which, s * HALF:(s + 1) * HALF], bank[4 + ring % 2],
                                               ACT.Identity, bias=qk_b[:, which:which + 1]
                                               ).then_inc(part_hi_ready, 1)
                                ring += 1
                    elif what == "piece":
                        ring += 1
                    elif what == "scores":
                        t, n = arg
                        s, j = STEPS[n]
                        w = HALF - max(j * P - s * HALF, 0)
                        it = b * (NQ * NS) + (t * NS + n)
                        if t > 0 or n >= 2:
                            act.wait_ge(pv_done, it - 1)
                        for p in range(2):
                            act.wait_ge(st_done[p], it + 1)
                            act.activation(probs[n % 2][:, 2 * p:2 * p + 2, 0:w], banks[:, 2 * p:2 * p + 2, 0:w],
                                           ACT.Exp, scale=1.0 / HD ** 0.5).then_inc(exp_done[p], 1)
                barrier(act, b, 2)
                for i in range(TT):
                    act.wait_ge(at_done, b * TT + i + 1)
                    act.copy(xhi[:, :, i * P:(i + 1) * P], turned(bank[2 + i % 2])).then_inc(at_hi, 1)
                barrier(act, b, 3)
                norm_hi(b * 4 + 1)
                barrier(act, b, 4)
                ffn(b, 0, NF0)
                barrier(act, b, 5)
                norm_hi(b * 4 + 2)
                barrier(act, b, 6)
                act.wait_ge(dt_w_in, (b + 1) * 64)
                act.activation(neg_a[:], alog[:], ACT.Exp)
                act.wait_ge(dt_sum, b + 1)
                act.activation(dt_abs[:], dt_in[:], ACT.Abs)
                act.drain()
                act.activation(dt_abs[:], dt_abs[:], ACT.Exp, scale=-1.0)
                act.drain()
                act.activation(dt_sp[:], dt_abs[:], ACT.Ln, bias=ones[:, 0:1]).then_inc(dt_soft, 1)
                for k in (EC, WE, ED):
                    act.wait_ge(dt_cs, b * 3 + k + 1)
                    act.activation(tab[:, k, :, :].rearrange("p c h -> p (c h)"), bank[1 + k], ACT.Exp
                                   ).then_inc(dt_exp, 1)
                barrier(act, b, 7)

                def before_conv(src, pi, n, s, first=False):
                    ft, par = n % CT, n % 2
                    act.drain()
                    act.wait_ge(proj_done, pi + 1)
                    if not first:
                        act.wait_ge(xbc_ready, pi - 1)
                    act.copy(pre[par][:, 0:MK - 1], carry[:, ft, :] if s else zeros[:, 0:MK - 1])
                    act.copy(pre[par][:, MK - 1:], src)
                    if not s:
                        act.copy(carry[:, ft, :], src[:, HALF - MK + 1:HALF])
                    o = ft * (MK + 1)
                    act.activation(conv[par][:], src, ACT.Identity, scale=cpar[:, o + MK - 1:o + MK],
                                   bias=cpar[:, o + MK:o + MK + 1]).then_inc(pre_ready, 1)

                def conv_tanh(pi, n, s):
                    act.wait_ge(conv_ready, pi + 1)
                    act.activation(xbc[s][:, n % CT, :], conv[n % 2][:], ACT.Tanh, scale=0.5).then_inc(cth_ready, 1)

                def turned_hi(it):
                    act.wait_ge(yt_done, it + 1)
                    act.wait_ge(mo_done, START + it)
                    act.copy(yt_hi[:], turned(bank[2])).then_inc(yt_hi_ready, 1)

                def decay_exp(it):
                    act.wait_ge(d_done, START + it + 1)
                    act.wait_ge(intra_done, START + it)
                    act.activation(decay[:].rearrange("p (a h) l -> p a (h l)", a=2), banks[:, 4:6, :], ACT.Exp
                                   ).then_inc(decay_ready, 1)

                def m_group(g, last):
                    uses = m_uses(last)
                    at = 0
                    p0 = b * PROJ_PER_B + g * (2 * CT) + CT
                    for c in range(TT):
                        it = (b * MG + g) * TT + c
                        act.wait_ge(xtr_done, it + 1)
                        act.wait_ge(pool_x, START + it)
                        act.copy(x_tm[:], bank[2]).then_inc(x_tm_ready, 1)
                        if c > 0:
                            decay_exp(it)
                        while uses[at][0] == "proj":
                            n = uses[at][1]
                            if n == CT:
                                held(act, cpar_in, (b * MG + g + 2) * 16)
                            s1 = 1 if n < CT else 0
                            before_conv(bank[at % 2], p0 + n, n, s1)
                            if n % CT:
                                conv_tanh(p0 + (n - 1), n - 1, s1)
                            if n % CT == CT - 1:
                                conv_tanh(p0 + n, n, s1)
                            at += 1
                        act.wait_ge(gate_done, START + it + 1)
                        act.wait_ge(yn_ready, START + it)
                        act.activation(g_th[:], bank[at % 2], ACT.Tanh, scale=0.5).then_inc(gate_th, 1)
                        at += 1
                        if c == 0:
                            decay_exp(it)
                        else:
                            turned_hi(it - 1)
                        act.wait_ge(y_ready, START + it + 1)
                        act.activation(bank[7], yv[:], ACT.Square, accum_out=ss[:]).then_inc(ss_ready, 1)
                    turned_hi((b * MG + g) * TT + (TT - 1))

                held(act, cpar_in, (b * MG + 1) * 16)
                for n in range(CT):
                    pi = b * PROJ_PER_B + n
                    before_conv(bank[n % 2], pi, n, 0, n < 2)
                    if n:
                        conv_tanh(pi - 1, n - 1, 0)
                conv_tanh(b * PROJ_PER_B + (CT - 1), CT - 1, 0)
                with act.Fori(0, MG - 1) as g:
                    m_group(g, False)
                m_group(MG - 1, True)
                barrier(act, b, 8)
                norm_hi(b * 4 + 3)
                barrier(act, b, 9)
                ffn(b, 1, NF1)
                barrier(act, b, 10)
                barrier(act, b, 11)

        @block.vector
        def _(dve):
            dve.wait_ge(consts_ready, 1)

            def mean_rstd(src, var_sem, rstd_sem, e):
                dve.drain()
                for i in range(TT):
                    dve.bn_stats(stats[:, i, :], src[:, i, :])
                dve.drain()
                for i in range(TT):
                    dve.bn_aggr(mv[:, i, :], stats[:, i, :])
                dve.drain()
                dve.tensor_scalar(var_eps[:], mv[:, :, 1], EPS, None, ALU.add).then_inc(var_sem, 1)
                dve.wait_ge(rstd_sem, e + 1)

            def add_normed(e):
                mean_rstd(Y, post_var, post_rstd, e)
                for i in range(TT):
                    dve.tensor_scalar(Y[:, i, :], Y[:, i, :], mv[:, i, 0:1], rstd[:, i:i + 1],
                                      ALU.subtract, ALU.mult)
                dve.drain()
                for i in range(TT):
                    dve.tensor_tensor(X[:, i, :], X[:, i, :], Y[:, i, :], ALU.add)

            def norm_lo(e, i):
                dve.wait_ge(xt_hi, e * TT + i + 1)
                dve.tensor_tensor(xlo[:, :, i * P:(i + 1) * P], bank[i % 2].rearrange("p (k t) -> p k t", t=P),
                                  xhi[:, :, i * P:(i + 1) * P].bitcast(F32), ALU.subtract).then_inc(xt_free, 1)

            def norm_x(e):
                mean_rstd(X, pre_var, pre_rstd, e)
                for i in range(TT):
                    if i >= 2:
                        dve.wait_ge(xt_done, e * TT + i - 1)
                    dve.tensor_scalar(xn[:, i % 2, :], X[:, i, :], mv[:, i, 0:1], rstd[:, i:i + 1],
                                      ALU.subtract, ALU.mult).then_inc(xn_ready, 1)
                    if i:
                        norm_lo(e, i - 1)
                norm_lo(e, TT - 1)

            def ffn(b, i, n, lowrank):
                f = F[i]

                def scale(p, par):
                    for m in range(3):
                        it = (b * n + p * 2 + par) * 3 + m
                        dve.wait_ge(f["lr_done"], it + 1)
                        dve.tensor_tensor(f_raw[par][:, m, :], f_raw[par][:, m, :], bank[4 + (3 * par + m) % 2],
                                          ALU.mult).then_inc(f["weff"], 1)

                def hidden(t, par):
                    for s in range(2):
                        it = (b * n + t) * 2 + s
                        dve.drain()
                        dve.wait_ge(f["sg_done"], it + 1)
                        dve.wait_ge(f["u_done"], it + 1)
                        dve.tensor_tensor(hf[:, s, :], sg[:, s, :], bank[2 * s + 1], ALU.mult).then_inc(f["hf_done"], 1)
                        dve.wait_ge(f["hi_done"], it + 1)
                        cols = slice(s * HALF, (s + 1) * HALF)
                        dve.tensor_tensor(h_lo[par][:, cols], hf[:, s, :], h_hi[par][:, cols].bitcast(F32),
                                          ALU.subtract).then_inc(f["h_ready"], 1)

                def gather(t):
                    dve.drain()
                    for i in range(TT):
                        dve.wait_ge(f["dn_done"], (b * n + t) * TT + (i + 1))
                        dve.tensor_tensor(Y[:, i, :], bank[6 + i % 2], Y[:, i, :], ALU.add).then_inc(f["dn_used"], 1)

                def step(p, par, more2, more1):
                    if more2 and lowrank:
                        scale(p + 1, par)
                    if more1:
                        hidden(p * 2 + (par + 1), 1 - par)
                    gather(p * 2 + par)

                if lowrank:
                    scale(0, 0)
                    scale(0, 1)
                hidden(0, 0)
                held(dve, f["y_zero"], b + 1)
                with dve.Fori(0, (n - 2) // 2) as p:
                    for par in range(2):
                        step(p, par, True, True)
                for t in range((n - 2) // 2 * 2, n):
                    step(t // 2, t % 2, t + 2 < n, t + 1 < n)

            with dve.Fori(0, B) as b:
                held(dve, x_in, b * 16 + 16)
                norm_x(b * 4)
                barrier(dve, b, 0)
                dve.memset(V[:, :, :, HD:VW], 1.0)
                dve.wait_ge(wv_in, b * 32 + 32)
                for i in range(TT):
                    dve.wait_ge(v_done, b * TT + i + 1)
                    dve.tensor_tensor(V[:, i, :, 0:HD], bank[i % 2].rearrange("p (h d) -> p h d", d=HD),
                                      bv_sb[:].rearrange("p (h d) -> p h d", d=HD), ALU.add).then_inc(v_free, 1)
                barrier(dve, b, 1)
                dve.memset(bank[6], 0.0).then_inc(o_zero, 1)
                ring, misc, mx_turned = 0, 0, 0
                for what, *arg in ORDER:
                    if what == "proj":
                        f, = arg
                        for which in range(2):
                            for s in range(2):
                                cols = slice(s * HALF, (s + 1) * HALF)
                                dve.wait_ge(part_hi_ready, b * 16 + 4 * f + 2 * which + s + 1)
                                dve.scalar_tensor_tensor(out=part_lo[:, which, cols], in0=bank[4 + ring % 2],
                                                         scalar=qk_b[:, which:which + 1],
                                                         in1=part_hi[:, which, cols].bitcast(F32),
                                                         op0=ALU.add, op1=ALU.subtract
                                                         ).then_inc(part_lo_ready, 1)
                                dve.drain().then_inc(ring_free, 1)
                                ring += 1
                    elif what == "piece":
                        t, n = arg
                        h, i, s, cols, _ = PIECES[n]
                        if n == 0 and t > 0:
                            dve.wait_ge(misc_done, b * (3 * NQ) + mx_turned)
                        dve.wait_ge(ring_done, b * RING + ring + 1)
                        dve.tensor_reduce(mx[:, s, h * TT + i:h * TT + i + 1], bank[4 + ring % 2][:, 0:cols],
                                          AX.X, ALU.max).then_inc(ring_free, 1)
                        ring += 1
                    elif what == "maxima":
                        t, = arg
                        dve.drain()
                        m0, m1 = (mx[:, q, :].rearrange("p (h i) -> p h i", i=TT)[:, :, CPH:TT] for q in range(2))
                        dve.tensor_tensor(m0, m0, m1, ALU.max).then_inc(mx_ready, 1)
                        misc += 1
                        mx_turned = misc
                        dve.wait_ge(misc_done, b * (3 * NQ) + misc)
                        dve.wait_ge(mt_in, START + (b * NQ + t) * 32)
                        src = bank[7][0:QUAD * TT, 0:P]
                        dve.tensor_scalar(mt_hi[:], src, -1.0, None, ALU.mult)
                        dve.drain()
                        dve.scalar_tensor_tensor(out=mt_lo[:], in0=src, scalar=-1.0, in1=mt_hi[:].bitcast(F32),
                                                 op0=ALU.mult, op1=ALU.subtract
                                                 ).then_inc(mt_ready, 1)
                        dve.drain().then_inc(misc_free, 1)
                    elif what == "values":
                        t, n = arg
                        s, j = STEPS[n]
                        if j == CPH * (s + 1) - 1:
                            dve.wait_ge(pv_done, b * (NQ * NS) + (t * NS + n) + 1)
                            dve.tensor_copy(ot[:], bank[6]).then_inc(ot_ready, 1)
                    elif what == "turn":
                        t, s = arg
                        misc += 1
                        dve.wait_ge(misc_done, b * (3 * NQ) + misc)
                        o = bank[7].rearrange("p (k h r) -> p k h r", k=CPH, h=QUAD)
                        dve.reciprocal(rsum[:], o[:, :, :, HD])
                        dve.drain()
                        cols = slice(t * QUAD * HD, (t + 1) * QUAD * HD)
                        dst = Y[:, s * CPH:(s + 1) * CPH, cols].rearrange("p k (h d) -> p k h d", d=HD)
                        dve.tensor_tensor(dst, o[:, :, :, 0:HD],
                                          rsum[:].unsqueeze(3).broadcast_to([P, CPH, QUAD, HD]), ALU.mult
                                          ).then_inc(misc_free, 1)
                barrier(dve, b, 2)
                dve.wait_ge(wo_in, b * 32 + 32)
                for i in range(TT + 1):
                    if i < TT:
                        dve.wait_ge(at_hi, b * TT + i + 1)
                        tok = slice(i * P, (i + 1) * P)
                        dve.tensor_tensor(xlo[:, :, tok], bank[2 + i % 2].rearrange("p (k t) -> p k t", t=P),
                                          xhi[:, :, tok].bitcast(F32), ALU.subtract).then_inc(at_free, 1)
                    if i > 0:
                        dve.wait_ge(o_done, b * TT + i)
                        dve.tensor_tensor(Y[:, i - 1, :], bank[(i - 1) % 2], bo_sb[:], ALU.add).then_inc(o_free, 1)
                barrier(dve, b, 3)
                add_normed(b * 4)
                norm_x(b * 4 + 1)
                barrier(dve, b, 4)
                ffn(b, 0, NF0, True)
                barrier(dve, b, 5)
                add_normed(b * 4 + 1)
                norm_x(b * 4 + 2)
                barrier(dve, b, 6)
                def by_token(par_tile):
                    return par_tile[:].unsqueeze(1).broadcast_to([P, TT, MH])

                dve.wait_ge(dt_w_in, (b + 1) * 64)
                dve.tensor_scalar(d_half[:], dsk[:], 0.5, None, ALU.mult)
                dve.wait_ge(dt_mm, (b + 1) * TT)
                dve.tensor_tensor(dt_in[:], bank[0].rearrange("p (c h) -> p c h", h=MH), by_token(dtb), ALU.add
                                  ).then_inc(dt_sum, 1)
                dve.wait_ge(dt_soft, b + 1)
                dve.scalar_tensor_tensor(out=dt_sp[:], in0=dt_in[:], scalar=0.0, in1=dt_sp[:],
                                         op0=ALU.max, op1=ALU.add)
                dve.tensor_scalar(neg_a[:], neg_a[:], -1.0, None, ALU.mult)
                dve.drain()
                dve.tensor_tensor(a_all[:], dt_sp[:], by_token(neg_a), ALU.mult).then_inc(dt_a, 1)
                dve.tensor_scalar(tab[:, DTH, :, :], dt_sp[:], 0.5, None, ALU.mult)
                dve.drain()
                dve.tensor_copy(a_r[:], a_all[:])
                dve.drain()
                dve.tensor_copy(tab[:, AHI, :, :], a_r[:].bitcast(F32))
                dve.tensor_tensor(tab[:, ALO, :, :], a_all[:], a_r[:].bitcast(F32), ALU.subtract)
                dve.wait_ge(dt_exp, b * 3 + 3)
                dve.tensor_scalar(tab[:, EC, :, :], tab[:, EC, :, :], 0.5, None, ALU.mult)
                dve.scalar_tensor_tensor(out=tab[:, WE, :, :], in0=tab[:, WE, :, :], scalar=0.25, in1=dt_sp[:],
                                         op0=ALU.mult, op1=ALU.mult)
                barrier(dve, b, 7)

                def convolve(pi, n):
                    ft, par = n % CT, n % 2
                    dve.wait_ge(pre_ready, pi + 1)
                    for k in range(MK - 1):
                        o = ft * (MK + 1) + k
                        r = dve.scalar_tensor_tensor(out=conv[par][:], in0=pre[par][:, k:k + HALF],
                                                     scalar=cpar[:, o:o + 1], in1=conv[par][:],
                                                     op0=ALU.mult, op1=ALU.add)
                        if k < MK - 2:
                            dve.drain()
                    r.then_inc(conv_ready, 1)

                def twice_silu(pi, n, s):
                    dve.wait_ge(cth_ready, pi + 1)
                    dve.scalar_tensor_tensor(out=xbc[s][:, n % CT, :], in0=xbc[s][:, n % CT, :], scalar=1.0,
                                             in1=conv[n % 2][:], op0=ALU.add, op1=ALU.mult).then_inc(xbc_ready, 1)

                def masked(it, sm):
                    dve.wait_ge(bc_done, it + 1)
                    dve.wait_ge(st_mm, START + sm)
                    dve.tensor_copy(b_tm[:], bank[3][:, 0:P])
                    dve.tensor_tensor(cb[:], bank[3][:, P:2 * P], quarter[:], ALU.mult).then_inc(bc_ready, 1)
                    dve.drain()
                    dve.wait_ge(decay_ready, START + it + 1)
                    dve.tensor_tensor(decay[:], decay[:], cb[:].unsqueeze(1).broadcast_to([P, HPG, P]), ALU.mult
                                      ).then_inc(m_ready, 1)

                def turned_lo(it):
                    dve.wait_ge(yt_hi_ready, it + 1)
                    dve.tensor_tensor(yt_lo[:], bank[2].rearrange("p (k t) -> p k t", t=P), yt_hi[:].bitcast(F32),
                                      ALU.subtract).then_inc(yt_ready, 1)

                def gather(it, c):
                    dve.wait_ge(mo_done, START + it + 1)
                    dve.tensor_tensor(Y[:, c, :], bank[3], Y[:, c, :], ALU.add).then_inc(mo_used, 1)

                def by_head(t):
                    return t.rearrange("p (h d) -> p h d", d=MP)

                def m_group(g, last):
                    uses = m_uses(last)
                    at = 0
                    p0 = b * PROJ_PER_B + g * (2 * CT) + CT
                    sm = (b * MG + g) * (TT - 1)
                    dve.wait_ge(pool_x, START + (b * MG + g) * TT)
                    dve.wait_ge(inter_done, START + (b * MG + g) * TT)
                    dve.tensor_copy(gt[:].rearrange("p k c h -> p (k c) h"),
                                    tab[:].rearrange("p k c h -> p (k c) h")[:, :, bass.ds(g * HPG, HPG)])
                    dve.tensor_copy(gd[:], d_half[:, bass.ds(g * HPG, HPG)]).then_inc(gt_ready, 1)
                    dve.memset(state[:], 0.0).then_inc(state_ready, 1)
                    dve.drain()
                    for c in range(TT):
                        it = (b * MG + g) * TT + c
                        if c > 0:
                            masked(it, sm + c)
                        while uses[at][0] == "proj":
                            n = uses[at][1]
                            s1 = 1 if n < CT else 0
                            convolve(p0 + n, n)
                            if n % CT:
                                twice_silu(p0 + (n - 1), n - 1, s1)
                            if n % CT == CT - 1:
                                twice_silu(p0 + n, n, s1)
                            at += 1
                        dve.wait_ge(gate_th, it + 1)
                        dve.scalar_tensor_tensor(out=g_th[:], in0=g_th[:], scalar=1.0, in1=bank[at % 2],
                                                 op0=ALU.add, op1=ALU.mult).then_inc(gate_used, 1)
                        at += 1
                        if c == 0:
                            masked(it, sm)
                        dve.wait_ge(inter_done, START + it + 1)
                        dve.tensor_tensor(by_head(yv[:]), by_head(bank[6]),
                                          gt[:, EC, c, :].unsqueeze(2).broadcast_to([P, HPG, MP]), ALU.mult
                                          ).then_inc(inter_used, 1)
                        if c > 0:
                            turned_lo(it - 1)
                        dve.drain()
                        dve.wait_ge(intra_done, START + it + 1)
                        dve.tensor_tensor(yv[:], yv[:], bank[7], ALU.add)
                        dve.drain()
                        dve.wait_ge(pool_x, START + it + 1)
                        dve.tensor_tensor(yv[:], yv[:], xd[:], ALU.add).then_inc(y_ready, 1)
                        if c > 0:
                            gather(it - 1, c - 1)
                        if c < TT - 1:
                            dve.wait_ge(st_mm, START + sm + (c + 1))
                            dve.wait_ge(state_dec, sm + (c + 1))
                            dve.tensor_tensor(state[:], state[:], bank[6], ALU.add).then_inc(state_ready, 1)
                        dve.wait_ge(rg_ready, it + 1)
                        dve.scalar_tensor_tensor(out=yn[:], in0=yv[:], scalar=rg[:], in1=g_th[:],
                                                 op0=ALU.mult, op1=ALU.mult).then_inc(yn_ready, 1)
                    it = (b * MG + g) * TT + (TT - 1)
                    turned_lo(it)
                    gather(it, TT - 1)

                for n in range(CT):
                    pi = b * PROJ_PER_B + n
                    convolve(pi, n)
                    if n:
                        twice_silu(pi - 1, n - 1, 0)
                twice_silu(b * PROJ_PER_B + (CT - 1), CT - 1, 0)
                held(dve, m_zero, b + 1)
                with dve.Fori(0, MG - 1) as g:
                    m_group(g, False)
                m_group(MG - 1, True)
                barrier(dve, b, 8)
                add_normed(b * 4 + 2)
                norm_x(b * 4 + 3)
                barrier(dve, b, 9)
                ffn(b, 1, NF1, False)
                barrier(dve, b, 10)
                add_normed(b * 4 + 3)
                barrier(dve, b, 11)

        @block.gpsimd
        def _(pool):
            pool.memset(zeros[:], 0.0)
            pool.memset(ones[:], 1.0)
            pool.memset(half_neg[:], -0.5)
            for m, v in ((ident, 0.0), (ident_b, 0.0), (mask_qk, 0.0), (mask_kq, 0.0), (quarter, 0.25)):
                pool.memset(m[:], v)
            pool.drain()

            def select(m, src, op, p_step, x_step, fill):
                pool.affine_select(out=m[:], in_=src[:], compare_op=op, fill=fill, base=0,
                                   pattern=[[x_step, P]], channel_multiplier=p_step)

            select(ident, ident, ALU.not_equal, 1, -1, 1.0)
            select(ident_b, ident_b, ALU.not_equal, 1, -1, 1.0)
            select(mask_qk, mask_qk, ALU.is_ge, 1, -1, NEG)
            select(mask_kq, mask_kq, ALU.is_ge, -1, 1, NEG)
            select(quarter, quarter, ALU.is_ge, -1, 1, 0.0)
            select(upto, ones, ALU.is_ge, -1, 1, 0.0)
            select(after, ones, ALU.is_gt, 1, -1, 0.0)
            pool.drain()
            pool.tensor_copy(after_r[:], after[:])
            for semaphore in started:
                pool.drain().then_inc(semaphore, START)
            pool.drain().then_inc(consts_ready, 1)

            def split(hi, lo, raw):
                pool.tensor_scalar(hi, raw, 1.0, 1.0, ALU.mult, ALU.mult)
                pool.drain()
                return pool.tensor_tensor(lo, raw, hi.bitcast(F32), ALU.subtract)

            def root(var_sem, rstd_sem, e):
                pool.wait_ge(var_sem, e + 1)
                pool.tensor_tensor(rstd[:], var_eps[:], half_neg[:], ALU.pow).then_inc(rstd_sem, 1)

            def ffn(b, i, n, lowrank):
                f = F[i]
                pool.memset(Y[:], 0.0).then_inc(f["y_zero"], 1)

                def split_tile(p, par, first=False):
                    t = b * n + p * 2 + par
                    for m in range(3):
                        if lowrank:
                            held(pool, f["weff"], t * 3 + (m + 1))
                        elif m == 0:
                            held(pool, f[f"raw_in{par}"], (b * ((n + 1 - par) // 2) + p) * 16 + 16)
                        if not first:
                            if m == 0:
                                held(pool, f["u_done"], t * 2 - 2)
                            if m == 2:
                                held(pool, f["dn_done"], t * TT - TT)
                        split(f_hi[par][:, m, :], f_lo[par][:, m, :], f_raw[par][:, m, :]).then_inc(f["w_ready"], 1)

                split_tile(0, 0, True)
                split_tile(0, 1, True)
                with pool.Fori(1, n // 2) as p:
                    for par in range(2):
                        split_tile(p, par)
                if n % 2:
                    split_tile(n // 2, 0)

            with pool.Fori(0, B) as b:
                root(pre_var, pre_rstd, b * 4)
                barrier(pool, b, 0)
                held(pool, wv_in, b * 32 + 32)
                split(wv_hi[:], wv_lo[:], wv_raw[:]).then_inc(wv_ready, 1)
                barrier(pool, b, 1)
                ring = 0
                for what, *arg in ORDER:
                    if what == "proj":
                        f, = arg
                        held(pool, wqk_in, (b * (NQ // 2) + f + 1) * 32)
                        if f > 0:
                            held(pool, ring_done, b * RING + wqk_last_use)
                        split(wqk_hi[:], wqk_lo[:], wqk_raw[:]).then_inc(wqk_ready, 2)
                        ring += 4
                        wqk_last_use = ring
                    elif what == "piece":
                        ring += 1
                barrier(pool, b, 2)
                held(pool, wo_in, b * 32 + 32)
                split(wo_hi[:], wo_lo[:], wo_raw[:]).then_inc(wo_ready, 1)
                barrier(pool, b, 3)
                root(post_var, post_rstd, b * 4)
                root(pre_var, pre_rstd, b * 4 + 1)
                barrier(pool, b, 4)
                ffn(b, 0, NF0, True)
                barrier(pool, b, 5)
                root(post_var, post_rstd, b * 4 + 1)
                root(pre_var, pre_rstd, b * 4 + 2)
                barrier(pool, b, 6)
                held(pool, dt_w_in, (b + 1) * 64)
                split(wdt_hi[:], wdt_lo[:], wdt_raw[:]).then_inc(dt_w_ready, 1)
                barrier(pool, b, 7)

                pool.memset(Y[:], 0.0).then_inc(m_zero, 1)

                def split_m(hi, lo, n, g):
                    held(pool, m_raw_in[n % 2], (b * (MG * W_PER_G // 2) + g * (W_PER_G // 2) + n // 2) * 16 + 16)
                    raw = m_raw[:, n % 2, :]
                    if n >= CT + KT:
                        k = n - CT - KT
                        col = CT * (MK + 1) + k
                        pool.tensor_scalar(raw, raw, cpar[:, col:col + 1], 0.5, ALU.mult, ALU.mult)
                        pool.drain()
                    split(hi, lo, raw).then_inc(m_split, 1)

                def decay_terms(c, it):
                    pool.wait_ge(d_done, START + it)
                    for dst, kind in ((au_hi, AHI), (au_lo, ALO)):
                        r = pool.tensor_tensor(dst[:], upto[:].unsqueeze(1).broadcast_to([P, HPG, P]),
                                               gt[:, kind, c, :].unsqueeze(2).broadcast_to([P, HPG, P]), ALU.mult)
                    r.then_inc(au_ready, 1)

                def by_head(t):
                    return t.rearrange("p (h d) -> p h d", d=MP)

                def per_head(t):
                    return t.unsqueeze(2).broadcast_to([P, HPG, MP])

                def m_group(g, last):
                    pool.wait_ge(gt_ready, b * MG + g + 1)
                    decay_terms(0, (b * MG + g) * TT)
                    pool.wait_ge(gate_done, START + (b * MG + g) * TT)
                    for k in range(KT):
                        split_m(wg_hi[:, k, :], wg_lo[:, k, :], CT + k, g)
                    sm = (b * MG + g) * (TT - 1)
                    for c in range(TT):
                        it = (b * MG + g) * TT + c
                        pool.wait_ge(x_tm_ready, START + it + 1)
                        pool.wait_ge(intra_done, START + it)
                        pool.tensor_tensor(by_head(xdt[:]), by_head(x_tm[:]), per_head(gt[:, DTH, c, :]), ALU.mult)
                        if c < TT - 1:
                            pool.wait_ge(st_mm, START + sm + c)
                            pool.tensor_tensor(by_head(xw[:]), by_head(x_tm[:]), per_head(gt[:, WE, c, :]), ALU.mult)
                        pool.wait_ge(y_ready, START + it)
                        pool.tensor_tensor(by_head(xd[:]), by_head(x_tm[:]), per_head(gd[:]), ALU.mult
                                           ).then_inc(pool_x, 1)
                        if c < TT - 1:
                            pool.wait_ge(state_ready, it + 1)
                            pool.wait_ge(inter_done, START + it + 1)
                            pool.tensor_tensor(by_head(state[:]), by_head(state[:]), per_head(gt[:, ED, c, :]),
                                               ALU.mult).then_inc(state_dec, 1)
                            decay_terms(c + 1, it + 1)
                        if c == 0:
                            pool.wait_ge(mo_done, START + it)
                            for k in range(XT):
                                split_m(wy_hi[:, k, :], wy_lo[:, k, :], CT + KT + k, g)
                        held(pool, ss_ready, START + it + 1)
                        pool.tensor_scalar(rg[:], ss[:], 1.0 / GI, EPS, ALU.mult, ALU.add)
                        pool.drain()
                        pool.tensor_tensor(rg[:], rg[:], half_neg[:, 0:1], ALU.pow).then_inc(rg_ready, 1)
                        if not last:
                            for ft in SPLIT_AT.get(c, ()):
                                pool.wait_ge(proj_done, b * PROJ_PER_B + g * (2 * CT) + (CT + ft + 1))
                                split_m(wx_hi[:, ft, :], wx_lo[:, ft, :], ft, g + 1)

                for ft in range(CT):
                    split_m(wx_hi[:, ft, :], wx_lo[:, ft, :], ft, 0)
                with pool.Fori(0, MG - 1) as g:
                    m_group(g, False)
                m_group(MG - 1, True)
                barrier(pool, b, 8)
                root(post_var, post_rstd, b * 4 + 2)
                root(pre_var, pre_rstd, b * 4 + 3)
                barrier(pool, b, 9)
                ffn(b, 1, NF1, False)
                barrier(pool, b, 10)
                root(post_var, post_rstd, b * 4 + 3)
                barrier(pool, b, 11)


def kernel(**inputs):
    import numpy as np
    import concourse.bacc as bacc
    from concourse.bass_utils import run_bass_kernel_spmd as run

    a = {k: np.asarray(v) for k, v in inputs.items()}

    def by_out(w):
        n = w.shape[0] // P
        return w.reshape(n, P, KT, P).transpose(0, 3, 2, 1).reshape(n, P, KT * P)

    def by_in(w):
        return w.T.reshape(-1, P, w.shape[0])

    def rows(w, n):
        return np.pad(w, ((0, n - w.shape[0]), (0, 0)))

    def everywhere(v):
        return np.broadcast_to(v[None, :], (P, v.shape[0]))

    wq, wk = by_out(a["L0_attn_Wq"]), by_out(a["L0_attn_Wk"])
    qk = np.stack([wq, wk], 1).reshape(2 * KT, P, D)
    arrays = {
        "x": a["L0_attn_x"],
        "w_attn": np.concatenate([by_in(a["L0_attn_Wv"]), qk, by_in(a["L0_attn_Wo"])]),
        "qk_bias": np.stack([a["L0_attn_bq"].reshape(KT, P), a["L0_attn_bk"].reshape(KT, P)], 2),
        "bv": everywhere(a["L0_attn_bv"]),
        "bo": everywhere(a["L0_attn_bo"]),
        "w_ffn0": np.stack([by_out(a["L0_ffn_gate_w"]), by_out(a["L0_ffn_up_w"]), by_in(a["L0_ffn_down_w"])], 1),
        "lr0": np.concatenate([a["L0_ffn_gate_su"].reshape(NF0, P, RANK).transpose(0, 2, 1),
                               a["L0_ffn_up_su"].reshape(NF0, P, RANK).transpose(0, 2, 1),
                               a["L0_ffn_down_sv"].reshape(RANK, NF0, P).transpose(1, 0, 2)], 2),
        "lr0_const": np.concatenate([a["L0_ffn_gate_sv"], a["L0_ffn_up_sv"], a["L0_ffn_down_su"].T], 1),
    }
    gate_up = a["L1_ffn_w_gate_up"]
    half = gate_up.shape[0] // 2
    arrays["w_ffn1"] = np.stack([by_out(rows(gate_up[:half], NF1 * P)), by_out(rows(gate_up[half:], NF1 * P)),
                                 by_in(rows(a["L1_ffn_w_down"].T, NF1 * P).T)], 1)

    inner, gn = MH * MP, MG * MN
    proj = a["L1_attn_in_proj_w"]

    def channels(v):
        rest = v.shape[1:]
        return np.concatenate([v[:inner].reshape(MG, XT, P, *rest), v[inner:inner + gn].reshape(MG, 1, P, *rest),
                               v[inner + gn:].reshape(MG, 1, P, *rest)], 1)

    xbc_w = channels(proj[inner:2 * inner + 2 * gn])
    arrays["w_mamba"] = np.concatenate([
        by_out(xbc_w.reshape(-1, D)).reshape(MG, CT, P, D),
        proj[:inner].reshape(MG, GI, KT, P).transpose(0, 2, 3, 1),
        a["L1_attn_out_proj_w"].T.reshape(MG, XT, P, D)], 1)
    arrays["w_dt"] = proj[-MH:].T.reshape(KT, P, MH).transpose(1, 0, 2)
    taps = np.concatenate([channels(a["L1_attn_conv_weight"]), channels(a["L1_attn_conv_bias"][:, None])], 3)
    arrays["conv_par"] = np.concatenate([taps.transpose(0, 2, 1, 3).reshape(MG, P, CT * (MK + 1)),
                                         a["L1_attn_norm_weight"].reshape(MG, XT, P).transpose(0, 2, 1)], 2)
    arrays["dt_bias"] = everywhere(a["L1_attn_dt_bias"])
    arrays["a_log"] = everywhere(a["L1_attn_A_log"])
    arrays["d_skip"] = everywhere(a["L1_attn_D"])

    nc = bacc.Bacc("TRN2", target_bir_lowering=False, num_devices=1)
    feed, args = {}, {}
    for name, v in arrays.items():
        v = np.ascontiguousarray(v)
        feed[f"in_{name}"] = v
        args[name] = nc.dram_tensor(f"in_{name}", v.shape, mybir.dt.from_np(v.dtype), kind="ExternalInput").ap()
    args["out"] = nc.dram_tensor("out_y", (B, L, D), F32, kind="ExternalOutput").ap()
    build(nc, **args)
    r = run(nc, [feed], core_ids=[0])
    return r.results[0]["out_y"]
```

```python
from contextlib import ExitStack

import concourse.bass as bass
from concourse import mybir

ALU = mybir.AluOpType
ACT = mybir.ActivationFunctionType
AX = mybir.AxisListType
F32 = mybir.dt.float32
F32R = mybir.dt.float32r
BF16 = mybir.dt.bfloat16

B, L, D = 2, 1024, 512
P = 128
TT = L // P
KT = D // P
HALF = 512
EPS = 1e-5
NEG = -1e30

AH, HD = 32, 16
QUAD = 4
NQ = AH // QUAD
VW = HD + 1
ROWS = 3 * HD

NF0 = 1792 // P
NF1 = (1376 + P - 1) // P
RANK = 4

MH, MP, MN, MG, MK = 64, 64, 128, 8, 4
HPG = MH // MG
GI = HPG * MP
XT = GI // P
CT = XT + 2
UNITS = 2 * MG
CPH = HALF // P
PROJ_AT = [(0, 1), (2,), (3, 4), (5,)]
SPLIT_AT = {1: (0, 1), 2: (2,), 3: (3, 4), 4: (5,)}
W_PER_G = CT + KT + XT
PROJ_PER_B = 2 * CT * MG

START = 1
BARRIERS = 12


def build(nc, x, w_attn, qk_bias, bv, bo, w_ffn0, lr0, lr0_const, w_ffn1,
          w_mamba, w_dt, conv_par, dt_bias, a_log, d_skip, out):
    ctx = ExitStack()
    with ctx:
        def sb(name, shape, dt=F32, stack=ctx):
            return stack.enter_context(nc.sbuf_tensor(name, shape, dt))

        def sem(name):
            return ctx.enter_context(nc.semaphore(name))

        banks = ctx.enter_context(nc.psum_tensor("banks", [P, 8, HALF], F32))
        bank = [banks[:, i, :] for i in range(8)]

        X = sb("X", [P, TT, D])
        Y = sb("Y", [P, TT, D])
        xhi = sb("xhi", [P, KT, L], F32R)
        xlo = sb("xlo", [P, KT, L], F32R)
        ones = sb("ones", [P, P])
        ident = sb("ident", [P, P])
        ident_b = sb("ident_b", [P, P], BF16)
        mask_qk = sb("mask_qk", [P, P], BF16)
        mask_kq = sb("mask_kq", [P, P], BF16)
        upto = sb("upto", [P, P])
        after = sb("after", [P, P])
        after_r = sb("after_r", [P, P], F32R)
        quarter = sb("quarter", [P, P])
        zeros = sb("zeros", [P, MK])
        half_neg = sb("half_neg", [P, TT])
        stats = sb("stats", [P, TT, 6])
        mv = sb("mv", [P, TT, 2])
        var_eps = sb("var_eps", [P, TT])
        rstd = sb("rstd", [P, TT])

        with ExitStack() as s:
            xn = sb("xn", [P, 2, D], stack=s)
        with ExitStack() as s:
            V = sb("V", [P, TT, AH, VW], stack=s)
            with ExitStack() as s2:
                wv_raw = sb("wv_raw", [P, KT, D], stack=s2)
                wv_hi = sb("wv_hi", [P, KT, D], F32R, stack=s2)
                wv_lo = sb("wv_lo", [P, KT, D], F32R, stack=s2)
                bv_sb = sb("bv_sb", [P, D], stack=s2)
            with ExitStack() as s2:
                stack_q = [sb(f"stack_q{i}", [P, QUAD, L], F32R, stack=s2) for i in range(2)]
                stack_k = [sb(f"stack_k{i}", [P, QUAD, L], F32R, stack=s2) for i in range(2)]
                part_hi = sb("part_hi", [P, 2, L], F32R, stack=s2)
                part_lo = sb("part_lo", [P, 2, L], F32R, stack=s2)
                wqk_raw = sb("wqk_raw", [P, 2, D], stack=s2)
                wqk_hi = sb("wqk_hi", [P, 2, D], F32R, stack=s2)
                wqk_lo = sb("wqk_lo", [P, 2, D], F32R, stack=s2)
                qk_b = sb("qk_b", [P, 2], stack=s2)
                probs = [sb(f"probs{i}", [P, QUAD, HALF], stack=s2) for i in range(2)]
                ot = sb("ot", [P, HALF], stack=s2)
                mx = sb("mx", [P, 2, QUAD * TT], stack=s2)
                mt_hi = sb("mt_hi", [QUAD * TT, P], F32R, stack=s2)
                mt_lo = sb("mt_lo", [QUAD * TT, P], F32R, stack=s2)
                rsum = sb("rsum", [P, CPH, QUAD], stack=s2)
        with ExitStack() as s:
            wo_raw = sb("wo_raw", [P, KT, D], stack=s)
            wo_hi = sb("wo_hi", [P, KT, D], F32R, stack=s)
            wo_lo = sb("wo_lo", [P, KT, D], F32R, stack=s)
            bo_sb = sb("bo_sb", [P, D], stack=s)
        with ExitStack() as s:
            f_raw = [sb(f"f_raw{i}", [P, 3, D], stack=s) for i in range(2)]
            f_hi = [sb(f"f_hi{i}", [P, 3, D], F32R, stack=s) for i in range(2)]
            f_lo = [sb(f"f_lo{i}", [P, 3, D], F32R, stack=s) for i in range(2)]
            f_lr = [sb(f"f_lr{i}", [RANK, 3 * P], stack=s) for i in range(2)]
            f_lrc = sb("f_lrc", [RANK, 3 * D], stack=s)
            sg = sb("sg", [P, 2, HALF], stack=s)
            hf = sb("hf", [P, 2, HALF], stack=s)
            h_hi = [sb(f"h_hi{i}", [P, L], F32R, stack=s) for i in range(2)]
            h_lo = [sb(f"h_lo{i}", [P, L], F32R, stack=s) for i in range(2)]
        with ExitStack() as s:
            EC, WE, ED, DTH, AHI, ALO = range(6)
            tab = sb("tab", [P, 6, TT, MH], stack=s)
            d_half = sb("d_half", [P, MH], stack=s)
            with ExitStack() as s2:
                wdt_raw = sb("wdt_raw", [P, KT, MH], stack=s2)
                wdt_hi = sb("wdt_hi", [P, KT, MH], F32R, stack=s2)
                wdt_lo = sb("wdt_lo", [P, KT, MH], F32R, stack=s2)
                dtb = sb("dtb", [P, MH], stack=s2)
                alog = sb("alog", [P, MH], stack=s2)
                neg_a = sb("neg_a", [P, MH], stack=s2)
                dsk = sb("dsk", [P, MH], stack=s2)
                dt_in = sb("dt_in", [P, TT, MH], stack=s2)
                dt_abs = sb("dt_abs", [P, TT, MH], stack=s2)
                dt_sp = sb("dt_sp", [P, TT, MH], stack=s2)
                a_all = sb("a_all", [P, TT, MH], stack=s2)
                a_r = sb("a_r", [P, TT, MH], F32R, stack=s2)
            with ExitStack() as s2:
                m_raw = sb("m_raw", [P, 2, D], stack=s2)
                wx_hi = sb("wx_hi", [P, CT, D], F32R, stack=s2)
                wx_lo = sb("wx_lo", [P, CT, D], F32R, stack=s2)
                wg_hi = sb("wg_hi", [P, KT, D], F32R, stack=s2)
                wg_lo = sb("wg_lo", [P, KT, D], F32R, stack=s2)
                wy_hi = sb("wy_hi", [P, XT, D], F32R, stack=s2)
                wy_lo = sb("wy_lo", [P, XT, D], F32R, stack=s2)
                cpar = sb("cpar", [P, CT * (MK + 1) + XT], stack=s2)
                gt = sb("gt", [P, 6, TT, HPG], stack=s2)
                gd = sb("gd", [P, 2, HPG], stack=s2)
                xbc = [sb(f"xbc{i}", [P, CT, HALF], stack=s2) for i in range(2)]
                pre = [sb(f"pre{i}", [P, MK - 1 + HALF], stack=s2) for i in range(2)]
                carry = sb("carry", [P, CT, MK - 1], stack=s2)
                conv = [sb(f"conv{i}", [P, HALF], stack=s2) for i in range(2)]
                x_tm = sb("x_tm", [P, GI], stack=s2)
                b_tm = sb("b_tm", [P, MN], stack=s2)
                cb = sb("cb", [P, P], stack=s2)
                au_hi = sb("au_hi", [P, HPG, P], F32R, stack=s2)
                au_lo = sb("au_lo", [P, HPG, P], F32R, stack=s2)
                decay = sb("decay", [P, HPG, P], stack=s2)
                xdt = sb("xdt", [P, GI], stack=s2)
                xw = sb("xw", [P, GI], stack=s2)
                xd = sb("xd", [P, GI], stack=s2)
                state = sb("state", [P, GI], stack=s2)
                g_th = sb("g_th", [P, GI], stack=s2)
                yv = sb("yv", [P, GI], stack=s2)
                ss = sb("ss", [P, 1], stack=s2)
                rg = sb("rg", [P, 1], stack=s2)
                yn = sb("yn", [P, GI], stack=s2)
                yt_hi = sb("yt_hi", [P, XT, P], F32R, stack=s2)
                yt_lo = sb("yt_lo", [P, XT, P], F32R, stack=s2)

        consts_ready = sem("consts_ready")
        phase_end = sem("phase_end")
        held_waits = sem("held_waits")
        x_in = sem("x_in")
        out_done = sem("out_done")
        post_var, post_rstd = sem("post_var"), sem("post_rstd")
        pre_var, pre_rstd = sem("pre_var"), sem("pre_rstd")
        xn_ready, xt_done, xt_hi, xt_free = (sem(n) for n in ("xn_ready", "xt_done", "xt_hi", "xt_free"))
        wv_in, wv_ready, v_done, v_free = (sem(n) for n in ("wv_in", "wv_ready", "v_done", "v_free"))
        wo_in, wo_ready, at_done, at_hi, at_free, o_done, o_free = (
            sem(n) for n in ("wo_in", "wo_ready", "at_done", "at_hi", "at_free", "o_done", "o_free"))
        wqk_in, wqk_ready, wqk_used = sem("wqk_in"), sem("wqk_ready"), sem("wqk_used")
        ring_done, ring_free = sem("ring_done"), sem("ring_free")
        part_hi_ready, part_lo_ready = sem("part_hi_ready"), sem("part_lo_ready")
        stacked = [sem("stacked0"), sem("stacked1")]
        ones_rows = sem("ones_rows")
        mx_ready, misc_done, misc_free = sem("mx_ready"), sem("misc_done"), sem("misc_free")
        mt_ready, mt_in = sem("mt_ready"), sem("mt_in")
        st_done = [sem("st_done0"), sem("st_done1")]
        exp_done = [sem("exp_done0"), sem("exp_done1")]
        pv_done, ot_ready, o_zero = sem("pv_done"), sem("ot_ready"), sem("o_zero")
        F = [{n: sem(f"{n}_{i}") for n in (
            "raw_in0", "raw_in1", "lr_const", "lr_done", "weff", "w_ready", "g_done", "u_done", "sg_done",
            "hf_done", "hi_done", "h_ready", "dn_done", "dn_used", "y_zero")}
            for i in range(2)]
        dt_w_in, dt_w_ready, dt_mm, dt_sum, dt_soft, dt_a, dt_cs, dt_exp = (
            sem(n) for n in ("dt_w_in", "dt_w_ready", "dt_mm", "dt_sum", "dt_soft", "dt_a", "dt_cs", "dt_exp"))
        m_raw_in = [sem("m_raw_in0"), sem("m_raw_in1")]
        m_hi, m_split, cpar_in = sem("m_hi"), sem("m_split"), sem("cpar_in")
        gt_ready, m_zero = sem("gt_ready"), sem("m_zero")
        proj_done, gate_done = sem("proj_done"), sem("gate_done")
        pre_ready, conv_ready, cth_ready, xbc_ready = (
            sem(n) for n in ("pre_ready", "conv_ready", "cth_ready", "xbc_ready"))
        gate_th, gate_used = sem("gate_th"), sem("gate_used")
        xtr_done, x_tm_ready = sem("xtr_done"), sem("x_tm_ready")
        bc_done, bc_ready = sem("bc_done"), sem("bc_ready")
        au_ready, d_done, decay_ready, m_ready = (sem(n) for n in ("au_ready", "d_done", "decay_ready", "m_ready"))
        pool_x = sem("pool_x")
        inter_done, inter_used, intra_done, y_ready = (
            sem(n) for n in ("inter_done", "inter_used", "intra_done", "y_ready"))
        ss_ready, rg_ready, yn_ready = sem("ss_ready"), sem("rg_ready"), sem("yn_ready")
        yt_done, yt_hi_ready, yt_ready, mo_done, mo_used = (
            sem(n) for n in ("yt_done", "yt_hi_ready", "yt_ready", "mo_done", "mo_used"))
        st_mm, state_ready, state_dec = sem("st_mm"), sem("state_ready"), sem("state_dec")

        started = [misc_free, *exp_done, ot_ready, mt_in, gate_used, gate_done, yn_ready, yt_ready, x_tm_ready,
                   bc_ready, d_done, decay_ready, pool_x, inter_done, inter_used, intra_done, y_ready, ss_ready,
                   mo_done, mo_used, st_mm]

        block = ctx.enter_context(nc.Block())

        def held(eng, semaphore, value):
            eng.wait_ge(semaphore, value)
            eng.sem_inc(held_waits, 1)

        def barrier(eng, b, k):
            eng.drain().then_inc(phase_end, 1)
            held(eng, phase_end, b * (5 * BARRIERS) + 5 * (k + 1))

        STEPS = [(s, j) for s in range(2) for j in range(CPH * (s + 1))]
        PIECES = [(h, i, s, min((i + 1) * P - s * HALF, HALF), s == i // CPH)
                  for h in range(QUAD) for i in range(TT) for s in range(i // CPH + 1)]
        NS, NP = len(STEPS), len(PIECES)
        RING = 4 * (NQ // 2) + NQ * NP
        STACKED = 16 * 6 * QUAD
        AHEAD = 12

        def attention_order():
            yield "proj", 0
            yield "proj", 1
            for n in range(NP):
                yield "piece", 0, n
            yield "maxima", 0
            for n in range(AHEAD):
                yield "piece", 1, n
            for t in range(NQ):
                if t in (1, 3):
                    yield "proj", (t + 3) // 2
                if t > 0 and t + 1 < NQ:
                    for n in range(AHEAD):
                        yield "piece", t + 1, n
                at = AHEAD
                for n in range(NS):
                    for q in range(4):
                        if q < 2:
                            yield "scores", t, n, q
                        elif n > 0:
                            yield "values", t, n - 1, q - 2
                        if t + 1 < NQ and at < NP:
                            yield "piece", t + 1, at
                            at += 1
                    if n == 1 and t > 0:
                        yield "turn", t - 1, 1
                    if n == 7:
                        yield "turn", t, 0
                    if n == 10 and t + 1 < NQ:
                        yield "maxima", t + 1
                for q in range(2):
                    yield "values", t, NS - 1, q
            yield "turn", NQ - 1, 1

        ORDER = list(attention_order())

        def m_uses(last):
            uses = []
            for c in range(TT):
                s = c // CPH
                if not (last and s == 1):
                    uses += [("proj", s * CT + ft) for ft in PROJ_AT[c % CPH]]
                uses.append(("gate", c))
            return uses

        @block.sync
        def _(sp):
            sp.wait_ge(consts_ready, 1)
            with sp.Fori(0, B) as b:
                sp.dma_start(X[:], x[b].rearrange("(t p) d -> p t d", p=P)).then_inc(x_in, 16)
                barrier(sp, b, 0)
                sp.dma_start(wv_raw[:], w_attn[0:KT].rearrange("n p c -> p n c")).then_inc(wv_in, 16)
                sp.dma_start(bv_sb[:], bv).then_inc(wv_in, 16)
                barrier(sp, b, 1)
                for i in range(2):
                    for row in (ROWS, ROWS + 1, 64 + ROWS, 64 + ROWS + 1):
                        sp.dma_start(stack_k[i][row:row + 1, :, :].bitcast(F32), ones[0:QUAD * TT, :]
                                     ).then_inc(ones_rows, 16)

                def load_qk(f):
                    if f > 0:
                        held(sp, wqk_ready, b * 8 + 2 * f)
                        held(sp, part_lo_ready, b * 16 + 4 * f)
                    sp.dma_start(wqk_raw[:], w_attn[KT + 2 * f:KT + 2 * f + 2].rearrange("n p c -> p n c")
                                 ).then_inc(wqk_in, 16)
                    sp.dma_start(qk_b[:], qk_bias[f]).then_inc(wqk_in, 16)

                def stack(t):
                    f, par = t // 2, t % 2
                    held(sp, part_hi_ready, b * 16 + 4 * f + 4)
                    held(sp, part_lo_ready, b * 16 + 4 * f + 4)
                    if t >= 4:
                        held(sp, pv_done, b * (NQ * NS) + (t - 3) * NS)
                    for h in range(QUAD):
                        src = slice(HD * (QUAD * par + h), HD * (QUAD * par + h + 1))
                        for dst, which, parts in ((stack_q[f % 2], 0, (part_hi, part_hi, part_lo)),
                                                  (stack_k[f % 2], 1, (part_hi, part_lo, part_hi))):
                            for r, part in enumerate(parts):
                                at = 64 * par + HD * r
                                sp.dma_start(dst[at:at + HD, h, :].bitcast(F32),
                                             part[src, which, :].bitcast(F32)).then_inc(stacked[par], 16)

                def put_maxima(t):
                    held(sp, mt_ready, b * NQ + t + 1)
                    for r, part in ((0, mt_hi), (1, mt_lo)):
                        at = 64 * (t % 2) + ROWS + r
                        sp.dma_start(stack_q[t // 2 % 2][at:at + 1, :, :].bitcast(F32),
                                     part[:].bitcast(F32)).then_inc(mt_in, 16)

                load_qk(0)
                stack(0)
                stack(1)
                load_qk(1)
                stack(2)
                stack(3)
                put_maxima(0)
                load_qk(2)
                put_maxima(1)
                stack(4)
                put_maxima(2)
                stack(5)
                load_qk(3)
                put_maxima(3)
                stack(6)
                put_maxima(4)
                stack(7)
                for t in range(5, NQ):
                    put_maxima(t)
                barrier(sp, b, 2)
                sp.dma_start(wo_raw[:], w_attn[3 * KT:4 * KT].rearrange("n p c -> p n c")).then_inc(wo_in, 16)
                sp.dma_start(bo_sb[:], bo).then_inc(wo_in, 16)
                barrier(sp, b, 3)
                barrier(sp, b, 4)

                def ffn_loads(i, w, n, lowrank):
                    f = F[i]

                    def load(p, par, first):
                        t = p * 2 + par
                        if not first:
                            held(sp, f["w_ready"], (b * n + t) * 3 - 3)
                        sp.dma_start(f_raw[par][:], w[t].rearrange("m p c -> p m c")).then_inc(f[f"raw_in{par}"], 16)
                        if lowrank:
                            sp.dma_start(f_lr[par][:], lr0[t]).then_inc(f[f"raw_in{par}"], 16)

                    load(0, 0, True)
                    load(0, 1, True)
                    with sp.Fori(1, n // 2) as p:
                        for par in range(2):
                            load(p, par, False)
                    if n % 2:
                        load(n // 2, 0, False)

                sp.dma_start(f_lrc[:], lr0_const).then_inc(F[0]["lr_const"], 16)
                ffn_loads(0, w_ffn0, NF0, True)
                barrier(sp, b, 5)
                barrier(sp, b, 6)
                for dst, src in ((wdt_raw[:], w_dt), (dtb[:], dt_bias), (alog[:], a_log), (dsk[:], d_skip)):
                    sp.dma_start(dst, src).then_inc(dt_w_in, 16)
                barrier(sp, b, 7)

                def m_load(g, at, use, first=False):
                    if not first:
                        held(sp, m_split, b * (MG * W_PER_G) + use - 1)
                    sp.dma_start(m_raw[:, at % 2, :], w_mamba[g, at]).then_inc(m_raw_in[at % 2], 16)

                sp.dma_start(cpar[:], conv_par[0]).then_inc(cpar_in, 16)
                for n in range(CT):
                    m_load(0, n, n, n < 2)

                def m_group(g, last):
                    for n in range(CT, W_PER_G):
                        m_load(g, n, g * W_PER_G + n)
                    if not last:
                        for n in range(CT - 1):
                            m_load(g + 1, n, g * W_PER_G + (W_PER_G + n))
                        held(sp, conv_ready, b * PROJ_PER_B + g * (2 * CT) + 2 * CT)
                        held(sp, m_split, b * (MG * W_PER_G) + g * W_PER_G + W_PER_G)
                        sp.dma_start(cpar[:], conv_par[g + 1]).then_inc(cpar_in, 16)
                        m_load(g + 1, CT - 1, g * W_PER_G + (W_PER_G + CT - 1))

                with sp.Fori(0, MG - 1) as g:
                    m_group(g, False)
                m_group(MG - 1, True)
                barrier(sp, b, 8)
                barrier(sp, b, 9)
                ffn_loads(1, w_ffn1, NF1, False)
                barrier(sp, b, 10)
                barrier(sp, b, 11)
                sp.dma_start(out[b].rearrange("(t p) d -> p t d", p=P), X[:]).then_inc(out_done, 16)
                held(sp, out_done, b * 16 + 16)

        @block.tensor
        def _(pe):
            pe.wait_ge(consts_ready, 1)

            def three(dst, a_hi, a_lo, w_hi, w_lo, kt, first, last):
                pe.matmul(dst, a_hi(kt), w_hi(kt), start=first, stop=False)
                pe.matmul(dst, a_lo(kt), w_hi(kt), start=False, stop=False)
                return pe.matmul(dst, a_hi(kt), w_lo(kt), start=False, stop=last)

            def tokens(dst, i, w_hi, w_lo, cols=None):
                tok = slice(i * P, (i + 1) * P)
                for kt in range(KT):
                    r = three(dst, lambda k: xhi[:, k, tok], lambda k: xlo[:, k, tok],
                              lambda k: w_hi[:, k, :], lambda k: w_lo[:, k, :], kt, kt == 0, kt == KT - 1)
                return r

            def features(dst, w_hi, w_lo, s):
                tok = slice(s * HALF, (s + 1) * HALF)
                for kt in range(KT):
                    r = three(dst, lambda k: w_hi[:, k * P:(k + 1) * P], lambda k: w_lo[:, k * P:(k + 1) * P],
                              lambda k: xhi[:, k, tok], lambda k: xlo[:, k, tok], kt, kt == 0, kt == KT - 1)
                return r

            def norm_turn(e):
                for i in range(TT):
                    pe.wait_ge(xn_ready, e * TT + i + 1)
                    if i >= 2:
                        pe.wait_ge(xt_free, e * TT + i - 1)
                    for k in range(KT):
                        r = pe.transpose(bank[i % 2][:, k * P:(k + 1) * P], xn[:, i % 2, k * P:(k + 1) * P],
                                         ident[:])
                    r.then_inc(xt_done, 1)

            def ffn(b, i, n, lowrank):
                f = F[i]

                def factor(p, par, m, first=False):
                    t = p * 2 + par
                    if m == 0:
                        pe.wait_ge(f[f"raw_in{par}"], (b * ((n + 1 - par) // 2) + p) * 32 + 32)
                    dst = bank[4 + (3 * par + m) % 2]
                    if not (first and m < 2):
                        pe.wait_ge(f["weff"], (b * n + t) * 3 + m - 1)
                    if m < 2:
                        for k in range(KT):
                            r = pe.matmul(dst[:, k * P:(k + 1) * P],
                                          f_lrc[:, m * D + k * P:m * D + (k + 1) * P],
                                          f_lr[par][:, m * P:(m + 1) * P], start=True, stop=True,
                                          skip_group_check=True)
                    else:
                        r = pe.matmul(dst[:], f_lr[par][:, 2 * P:3 * P], f_lrc[:, 2 * D:3 * D],
                                      start=True, stop=True)
                    r.then_inc(f["lr_done"], 1)

                def gate(t, par, s, first=False):
                    if s == 0:
                        pe.wait_ge(f["w_ready"], (b * n + t) * 3 + 1)
                    if not first:
                        pe.wait_ge(f["hf_done"], (b * n + t) * 2 + s - 1)
                    features(bank[2 * s][:], f_hi[par][:, 0, :], f_lo[par][:, 0, :], s).then_inc(f["g_done"], 1)

                def up(t, par, s):
                    if s == 0:
                        pe.wait_ge(f["w_ready"], (b * n + t) * 3 + 2)
                    features(bank[2 * s + 1][:], f_hi[par][:, 1, :], f_lo[par][:, 1, :], s).then_inc(f["u_done"], 1)

                def down(t, par, i, first=False):
                    if i == 0:
                        pe.wait_ge(f["w_ready"], (b * n + t) * 3 + 3)
                    if i % CPH == 0:
                        pe.wait_ge(f["h_ready"], (b * n + t) * 2 + (i // CPH + 1))
                    for i in (i, i + 1):
                        if not (first and i < 2):
                            pe.wait_ge(f["dn_used"], (b * n + t) * TT + i - 1)
                        tok = slice(i * P, (i + 1) * P)
                        three(bank[6 + i % 2][:], lambda k: h_hi[par][:, tok], lambda k: h_lo[par][:, tok],
                              lambda k: f_hi[par][:, 2, :], lambda k: f_lo[par][:, 2, :], 0, True, True
                              ).then_inc(f["dn_done"], 1)

                def step(p, par, more2, more1, first=False):
                    t = p * 2 + par
                    for q in range(4):
                        if more2 and lowrank and q < 3:
                            factor(p + 1, par, q)
                        if more1:
                            (gate if q % 2 == 0 else up)(t + 1, 1 - par, q // 2)
                        down(t, par, 2 * q, first)

                if lowrank:
                    pe.wait_ge(f["lr_const"], b * 16 + 16)
                    for par in range(2):
                        for m in range(3):
                            factor(0, par, m, par == 0)
                for s in range(2):
                    gate(0, 0, s, True)
                    up(0, 0, s)
                step(0, 0, True, True, True)
                step(0, 1, True, True)
                with pe.Fori(1, (n - 2) // 2) as p:
                    for par in range(2):
                        step(p, par, True, True)
                for t in range((n - 2) // 2 * 2, n):
                    step(t // 2, t % 2, t + 2 < n, t + 1 < n)

            with pe.Fori(0, B) as b:
                norm_turn(b * 4)
                barrier(pe, b, 0)
                pe.wait_ge(wv_ready, b + 1)
                for i in range(TT):
                    if i >= 2:
                        pe.wait_ge(v_free, b * TT + i - 1)
                    tokens(bank[i % 2][:], i, wv_hi, wv_lo).then_inc(v_done, 1)
                barrier(pe, b, 1)
                pe.wait_ge(ones_rows, (b + 1) * (16 * 8))
                pe.wait_ge(o_zero, b + 1)
                ring = 0
                misc = 0
                for what, *arg in ORDER:
                    if what == "proj":
                        f, = arg
                        pe.wait_ge(wqk_ready, b * 8 + 2 * f + 2)
                        for which in range(2):
                            for s in range(2):
                                if ring >= 2:
                                    pe.wait_ge(ring_free, b * RING + ring - 1)
                                features(bank[4 + ring % 2][:], wqk_hi[:, which, :], wqk_lo[:, which, :], s
                                         ).then_inc(ring_done, 1)
                                ring += 1
                    elif what == "piece":
                        t, n = arg
                        h, i, s, cols, diag = PIECES[n]
                        base, buf = 64 * (t % 2), t // 2 % 2
                        if n == 0:
                            pe.wait_ge(stacked[t % 2], (b * (NQ // 2) + t // 2 + 1) * STACKED)
                        pe.wait_ge(ring_free, b * RING + ring - 1)
                        dst = bank[4 + ring % 2]
                        r = pe.matmul(dst[:, 0:cols], stack_q[buf][base:base + ROWS, h, i * P:(i + 1) * P],
                                      stack_k[buf][base:base + ROWS, h, s * HALF:s * HALF + cols],
                                      start=True, stop=True)
                        if diag:
                            r = pe.matmul(dst[:, cols - P:cols], ident_b[:], mask_qk[:], start=False, stop=True,
                                          skip_group_check=True)
                        r.then_inc(ring_done, 1)
                        ring += 1
                    elif what == "maxima":
                        t, = arg
                        pe.wait_ge(mx_ready, b * NQ + t + 1)
                        pe.wait_ge(misc_free, START + b * (3 * NQ) + misc)
                        pe.transpose(bank[7][0:QUAD * TT, 0:P], mx[:, 0, :], ident[:]).then_inc(misc_done, 1)
                        misc += 1
                    elif what == "scores":
                        t, n, p = arg
                        s, j = STEPS[n]
                        lo = max(j * P - s * HALF, 0)
                        base, buf = 64 * (t % 2), t // 2 % 2
                        it = b * (NQ * NS) + (t * NS + n)
                        if n == 0 and p == 0:
                            pe.wait_ge(mt_in, START + (b * NQ + t + 1) * 32)
                        diag = j * P >= s * HALF
                        pe.wait_ge(exp_done[p], START + it)
                        for h in (2 * p, 2 * p + 1):
                            dst = bank[h]
                            r = pe.matmul(dst[:, 0:HALF - lo],
                                          stack_k[buf][base:base + ROWS + 2, h, j * P:(j + 1) * P],
                                          stack_q[buf][base:base + ROWS + 2, h, s * HALF + lo:(s + 1) * HALF],
                                          start=True, stop=True)
                            if diag:
                                r = pe.matmul(dst[:, 0:P], ident_b[:], mask_kq[:], start=False, stop=True,
                                              skip_group_check=True)
                        r.then_inc(st_done[p], 1)
                    elif what == "values":
                        t, n, p = arg
                        s, j = STEPS[n]
                        lo = max(j * P - s * HALF, 0)
                        it = b * (NQ * NS) + (t * NS + n)
                        if j == 0 and p == 0:
                            pe.wait_ge(ot_ready, START + b * (2 * NQ) + 2 * t + s)
                        pe.wait_ge(exp_done[p], START + it + 1)
                        for h in (2 * p, 2 * p + 1):
                            r = pe.matmul(bank[6][32 * h:32 * h + VW, lo:HALF], V[:, j, QUAD * t + h, :],
                                          probs[n % 2][:, h, 0:HALF - lo], start=j == 0,
                                          stop=j == CPH * (s + 1) - 1, skip_group_check=True,
                                          tile_position=(0, 32 * h))
                        if p == 1:
                            r.then_inc(pv_done, 1)
                    elif what == "turn":
                        t, s = arg
                        pe.wait_ge(ot_ready, START + b * (2 * NQ) + 2 * t + s + 1)
                        pe.wait_ge(misc_free, START + b * (3 * NQ) + misc)
                        for k in range(CPH):
                            r = pe.transpose(bank[7][:, k * P:(k + 1) * P], ot[:, k * P:(k + 1) * P], ident[:])
                        r.then_inc(misc_done, 1)
                        misc += 1
                barrier(pe, b, 2)
                for i in range(TT + 1):
                    if i < TT:
                        if i >= 2:
                            pe.wait_ge(at_free, b * TT + i - 1)
                        for k in range(KT):
                            r = pe.transpose(bank[2 + i % 2][:, k * P:(k + 1) * P], Y[:, i, k * P:(k + 1) * P],
                                             ident[:])
                        r.then_inc(at_done, 1)
                    if i > 0:
                        if i == 1:
                            pe.wait_ge(wo_ready, b + 1)
                        pe.wait_ge(at_free, b * TT + i)
                        if i >= 3:
                            pe.wait_ge(o_free, b * TT + i - 2)
                        tokens(bank[(i - 1) % 2][:], i - 1, wo_hi, wo_lo).then_inc(o_done, 1)
                barrier(pe, b, 3)
                norm_turn(b * 4 + 1)
                barrier(pe, b, 4)
                ffn(b, 0, NF0, True)
                barrier(pe, b, 5)
                norm_turn(b * 4 + 2)
                barrier(pe, b, 6)
                pe.wait_ge(dt_w_ready, b + 1)
                for i in range(TT):
                    tokens(bank[0][:, i * MH:(i + 1) * MH], i, wdt_hi, wdt_lo).then_inc(dt_mm, 1)
                pe.wait_ge(dt_a, b + 1)
                for k, m in enumerate((upto, after, ones)):
                    pe.matmul(bank[1 + k][:], m[:], a_all[:].rearrange("p c h -> p (c h)"), start=True, stop=True
                              ).then_inc(dt_cs, 1)
                barrier(pe, b, 7)

                def project(g, s, ft):
                    pe.wait_ge(m_split, b * (MG * W_PER_G) + g * W_PER_G + (ft + 1))
                    features(bank[ft % 2][:], wx_hi[:, ft, :], wx_lo[:, ft, :], s).then_inc(proj_done, 1)

                def bank_read(g, at, uses):
                    if at < 2:
                        pe.wait_ge(pre_ready, b * PROJ_PER_B + CT + g * (2 * CT))
                        pe.wait_ge(gate_used, START + (b * MG + g) * TT)
                        return
                    kind, n = uses[at - 2]
                    if kind == "proj":
                        pe.wait_ge(pre_ready, b * PROJ_PER_B + CT + g * (2 * CT) + (n + 1))
                    else:
                        pe.wait_ge(gate_used, START + (b * MG + g) * TT + (n + 1))

                def turn_out(it):
                    pe.wait_ge(yn_ready, START + it + 1)
                    for k in range(XT):
                        r = pe.transpose(bank[2][:, k * P:(k + 1) * P], yn[:, k * P:(k + 1) * P], ident[:])
                    r.then_inc(yt_done, 1)

                def project_out(it):
                    pe.wait_ge(yt_ready, START + it + 1)
                    for k in range(XT):
                        r = three(bank[3][:], lambda q: yt_hi[:, q, :], lambda q: yt_lo[:, q, :],
                                  lambda q: wy_hi[:, q, :], lambda q: wy_lo[:, q, :], k, k == 0, k == XT - 1)
                    r.then_inc(mo_done, 1)

                def decays(it):
                    pe.wait_ge(au_ready, it + 1)
                    pe.wait_ge(decay_ready, START + it)
                    for q in range(2):
                        h4 = slice(q * HPG // 2, (q + 1) * HPG // 2)
                        dst = bank[4 + q][:].rearrange("p (h l) -> p h l", l=P)
                        pe.matmul(dst, after_r[:], au_hi[:, h4, :], start=True, stop=False)
                        r = pe.matmul(dst, after_r[:], au_lo[:, h4, :], start=False, stop=True)
                    r.then_inc(d_done, 1)

                def m_group(g, first, last):
                    uses = m_uses(last)
                    at = 0
                    for c in range(TT):
                        it = (b * MG + g) * TT + c
                        s, ck = c // CPH, slice(c % CPH * P, (c % CPH + 1) * P)
                        start = first and c == 0
                        if c % CPH == 0:
                            pe.wait_ge(xbc_ready, b * PROJ_PER_B + g * (2 * CT) + (s * CT + CT))
                        pe.wait_ge(yt_ready, START + (it if start else it - 1))
                        pe.wait_ge(x_tm_ready, START + it)
                        for k in range(XT):
                            r = pe.transpose(bank[2][:, k * P:(k + 1) * P], xbc[s][:, k, ck], ident[:])
                        r.then_inc(xtr_done, 1)
                        pe.wait_ge(mo_used, START + (it if start else it - 1))
                        pe.wait_ge(bc_ready, START + it)
                        pe.transpose(bank[3][:, 0:P], xbc[s][:, XT, ck], ident[:])
                        pe.matmul(bank[3][:, P:2 * P], xbc[s][:, XT, ck], xbc[s][:, XT + 1, ck],
                                  start=True, stop=True, skip_group_check=True).then_inc(bc_done, 1)
                        if not start:
                            decays(it)
                        while uses[at][0] == "proj":
                            n = uses[at][1]
                            bank_read(g, at, uses)
                            ft = n % CT
                            if n < CT:
                                features(bank[at % 2][:], wx_hi[:, ft, :], wx_lo[:, ft, :], 1).then_inc(proj_done, 1)
                            else:
                                pe.wait_ge(m_split, b * (MG * W_PER_G) + (g + 1) * W_PER_G + (ft + 1))
                                features(bank[at % 2][:], wx_hi[:, ft, :], wx_lo[:, ft, :], 0).then_inc(proj_done, 1)
                            at += 1
                        if start:
                            decays(it)
                        else:
                            pe.wait_ge(x_tm_ready, START + it + 1)
                            turn_out(it - 1)
                        bank_read(g, at, uses)
                        if c == 0:
                            pe.wait_ge(m_split, b * (MG * W_PER_G) + g * W_PER_G + (CT + KT))
                        tokens(bank[at % 2][:], c, wg_hi, wg_lo).then_inc(gate_done, 1)
                        at += 1
                        pe.wait_ge(state_ready, it + 1)
                        if c == 0:
                            pe.wait_ge(inter_used, START + it)
                        pe.matmul(bank[6][:], xbc[s][:, XT + 1, ck], state[:], start=True, stop=True
                                  ).then_inc(inter_done, 1)
                        pe.wait_ge(m_ready, it + 1)
                        pe.wait_ge(pool_x, START + it + 1)
                        pe.wait_ge(ss_ready, START + it)
                        for h in range(HPG):
                            r = pe.matmul(bank[7][:, h * MP:(h + 1) * MP], decay[:, h, :], xdt[:, h * MP:(h + 1) * MP],
                                          start=True, stop=True, skip_group_check=True)
                        r.then_inc(intra_done, 1)
                        if not start:
                            if c == 1:
                                pe.wait_ge(m_split, b * (MG * W_PER_G) + g * W_PER_G + W_PER_G)
                            pe.wait_ge(bc_ready, START + it + 1)
                            project_out(it - 1)
                        if c < TT - 1:
                            pe.wait_ge(inter_used, START + it + 1)
                            pe.matmul(bank[6][:], b_tm[:], xw[:], start=True, stop=True).then_inc(st_mm, 1)

                for ft in range(CT):
                    if ft >= 2:
                        pe.wait_ge(pre_ready, b * PROJ_PER_B + ft - 1)
                    project(0, 0, ft)
                m_group(0, True, False)
                with pe.Fori(1, MG - 1) as g:
                    m_group(g, False, False)
                m_group(MG - 1, False, True)
                turn_out((b + 1) * (MG * TT) - 1)
                project_out((b + 1) * (MG * TT) - 1)
                barrier(pe, b, 8)
                norm_turn(b * 4 + 3)
                barrier(pe, b, 9)
                ffn(b, 1, NF1, False)
                barrier(pe, b, 10)
                barrier(pe, b, 11)

        @block.scalar
        def _(act):
            act.wait_ge(consts_ready, 1)

            def turned(src):
                return src.rearrange("p (k t) -> p k t", t=P)

            def norm_hi(e):
                for i in range(TT):
                    act.wait_ge(xt_done, e * TT + i + 1)
                    act.copy(xhi[:, :, i * P:(i + 1) * P], turned(bank[i % 2])).then_inc(xt_hi, 1)

            def ffn(b, i, n):
                f = F[i]

                def hidden(p, par, first=False):
                    for s in range(2):
                        it = (b * n + p * 2 + par) * 2 + s
                        act.wait_ge(f["g_done"], it + 1)
                        act.activation(sg[:, s, :], bank[2 * s], ACT.Silu).then_inc(f["sg_done"], 1)
                        act.wait_ge(f["hf_done"], it + 1)
                        if not first:
                            act.wait_ge(f["dn_done"], (b * n + p * 2 + par) * TT - TT)
                        act.copy(h_hi[par][:, s * HALF:(s + 1) * HALF], hf[:, s, :]).then_inc(f["hi_done"], 1)

                hidden(0, 0, True)
                hidden(0, 1, True)
                with act.Fori(1, n // 2) as p:
                    for par in range(2):
                        hidden(p, par)
                if n % 2:
                    hidden(n // 2, 0)

            with act.Fori(0, B) as b:
                norm_hi(b * 4)
                barrier(act, b, 0)
                barrier(act, b, 1)
                ring = 0
                for what, *arg in ORDER:
                    if what == "proj":
                        f, = arg
                        act.wait_ge(wqk_in, (b * (NQ // 2) + f + 1) * 32)
                        if f > 0:
                            act.wait_ge(stacked[0], (b * (NQ // 2) + f) * STACKED)
                            act.wait_ge(stacked[1], (b * (NQ // 2) + f) * STACKED)
                        for which in range(2):
                            for s in range(2):
                                act.wait_ge(ring_done, b * RING + ring + 1)
                                act.activation(part_hi[:, which, s * HALF:(s + 1) * HALF], bank[4 + ring % 2],
                                               ACT.Identity, bias=qk_b[:, which:which + 1]
                                               ).then_inc(part_hi_ready, 1)
                                ring += 1
                    elif what == "piece":
                        ring += 1
                    elif what == "scores":
                        t, n, p = arg
                        s, j = STEPS[n]
                        w = HALF - max(j * P - s * HALF, 0)
                        it = b * (NQ * NS) + (t * NS + n)
                        if p == 0 and (t > 0 or n >= 2):
                            act.wait_ge(pv_done, it - 1)
                        act.wait_ge(st_done[p], it + 1)
                        act.activation(probs[n % 2][:, 2 * p:2 * p + 2, 0:w], banks[:, 2 * p:2 * p + 2, 0:w],
                                       ACT.Exp, scale=1.0 / HD ** 0.5).then_inc(exp_done[p], 1)
                barrier(act, b, 2)
                for i in range(TT):
                    act.wait_ge(at_done, b * TT + i + 1)
                    act.copy(xhi[:, :, i * P:(i + 1) * P], turned(bank[2 + i % 2])).then_inc(at_hi, 1)
                barrier(act, b, 3)
                norm_hi(b * 4 + 1)
                barrier(act, b, 4)
                ffn(b, 0, NF0)
                barrier(act, b, 5)
                norm_hi(b * 4 + 2)
                barrier(act, b, 6)
                act.wait_ge(dt_w_in, (b + 1) * 64)
                act.activation(neg_a[:], alog[:], ACT.Exp)
                act.wait_ge(dt_sum, b + 1)
                act.activation(dt_abs[:], dt_in[:], ACT.Abs)
                act.drain()
                act.activation(dt_abs[:], dt_abs[:], ACT.Exp, scale=-1.0)
                act.drain()
                act.activation(dt_sp[:], dt_abs[:], ACT.Ln, bias=ones[:, 0:1]).then_inc(dt_soft, 1)
                for k in (EC, WE, ED):
                    act.wait_ge(dt_cs, b * 3 + k + 1)
                    act.activation(tab[:, k, :, :].rearrange("p c h -> p (c h)"), bank[1 + k], ACT.Exp
                                   ).then_inc(dt_exp, 1)
                barrier(act, b, 7)

                def before_conv(src, pi, n, s, first=False):
                    ft, par = n % CT, n % 2
                    act.drain()
                    act.wait_ge(proj_done, pi + 1)
                    if not first:
                        act.wait_ge(xbc_ready, pi - 1)
                    act.copy(pre[par][:, 0:MK - 1], carry[:, ft, :] if s else zeros[:, 0:MK - 1])
                    act.copy(pre[par][:, MK - 1:], src)
                    if not s:
                        act.copy(carry[:, ft, :], src[:, HALF - MK + 1:HALF])
                    o = ft * (MK + 1)
                    act.activation(conv[par][:], src, ACT.Identity, scale=cpar[:, o + MK - 1:o + MK],
                                   bias=cpar[:, o + MK:o + MK + 1]).then_inc(pre_ready, 1)

                def conv_tanh(pi, n, s):
                    act.wait_ge(conv_ready, pi + 1)
                    act.activation(xbc[s][:, n % CT, :], conv[n % 2][:], ACT.Tanh, scale=0.5).then_inc(cth_ready, 1)

                def turned_hi(it):
                    act.wait_ge(yt_done, it + 1)
                    act.wait_ge(mo_done, START + it)
                    act.copy(yt_hi[:], turned(bank[2])).then_inc(yt_hi_ready, 1)

                def decay_exp(it):
                    act.wait_ge(d_done, START + it + 1)
                    act.wait_ge(intra_done, START + it)
                    act.activation(decay[:].rearrange("p (a h) l -> p a (h l)", a=2), banks[:, 4:6, :], ACT.Exp
                                   ).then_inc(decay_ready, 1)

                def split_hi(dst, n, g):
                    act.wait_ge(m_raw_in[n % 2], (b * (MG * W_PER_G // 2) + g * (W_PER_G // 2) + n // 2) * 16 + 16)
                    raw = m_raw[:, n % 2, :]
                    if n >= CT + KT:
                        col = CT * (MK + 1) + (n - CT - KT)
                        act.activation(raw, raw, ACT.Copy, scale=cpar[:, col:col + 1])
                        act.drain()
                    act.copy(dst, raw).then_inc(m_hi, 1)

                def m_group(g, first, last):
                    uses = m_uses(last)
                    at = 0
                    p0 = b * PROJ_PER_B + g * (2 * CT) + CT
                    for c in range(TT):
                        it = (b * MG + g) * TT + c
                        start = first and c == 0
                        act.wait_ge(xtr_done, it + 1)
                        act.wait_ge(pool_x, START + it)
                        act.copy(x_tm[:], bank[2]).then_inc(x_tm_ready, 1)
                        if c == 0 and not first:
                            for k in range(2, KT):
                                split_hi(wg_hi[:, k, :], CT + k, g)
                        if not start:
                            decay_exp(it)
                        while uses[at][0] == "proj":
                            n = uses[at][1]
                            if n == CT:
                                held(act, cpar_in, (b * MG + g + 2) * 16)
                            s1 = 1 if n < CT else 0
                            before_conv(bank[at % 2], p0 + n, n, s1)
                            if n % CT:
                                conv_tanh(p0 + (n - 1), n - 1, s1)
                            if n % CT == CT - 1:
                                conv_tanh(p0 + n, n, s1)
                            at += 1
                        if start:
                            decay_exp(it)
                        else:
                            turned_hi(it - 1)
                        act.wait_ge(gate_done, START + it + 1)
                        act.wait_ge(yn_ready, START + it)
                        act.activation(g_th[:], bank[at % 2], ACT.Tanh, scale=0.5).then_inc(gate_th, 1)
                        at += 1
                        act.wait_ge(y_ready, START + it + 1)
                        act.activation(bank[7], yv[:], ACT.Square, accum_out=ss[:]).then_inc(ss_ready, 1)
                        if c == 0:
                            act.wait_ge(mo_done, START + it)
                            for k in range(XT):
                                split_hi(wy_hi[:, k, :], CT + KT + k, g)
                        if not last:
                            if c == TT - 1:
                                for k in range(2):
                                    split_hi(wg_hi[:, k, :], CT + k, g + 1)
                            for ft in SPLIT_AT.get(c, ()):
                                act.wait_ge(proj_done, b * PROJ_PER_B + g * (2 * CT) + (CT + ft + 1))
                                split_hi(wx_hi[:, ft, :], ft, g + 1)

                held(act, cpar_in, (b * MG + 1) * 16)
                for n in range(CT):
                    split_hi(wx_hi[:, n, :], n, 0)
                for k in range(KT):
                    split_hi(wg_hi[:, k, :], CT + k, 0)
                for n in range(CT):
                    pi = b * PROJ_PER_B + n
                    before_conv(bank[n % 2], pi, n, 0, n < 2)
                    if n:
                        conv_tanh(pi - 1, n - 1, 0)
                conv_tanh(b * PROJ_PER_B + (CT - 1), CT - 1, 0)
                m_group(0, True, False)
                with act.Fori(1, MG - 1) as g:
                    m_group(g, False, False)
                m_group(MG - 1, False, True)
                turned_hi((b + 1) * (MG * TT) - 1)
                barrier(act, b, 8)
                norm_hi(b * 4 + 3)
                barrier(act, b, 9)
                ffn(b, 1, NF1)
                barrier(act, b, 10)
                barrier(act, b, 11)

        @block.vector
        def _(dve):
            dve.wait_ge(consts_ready, 1)

            def mean_rstd(src, var_sem, rstd_sem, e):
                dve.drain()
                for i in range(TT):
                    dve.bn_stats(stats[:, i, :], src[:, i, :])
                dve.drain()
                for i in range(TT):
                    dve.bn_aggr(mv[:, i, :], stats[:, i, :])
                dve.drain()
                dve.tensor_scalar(var_eps[:], mv[:, :, 1], EPS, None, ALU.add).then_inc(var_sem, 1)
                dve.wait_ge(rstd_sem, e + 1)

            def add_normed(e):
                mean_rstd(Y, post_var, post_rstd, e)
                for i in range(TT):
                    dve.tensor_scalar(Y[:, i, :], Y[:, i, :], mv[:, i, 0:1], rstd[:, i:i + 1],
                                      ALU.subtract, ALU.mult)
                dve.drain()
                for i in range(TT):
                    dve.tensor_tensor(X[:, i, :], X[:, i, :], Y[:, i, :], ALU.add)

            def norm_lo(e, i):
                dve.wait_ge(xt_hi, e * TT + i + 1)
                dve.tensor_tensor(xlo[:, :, i * P:(i + 1) * P], bank[i % 2].rearrange("p (k t) -> p k t", t=P),
                                  xhi[:, :, i * P:(i + 1) * P].bitcast(F32), ALU.subtract).then_inc(xt_free, 1)

            def norm_x(e):
                mean_rstd(X, pre_var, pre_rstd, e)
                for i in range(TT):
                    if i >= 2:
                        dve.wait_ge(xt_done, e * TT + i - 1)
                    dve.tensor_scalar(xn[:, i % 2, :], X[:, i, :], mv[:, i, 0:1], rstd[:, i:i + 1],
                                      ALU.subtract, ALU.mult).then_inc(xn_ready, 1)
                    if i:
                        norm_lo(e, i - 1)
                norm_lo(e, TT - 1)

            def ffn(b, i, n, lowrank):
                f = F[i]

                def scale(p, par, m):
                    it = (b * n + p * 2 + par) * 3 + m
                    dve.wait_ge(f["lr_done"], it + 1)
                    dve.tensor_tensor(f_raw[par][:, m, :], f_raw[par][:, m, :], bank[4 + (3 * par + m) % 2],
                                      ALU.mult).then_inc(f["weff"], 1)

                def hidden(t, par, s):
                    it = (b * n + t) * 2 + s
                    dve.drain()
                    dve.wait_ge(f["sg_done"], it + 1)
                    dve.wait_ge(f["u_done"], it + 1)
                    dve.tensor_tensor(hf[:, s, :], sg[:, s, :], bank[2 * s + 1], ALU.mult).then_inc(f["hf_done"], 1)

                def hidden_lo(t, par, s):
                    dve.wait_ge(f["hi_done"], (b * n + t) * 2 + s + 1)
                    cols = slice(s * HALF, (s + 1) * HALF)
                    dve.tensor_tensor(h_lo[par][:, cols], hf[:, s, :], h_hi[par][:, cols].bitcast(F32),
                                      ALU.subtract).then_inc(f["h_ready"], 1)

                def gather(t, i):
                    for i in (i, i + 1):
                        dve.wait_ge(f["dn_done"], (b * n + t) * TT + (i + 1))
                        dve.tensor_tensor(Y[:, i, :], bank[6 + i % 2], Y[:, i, :], ALU.add).then_inc(f["dn_used"], 1)

                def step(p, par, more2, more1):
                    t = p * 2 + par
                    for q in range(4):
                        if more2 and lowrank and q < 3:
                            scale(p + 1, par, q)
                        if more1 and q % 2:
                            hidden(t + 1, 1 - par, q // 2)
                        gather(t, 2 * q)
                        if more1 and q % 2:
                            hidden_lo(t + 1, 1 - par, q // 2)

                if lowrank:
                    for par in range(2):
                        for m in range(3):
                            scale(0, par, m)
                for s in range(2):
                    hidden(0, 0, s)
                    dve.drain()
                    hidden_lo(0, 0, s)
                held(dve, f["y_zero"], b + 1)
                with dve.Fori(0, (n - 2) // 2) as p:
                    for par in range(2):
                        step(p, par, True, True)
                for t in range((n - 2) // 2 * 2, n):
                    step(t // 2, t % 2, t + 2 < n, t + 1 < n)

            with dve.Fori(0, B) as b:
                held(dve, x_in, b * 16 + 16)
                norm_x(b * 4)
                barrier(dve, b, 0)
                dve.memset(V[:, :, :, HD:VW], 1.0)
                dve.wait_ge(wv_in, b * 32 + 32)
                for i in range(TT):
                    dve.wait_ge(v_done, b * TT + i + 1)
                    dve.tensor_tensor(V[:, i, :, 0:HD], bank[i % 2].rearrange("p (h d) -> p h d", d=HD),
                                      bv_sb[:].rearrange("p (h d) -> p h d", d=HD), ALU.add).then_inc(v_free, 1)
                barrier(dve, b, 1)
                dve.memset(bank[6], 0.0).then_inc(o_zero, 1)
                ring, misc, mx_turned = 0, 0, 0
                for what, *arg in ORDER:
                    if what == "proj":
                        f, = arg
                        for which in range(2):
                            for s in range(2):
                                cols = slice(s * HALF, (s + 1) * HALF)
                                dve.wait_ge(part_hi_ready, b * 16 + 4 * f + 2 * which + s + 1)
                                dve.scalar_tensor_tensor(out=part_lo[:, which, cols], in0=bank[4 + ring % 2],
                                                         scalar=qk_b[:, which:which + 1],
                                                         in1=part_hi[:, which, cols].bitcast(F32),
                                                         op0=ALU.add, op1=ALU.subtract
                                                         ).then_inc(part_lo_ready, 1)
                                dve.drain().then_inc(ring_free, 1)
                                ring += 1
                    elif what == "piece":
                        t, n = arg
                        h, i, s, cols, _ = PIECES[n]
                        if n == 0 and t > 0:
                            dve.wait_ge(misc_done, b * (3 * NQ) + mx_turned)
                        dve.wait_ge(ring_done, b * RING + ring + 1)
                        dve.tensor_reduce(mx[:, s, h * TT + i:h * TT + i + 1], bank[4 + ring % 2][:, 0:cols],
                                          AX.X, ALU.max).then_inc(ring_free, 1)
                        ring += 1
                    elif what == "maxima":
                        t, = arg
                        dve.drain()
                        m0, m1 = (mx[:, q, :].rearrange("p (h i) -> p h i", i=TT)[:, :, CPH:TT] for q in range(2))
                        dve.tensor_tensor(m0, m0, m1, ALU.max).then_inc(mx_ready, 1)
                        misc += 1
                        mx_turned = misc
                        dve.wait_ge(misc_done, b * (3 * NQ) + misc)
                        dve.wait_ge(mt_in, START + (b * NQ + t) * 32)
                        src = bank[7][0:QUAD * TT, 0:P]
                        dve.tensor_scalar(mt_hi[:], src, -1.0, None, ALU.mult)
                        dve.drain()
                        dve.scalar_tensor_tensor(out=mt_lo[:], in0=src, scalar=-1.0, in1=mt_hi[:].bitcast(F32),
                                                 op0=ALU.mult, op1=ALU.subtract
                                                 ).then_inc(mt_ready, 1)
                        dve.drain().then_inc(misc_free, 1)
                    elif what == "values":
                        t, n, p = arg
                        s, j = STEPS[n]
                        if p == 1 and j == CPH * (s + 1) - 1:
                            dve.wait_ge(pv_done, b * (NQ * NS) + (t * NS + n) + 1)
                            dve.tensor_copy(ot[:], bank[6]).then_inc(ot_ready, 1)
                    elif what == "turn":
                        t, s = arg
                        misc += 1
                        dve.wait_ge(misc_done, b * (3 * NQ) + misc)
                        o = bank[7].rearrange("p (k h r) -> p k h r", k=CPH, h=QUAD)
                        dve.reciprocal(rsum[:], o[:, :, :, HD])
                        dve.drain()
                        cols = slice(t * QUAD * HD, (t + 1) * QUAD * HD)
                        dst = Y[:, s * CPH:(s + 1) * CPH, cols].rearrange("p k (h d) -> p k h d", d=HD)
                        dve.tensor_tensor(dst, o[:, :, :, 0:HD],
                                          rsum[:].unsqueeze(3).broadcast_to([P, CPH, QUAD, HD]), ALU.mult
                                          ).then_inc(misc_free, 1)
                barrier(dve, b, 2)
                dve.wait_ge(wo_in, b * 32 + 32)
                for i in range(TT + 1):
                    if i < TT:
                        dve.wait_ge(at_hi, b * TT + i + 1)
                        tok = slice(i * P, (i + 1) * P)
                        dve.tensor_tensor(xlo[:, :, tok], bank[2 + i % 2].rearrange("p (k t) -> p k t", t=P),
                                          xhi[:, :, tok].bitcast(F32), ALU.subtract).then_inc(at_free, 1)
                    if i > 0:
                        dve.wait_ge(o_done, b * TT + i)
                        dve.tensor_tensor(Y[:, i - 1, :], bank[(i - 1) % 2], bo_sb[:], ALU.add).then_inc(o_free, 1)
                barrier(dve, b, 3)
                add_normed(b * 4)
                norm_x(b * 4 + 1)
                barrier(dve, b, 4)
                ffn(b, 0, NF0, True)
                barrier(dve, b, 5)
                add_normed(b * 4 + 1)
                norm_x(b * 4 + 2)
                barrier(dve, b, 6)
                def by_token(par_tile):
                    return par_tile[:].unsqueeze(1).broadcast_to([P, TT, MH])

                dve.wait_ge(dt_w_in, (b + 1) * 64)
                dve.tensor_scalar(d_half[:], dsk[:], 0.5, None, ALU.mult)
                dve.wait_ge(dt_mm, (b + 1) * TT)
                dve.tensor_tensor(dt_in[:], bank[0].rearrange("p (c h) -> p c h", h=MH), by_token(dtb), ALU.add
                                  ).then_inc(dt_sum, 1)
                dve.wait_ge(dt_soft, b + 1)
                dve.scalar_tensor_tensor(out=dt_sp[:], in0=dt_in[:], scalar=0.0, in1=dt_sp[:],
                                         op0=ALU.max, op1=ALU.add)
                dve.tensor_scalar(neg_a[:], neg_a[:], -1.0, None, ALU.mult)
                dve.drain()
                dve.tensor_tensor(a_all[:], dt_sp[:], by_token(neg_a), ALU.mult).then_inc(dt_a, 1)
                dve.tensor_scalar(tab[:, DTH, :, :], dt_sp[:], 0.5, None, ALU.mult)
                dve.drain()
                dve.tensor_copy(a_r[:], a_all[:])
                dve.drain()
                dve.tensor_copy(tab[:, AHI, :, :], a_r[:].bitcast(F32))
                dve.tensor_tensor(tab[:, ALO, :, :], a_all[:], a_r[:].bitcast(F32), ALU.subtract)
                dve.wait_ge(dt_exp, b * 3 + 3)
                dve.tensor_scalar(tab[:, EC, :, :], tab[:, EC, :, :], 0.5, None, ALU.mult)
                dve.scalar_tensor_tensor(out=tab[:, WE, :, :], in0=tab[:, WE, :, :], scalar=0.25, in1=dt_sp[:],
                                         op0=ALU.mult, op1=ALU.mult)
                barrier(dve, b, 7)

                def convolve(pi, n):
                    ft, par = n % CT, n % 2
                    dve.wait_ge(pre_ready, pi + 1)
                    for k in range(MK - 1):
                        o = ft * (MK + 1) + k
                        r = dve.scalar_tensor_tensor(out=conv[par][:], in0=pre[par][:, k:k + HALF],
                                                     scalar=cpar[:, o:o + 1], in1=conv[par][:],
                                                     op0=ALU.mult, op1=ALU.add)
                        if k < MK - 2:
                            dve.drain()
                    r.then_inc(conv_ready, 1)

                def twice_silu(pi, n, s):
                    dve.wait_ge(cth_ready, pi + 1)
                    dve.scalar_tensor_tensor(out=xbc[s][:, n % CT, :], in0=xbc[s][:, n % CT, :], scalar=1.0,
                                             in1=conv[n % 2][:], op0=ALU.add, op1=ALU.mult).then_inc(xbc_ready, 1)

                def masked(it, sm):
                    dve.wait_ge(bc_done, it + 1)
                    dve.wait_ge(st_mm, START + sm)
                    dve.tensor_copy(b_tm[:], bank[3][:, 0:P])
                    dve.tensor_tensor(cb[:], bank[3][:, P:2 * P], quarter[:], ALU.mult).then_inc(bc_ready, 1)
                    dve.drain()
                    dve.wait_ge(decay_ready, START + it + 1)
                    dve.tensor_tensor(decay[:], decay[:], cb[:].unsqueeze(1).broadcast_to([P, HPG, P]), ALU.mult
                                      ).then_inc(m_ready, 1)

                def turned_lo(it):
                    dve.wait_ge(yt_hi_ready, it + 1)
                    dve.tensor_tensor(yt_lo[:], bank[2].rearrange("p (k t) -> p k t", t=P), yt_hi[:].bitcast(F32),
                                      ALU.subtract).then_inc(yt_ready, 1)

                def gather(it, c):
                    dve.wait_ge(mo_done, START + it + 1)
                    dve.tensor_tensor(Y[:, c, :], bank[3], Y[:, c, :], ALU.add).then_inc(mo_used, 1)

                def by_head(t):
                    return t.rearrange("p (h d) -> p h d", d=MP)

                def tables(g, s):
                    heads = bass.ds(g * HPG, HPG)
                    for kind in range(6):
                        dve.tensor_copy(gt[:, kind, s * CPH:(s + 1) * CPH, :],
                                        tab[:, kind, s * CPH:(s + 1) * CPH, heads])
                    dve.tensor_copy(gd[:, s, :], d_half[:, heads]).then_inc(gt_ready, 1)

                def m_group(g, first, last):
                    uses = m_uses(last)
                    at = 0
                    p0 = b * PROJ_PER_B + g * (2 * CT) + CT
                    sm = (b * MG + g) * (TT - 1)
                    held(dve, inter_done, START + (b * MG + g) * TT)
                    dve.memset(state[:], 0.0).then_inc(state_ready, 1)
                    for c in range(TT):
                        it = (b * MG + g) * TT + c
                        start = first and c == 0
                        if not start:
                            masked(it, sm + c)
                        while uses[at][0] == "proj":
                            n = uses[at][1]
                            s1 = 1 if n < CT else 0
                            convolve(p0 + n, n)
                            if n % CT:
                                twice_silu(p0 + (n - 1), n - 1, s1)
                            if n % CT == CT - 1:
                                twice_silu(p0 + n, n, s1)
                            at += 1
                        if start:
                            masked(it, sm)
                        else:
                            turned_lo(it - 1)
                        dve.wait_ge(gate_th, it + 1)
                        dve.scalar_tensor_tensor(out=g_th[:], in0=g_th[:], scalar=1.0, in1=bank[at % 2],
                                                 op0=ALU.add, op1=ALU.mult).then_inc(gate_used, 1)
                        at += 1
                        dve.wait_ge(inter_done, START + it + 1)
                        dve.tensor_tensor(by_head(yv[:]), by_head(bank[6]),
                                          gt[:, EC, c, :].unsqueeze(2).broadcast_to([P, HPG, MP]), ALU.mult
                                          ).then_inc(inter_used, 1)
                        dve.drain()
                        dve.wait_ge(intra_done, START + it + 1)
                        dve.tensor_tensor(yv[:], yv[:], bank[7], ALU.add)
                        dve.drain()
                        dve.wait_ge(pool_x, START + it + 1)
                        dve.tensor_tensor(yv[:], yv[:], xd[:], ALU.add).then_inc(y_ready, 1)
                        if c == 1:
                            tables(g, 1)
                        if c == TT - 2 and not last:
                            tables(g + 1, 0)
                        if not start:
                            gather(it - 1, (c - 1) % TT)
                        if c < TT - 1:
                            dve.wait_ge(st_mm, START + sm + (c + 1))
                            dve.wait_ge(state_dec, sm + (c + 1))
                            dve.tensor_tensor(state[:], state[:], bank[6], ALU.add).then_inc(state_ready, 1)
                        dve.wait_ge(rg_ready, it + 1)
                        dve.scalar_tensor_tensor(out=yn[:], in0=yv[:], scalar=rg[:], in1=g_th[:],
                                                 op0=ALU.mult, op1=ALU.mult).then_inc(yn_ready, 1)

                tables(0, 0)
                for n in range(CT):
                    pi = b * PROJ_PER_B + n
                    convolve(pi, n)
                    if n:
                        twice_silu(pi - 1, n - 1, 0)
                twice_silu(b * PROJ_PER_B + (CT - 1), CT - 1, 0)
                held(dve, m_zero, b + 1)
                m_group(0, True, False)
                with dve.Fori(1, MG - 1) as g:
                    m_group(g, False, False)
                m_group(MG - 1, False, True)
                turned_lo((b + 1) * (MG * TT) - 1)
                gather((b + 1) * (MG * TT) - 1, TT - 1)
                barrier(dve, b, 8)
                add_normed(b * 4 + 2)
                norm_x(b * 4 + 3)
                barrier(dve, b, 9)
                ffn(b, 1, NF1, False)
                barrier(dve, b, 10)
                add_normed(b * 4 + 3)
                barrier(dve, b, 11)

        @block.gpsimd
        def _(pool):
            pool.memset(zeros[:], 0.0)
            pool.memset(ones[:], 1.0)
            pool.memset(half_neg[:], -0.5)
            for m, v in ((ident, 0.0), (ident_b, 0.0), (mask_qk, 0.0), (mask_kq, 0.0), (quarter, 0.25)):
                pool.memset(m[:], v)
            pool.drain()

            def select(m, src, op, p_step, x_step, fill):
                pool.affine_select(out=m[:], in_=src[:], compare_op=op, fill=fill, base=0,
                                   pattern=[[x_step, P]], channel_multiplier=p_step)

            select(ident, ident, ALU.not_equal, 1, -1, 1.0)
            select(ident_b, ident_b, ALU.not_equal, 1, -1, 1.0)
            select(mask_qk, mask_qk, ALU.is_ge, 1, -1, NEG)
            select(mask_kq, mask_kq, ALU.is_ge, -1, 1, NEG)
            select(quarter, quarter, ALU.is_ge, -1, 1, 0.0)
            select(upto, ones, ALU.is_ge, -1, 1, 0.0)
            select(after, ones, ALU.is_gt, 1, -1, 0.0)
            pool.drain()
            pool.tensor_copy(after_r[:], after[:])
            for semaphore in started:
                pool.drain().then_inc(semaphore, START)
            pool.drain().then_inc(consts_ready, 1)

            def split(hi, lo, raw):
                pool.tensor_scalar(hi, raw, 1.0, 1.0, ALU.mult, ALU.mult)
                pool.drain()
                return pool.tensor_tensor(lo, raw, hi.bitcast(F32), ALU.subtract)

            def root(var_sem, rstd_sem, e):
                pool.wait_ge(var_sem, e + 1)
                pool.tensor_tensor(rstd[:], var_eps[:], half_neg[:], ALU.pow).then_inc(rstd_sem, 1)

            def ffn(b, i, n, lowrank):
                f = F[i]
                pool.memset(Y[:], 0.0).then_inc(f["y_zero"], 1)

                def split_tile(p, par, first=False):
                    t = b * n + p * 2 + par
                    for m in range(3):
                        if lowrank:
                            held(pool, f["weff"], t * 3 + (m + 1))
                        elif m == 0:
                            held(pool, f[f"raw_in{par}"], (b * ((n + 1 - par) // 2) + p) * 16 + 16)
                        if not first:
                            if m == 0:
                                held(pool, f["u_done"], t * 2 - 2)
                            if m == 2:
                                held(pool, f["dn_done"], t * TT - TT)
                        split(f_hi[par][:, m, :], f_lo[par][:, m, :], f_raw[par][:, m, :]).then_inc(f["w_ready"], 1)

                split_tile(0, 0, True)
                split_tile(0, 1, True)
                with pool.Fori(1, n // 2) as p:
                    for par in range(2):
                        split_tile(p, par)
                if n % 2:
                    split_tile(n // 2, 0)

            with pool.Fori(0, B) as b:
                root(pre_var, pre_rstd, b * 4)
                barrier(pool, b, 0)
                held(pool, wv_in, b * 32 + 32)
                split(wv_hi[:], wv_lo[:], wv_raw[:]).then_inc(wv_ready, 1)
                barrier(pool, b, 1)
                ring = 0
                for what, *arg in ORDER:
                    if what == "proj":
                        f, = arg
                        held(pool, wqk_in, (b * (NQ // 2) + f + 1) * 32)
                        if f > 0:
                            held(pool, ring_done, b * RING + wqk_last_use)
                        split(wqk_hi[:], wqk_lo[:], wqk_raw[:]).then_inc(wqk_ready, 2)
                        ring += 4
                        wqk_last_use = ring
                    elif what == "piece":
                        ring += 1
                barrier(pool, b, 2)
                held(pool, wo_in, b * 32 + 32)
                split(wo_hi[:], wo_lo[:], wo_raw[:]).then_inc(wo_ready, 1)
                barrier(pool, b, 3)
                root(post_var, post_rstd, b * 4)
                root(pre_var, pre_rstd, b * 4 + 1)
                barrier(pool, b, 4)
                ffn(b, 0, NF0, True)
                barrier(pool, b, 5)
                root(post_var, post_rstd, b * 4 + 1)
                root(pre_var, pre_rstd, b * 4 + 2)
                barrier(pool, b, 6)
                held(pool, dt_w_in, (b + 1) * 64)
                split(wdt_hi[:], wdt_lo[:], wdt_raw[:]).then_inc(dt_w_ready, 1)
                barrier(pool, b, 7)

                pool.memset(Y[:], 0.0).then_inc(m_zero, 1)

                def split_lo(hi, lo, n, g):
                    pool.wait_ge(m_hi, b * (MG * W_PER_G) + g * W_PER_G + (n + 1))
                    pool.tensor_tensor(lo, m_raw[:, n % 2, :], hi.bitcast(F32), ALU.subtract).then_inc(m_split, 1)

                def decay_terms(c, it):
                    pool.wait_ge(d_done, START + it)
                    for dst, kind in ((au_hi, AHI), (au_lo, ALO)):
                        r = pool.tensor_tensor(dst[:], upto[:].unsqueeze(1).broadcast_to([P, HPG, P]),
                                               gt[:, kind, c, :].unsqueeze(2).broadcast_to([P, HPG, P]), ALU.mult)
                    r.then_inc(au_ready, 1)

                def by_head(t):
                    return t.rearrange("p (h d) -> p h d", d=MP)

                def per_head(t):
                    return t.unsqueeze(2).broadcast_to([P, HPG, MP])

                def m_group(g, first, last):
                    sm = (b * MG + g) * (TT - 1)
                    for c in range(TT):
                        it = (b * MG + g) * TT + c
                        pool.wait_ge(x_tm_ready, START + it + 1)
                        pool.wait_ge(intra_done, START + it)
                        pool.tensor_tensor(by_head(xdt[:]), by_head(x_tm[:]), per_head(gt[:, DTH, c, :]), ALU.mult)
                        if c < TT - 1:
                            pool.wait_ge(st_mm, START + sm + c)
                            pool.tensor_tensor(by_head(xw[:]), by_head(x_tm[:]), per_head(gt[:, WE, c, :]), ALU.mult)
                        pool.wait_ge(y_ready, START + it)
                        pool.tensor_tensor(by_head(xd[:]), by_head(x_tm[:]), per_head(gd[:, c // CPH, :]), ALU.mult
                                           ).then_inc(pool_x, 1)
                        if c == 0 and not first:
                            for k in range(2, KT):
                                split_lo(wg_hi[:, k, :], wg_lo[:, k, :], CT + k, g)
                        if c < TT - 1:
                            pool.wait_ge(state_ready, it + 1)
                            pool.wait_ge(inter_done, START + it + 1)
                            pool.tensor_tensor(by_head(state[:]), by_head(state[:]), per_head(gt[:, ED, c, :]),
                                               ALU.mult).then_inc(state_dec, 1)
                            if c == CPH - 1:
                                pool.wait_ge(gt_ready, (b * MG + g) * 2 + 2)
                            decay_terms(c + 1, it + 1)
                        elif not last:
                            pool.wait_ge(gt_ready, (b * MG + g) * 2 + 3)
                            decay_terms(0, it + 1)
                        held(pool, ss_ready, START + it + 1)
                        pool.tensor_scalar(rg[:], ss[:], 4.0 / GI, 4 * EPS, ALU.mult, ALU.add)
                        pool.drain()
                        pool.tensor_tensor(rg[:], rg[:], half_neg[:, 0:1], ALU.pow).then_inc(rg_ready, 1)
                        if c == 0:
                            for k in range(XT):
                                split_lo(wy_hi[:, k, :], wy_lo[:, k, :], CT + KT + k, g)
                        if not last:
                            if c == TT - 1:
                                for k in range(2):
                                    split_lo(wg_hi[:, k, :], wg_lo[:, k, :], CT + k, g + 1)
                            for ft in SPLIT_AT.get(c, ()):
                                split_lo(wx_hi[:, ft, :], wx_lo[:, ft, :], ft, g + 1)

                for ft in range(CT):
                    split_lo(wx_hi[:, ft, :], wx_lo[:, ft, :], ft, 0)
                for k in range(KT):
                    split_lo(wg_hi[:, k, :], wg_lo[:, k, :], CT + k, 0)
                pool.wait_ge(gt_ready, b * (2 * MG) + 1)
                decay_terms(0, b * (MG * TT))
                m_group(0, True, False)
                with pool.Fori(1, MG - 1) as g:
                    m_group(g, False, False)
                m_group(MG - 1, False, True)
                barrier(pool, b, 8)
                root(post_var, post_rstd, b * 4 + 2)
                root(pre_var, pre_rstd, b * 4 + 3)
                barrier(pool, b, 9)
                ffn(b, 1, NF1, False)
                barrier(pool, b, 10)
                root(post_var, post_rstd, b * 4 + 3)
                barrier(pool, b, 11)


def kernel(**inputs):
    import numpy as np
    import concourse.bacc as bacc
    from concourse.bass_utils import run_bass_kernel_spmd as run

    a = {k: np.asarray(v) for k, v in inputs.items()}

    def by_out(w):
        n = w.shape[0] // P
        return w.reshape(n, P, KT, P).transpose(0, 3, 2, 1).reshape(n, P, KT * P)

    def by_in(w):
        return w.T.reshape(-1, P, w.shape[0])

    def rows(w, n):
        return np.pad(w, ((0, n - w.shape[0]), (0, 0)))

    def everywhere(v):
        return np.broadcast_to(v[None, :], (P, v.shape[0]))

    wq, wk = by_out(a["L0_attn_Wq"]), by_out(a["L0_attn_Wk"])
    qk = np.stack([wq, wk], 1).reshape(2 * KT, P, D)
    arrays = {
        "x": a["L0_attn_x"],
        "w_attn": np.concatenate([by_in(a["L0_attn_Wv"]), qk, by_in(a["L0_attn_Wo"])]),
        "qk_bias": np.stack([a["L0_attn_bq"].reshape(KT, P), a["L0_attn_bk"].reshape(KT, P)], 2),
        "bv": everywhere(a["L0_attn_bv"]),
        "bo": everywhere(a["L0_attn_bo"]),
        "w_ffn0": np.stack([by_out(a["L0_ffn_gate_w"]), by_out(a["L0_ffn_up_w"]), by_in(a["L0_ffn_down_w"])], 1),
        "lr0": np.concatenate([a["L0_ffn_gate_su"].reshape(NF0, P, RANK).transpose(0, 2, 1),
                               a["L0_ffn_up_su"].reshape(NF0, P, RANK).transpose(0, 2, 1),
                               a["L0_ffn_down_sv"].reshape(RANK, NF0, P).transpose(1, 0, 2)], 2),
        "lr0_const": np.concatenate([a["L0_ffn_gate_sv"], a["L0_ffn_up_sv"], a["L0_ffn_down_su"].T], 1),
    }
    gate_up = a["L1_ffn_w_gate_up"]
    half = gate_up.shape[0] // 2
    arrays["w_ffn1"] = np.stack([by_out(rows(gate_up[:half], NF1 * P)), by_out(rows(gate_up[half:], NF1 * P)),
                                 by_in(rows(a["L1_ffn_w_down"].T, NF1 * P).T)], 1)

    inner, gn = MH * MP, MG * MN
    proj = a["L1_attn_in_proj_w"]

    def channels(v):
        rest = v.shape[1:]
        return np.concatenate([v[:inner].reshape(MG, XT, P, *rest), v[inner:inner + gn].reshape(MG, 1, P, *rest),
                               v[inner + gn:].reshape(MG, 1, P, *rest)], 1)

    xbc_w = channels(proj[inner:2 * inner + 2 * gn])
    arrays["w_mamba"] = np.concatenate([
        by_out(xbc_w.reshape(-1, D)).reshape(MG, CT, P, D),
        proj[:inner].reshape(MG, GI, KT, P).transpose(0, 2, 3, 1),
        a["L1_attn_out_proj_w"].T.reshape(MG, XT, P, D)], 1)
    arrays["w_dt"] = proj[-MH:].T.reshape(KT, P, MH).transpose(1, 0, 2)
    taps = np.concatenate([channels(a["L1_attn_conv_weight"]), channels(a["L1_attn_conv_bias"][:, None])], 3)
    arrays["conv_par"] = np.concatenate([taps.transpose(0, 2, 1, 3).reshape(MG, P, CT * (MK + 1)),
                                         a["L1_attn_norm_weight"].reshape(MG, XT, P).transpose(0, 2, 1)], 2)
    arrays["dt_bias"] = everywhere(a["L1_attn_dt_bias"])
    arrays["a_log"] = everywhere(a["L1_attn_A_log"])
    arrays["d_skip"] = everywhere(a["L1_attn_D"])

    nc = bacc.Bacc("TRN2", target_bir_lowering=False, num_devices=1)
    feed, args = {}, {}
    for name, v in arrays.items():
        v = np.ascontiguousarray(v)
        feed[f"in_{name}"] = v
        args[name] = nc.dram_tensor(f"in_{name}", v.shape, mybir.dt.from_np(v.dtype), kind="ExternalInput").ap()
    args["out"] = nc.dram_tensor("out_y", (B, L, D), F32, kind="ExternalOutput").ap()
    build(nc, **args)
    r = run(nc, [feed], core_ids=[0])
    return r.results[0]["out_y"]
```

```python
from contextlib import ExitStack

import concourse.bass as bass
from concourse import mybir

ALU = mybir.AluOpType
ACT = mybir.ActivationFunctionType
AX = mybir.AxisListType
F32 = mybir.dt.float32
F32R = mybir.dt.float32r
BF16 = mybir.dt.bfloat16

B, L, D = 2, 1024, 512
P = 128
TT = L // P
KT = D // P
HALF = 512
EPS = 1e-5
NEG = -1e30

AH, HD = 32, 16
QUAD = 4
NQ = AH // QUAD
VW = HD + 1
ROWS = 3 * HD

NF0 = 1792 // P
NF1 = (1376 + P - 1) // P
RANK = 4

MH, MP, MN, MG, MK = 64, 64, 128, 8, 4
HPG = MH // MG
GI = HPG * MP
XT = GI // P
CT = XT + 2
UNITS = 2 * MG
CPH = HALF // P
PROJ_AT = [(0, 1), (2,), (3, 4), (5,)]
SPLIT_AT = {1: (0, 1), 2: (2,), 3: (3, 4), 4: (5,)}
W_PER_G = CT + KT + XT
PROJ_PER_B = 2 * CT * MG

START = 1
ATT, PROJ, FFN0, STEPS_DT, MAMBA, FFN1, PHASES = range(7)
POST, PRE = range(2)


def build(nc, x, w_attn, qk_bias, bv, bo, w_ffn0, lr0, lr0_const, w_ffn1,
          w_mamba, w_dt, conv_par, dt_bias, a_log, d_skip, out):
    ctx = ExitStack()
    with ctx:
        def sb(name, shape, dt=F32, stack=ctx):
            return stack.enter_context(nc.sbuf_tensor(name, shape, dt))

        def sem(name):
            return ctx.enter_context(nc.semaphore(name))

        banks = ctx.enter_context(nc.psum_tensor("banks", [P, 8, HALF], F32))
        bank = [banks[:, i, :] for i in range(8)]

        X = sb("X", [P, TT, D])
        Y = sb("Y", [P, TT, D])
        xhi = sb("xhi", [P, KT, L], F32R)
        xlo = sb("xlo", [P, KT, L], F32R)
        ones = sb("ones", [P, P])
        ident = sb("ident", [P, P])
        ident_b = sb("ident_b", [P, P], BF16)
        mask_qk = sb("mask_qk", [P, P], BF16)
        upto = sb("upto", [P, P])
        after = sb("after", [P, P])
        after_r = sb("after_r", [P, P], F32R)
        quarter = sb("quarter", [P, P])
        zeros = sb("zeros", [P, MK])
        half_neg = sb("half_neg", [P, TT])
        stats = sb("stats", [P, 2, TT, 6])
        mv = sb("mv", [P, 2, TT, 2])
        var_eps = sb("var_eps", [P, 2, TT])
        neg_mean = sb("neg_mean", [P, 2, TT])
        rstd = sb("rstd", [P, 2, TT])
        shift = sb("shift", [P, 2, TT])

        with ExitStack() as s:
            xn = sb("xn", [P, 2, D], stack=s)
        with ExitStack() as s:
            V = sb("V", [P, TT, AH, VW], stack=s)
            with ExitStack() as s2:
                stack_q = [sb("stack_q0", [P, QUAD, L], F32R, stack=s2)]
                stack_k = [sb("stack_k0", [P, QUAD, L], F32R, stack=s2)]
                part_hi = sb("part_hi", [P, 2, L], F32R, stack=s2)
                part_lo = sb("part_lo", [P, 2, L], F32R, stack=s2)
                wqk_raw = sb("wqk_raw", [P, 2, D], stack=s2)
                wqk_hi = sb("wqk_hi", [P, 2, D], F32R, stack=s2)
                wqk_lo = sb("wqk_lo", [P, 2, D], F32R, stack=s2)
                qk_b = sb("qk_b", [P, 2], stack=s2)
                probs = [sb(f"probs{i}", [P, QUAD, HALF], stack=s2) for i in range(2)]
                ot = sb("ot", [P, HALF], stack=s2)
                mx = sb("mx", [P, 2, QUAD * TT], stack=s2)
                mt_hi = sb("mt_hi", [QUAD * TT, P], F32R, stack=s2)
                mt_lo = sb("mt_lo", [QUAD * TT, P], F32R, stack=s2)
                rsum = sb("rsum", [P, CPH, QUAD], stack=s2)
                with ExitStack() as s3:
                    wv_raw = sb("wv_raw", [P, KT, D], stack=s3)
                    wv_hi = sb("wv_hi", [P, KT, D], F32R, stack=s3)
                    wv_lo = sb("wv_lo", [P, KT, D], F32R, stack=s3)
                    bv_sb = sb("bv_sb", [P, D], stack=s3)
                with ExitStack() as s3:
                    stack_q.append(sb("stack_q1", [P, QUAD, L], F32R, stack=s3))
                    stack_k.append(sb("stack_k1", [P, QUAD, L], F32R, stack=s3))
        with ExitStack() as s:
            sb("under_values", [P, TT, AH, VW], stack=s)
            wo_raw = sb("wo_raw", [P, KT, D], stack=s)
            wo_hi = sb("wo_hi", [P, KT, D], F32R, stack=s)
            wo_lo = sb("wo_lo", [P, KT, D], F32R, stack=s)
            bo_sb = sb("bo_sb", [P, D], stack=s)
        with ExitStack() as s:
            sb("under_xn_2", [P, 2, D], stack=s)
            f_raw = [sb(f"f_raw{i}", [P, 3, D], stack=s) for i in range(2)]
            f_hi = [sb(f"f_hi{i}", [P, 3, D], F32R, stack=s) for i in range(2)]
            f_lo = [sb(f"f_lo{i}", [P, 3, D], F32R, stack=s) for i in range(2)]
            f_lr = [sb(f"f_lr{i}", [RANK, 3 * P], stack=s) for i in range(2)]
            f_lrc = sb("f_lrc", [RANK, 3 * D], stack=s)
            sg = sb("sg", [P, 2, HALF], stack=s)
            hf = sb("hf", [P, 2, HALF], stack=s)
            h_hi = [sb(f"h_hi{i}", [P, L], F32R, stack=s) for i in range(2)]
            h_lo = [sb(f"h_lo{i}", [P, L], F32R, stack=s) for i in range(2)]
        with ExitStack() as s:
            EC, WE, ED, DTH, AHI, ALO = range(6)
            tab = sb("tab", [P, 6, TT, MH], stack=s)
            d_half = sb("d_half", [P, MH], stack=s)
            with ExitStack() as s2:
                m_raw = sb("m_raw", [P, 2, D], stack=s2)
                wx_hi = sb("wx_hi", [P, CT, D], F32R, stack=s2)
                wx_lo = sb("wx_lo", [P, CT, D], F32R, stack=s2)
                wg_hi = sb("wg_hi", [P, KT, D], F32R, stack=s2)
                wg_lo = sb("wg_lo", [P, KT, D], F32R, stack=s2)
                wy_hi = sb("wy_hi", [P, XT, D], F32R, stack=s2)
                wy_lo = sb("wy_lo", [P, XT, D], F32R, stack=s2)
                cpar = sb("cpar", [P, CT * (MK + 1) + XT], stack=s2)
                gt = sb("gt", [P, 6, TT, HPG], stack=s2)
                gd = sb("gd", [P, 2, HPG], stack=s2)
                xbc = [sb(f"xbc{i}", [P, CT, HALF], stack=s2) for i in range(2)]
                pre = [sb(f"pre{i}", [P, MK - 1 + HALF], stack=s2) for i in range(2)]
                carry = sb("carry", [P, CT, MK - 1], stack=s2)
                conv = [sb(f"conv{i}", [P, HALF], stack=s2) for i in range(2)]
                with ExitStack() as s3:
                    wdt_raw = sb("wdt_raw", [P, KT, MH], stack=s3)
                    wdt_hi = sb("wdt_hi", [P, KT, MH], F32R, stack=s3)
                    wdt_lo = sb("wdt_lo", [P, KT, MH], F32R, stack=s3)
                    dtb = sb("dtb", [P, MH], stack=s3)
                    alog = sb("alog", [P, MH], stack=s3)
                    neg_a = sb("neg_a", [P, MH], stack=s3)
                    dsk = sb("dsk", [P, MH], stack=s3)
                    dt_turned = sb("dt_turned", [MH, L], stack=s3)
                    dt_in = sb("dt_in", [P, TT, MH], stack=s3)
                    dt_abs = sb("dt_abs", [P, TT, MH], stack=s3)
                    dt_sp = sb("dt_sp", [P, TT, MH], stack=s3)
                    a_all = sb("a_all", [P, TT, MH], stack=s3)
                    a_r = sb("a_r", [P, TT, MH], F32R, stack=s3)
                x_tm = sb("x_tm", [P, GI], stack=s2)
                b_tm = sb("b_tm", [P, MN], stack=s2)
                cb = sb("cb", [P, P], stack=s2)
                au_hi = sb("au_hi", [P, HPG, P], F32R, stack=s2)
                au_lo = sb("au_lo", [P, HPG, P], F32R, stack=s2)
                decay = sb("decay", [P, HPG, P], stack=s2)
                xdt = sb("xdt", [P, GI], stack=s2)
                xw = sb("xw", [P, GI], stack=s2)
                xd = sb("xd", [P, GI], stack=s2)
                state = sb("state", [P, GI], stack=s2)
                g_th = sb("g_th", [P, GI], stack=s2)
                yv = sb("yv", [P, GI], stack=s2)
                ss = sb("ss", [P, 1], stack=s2)
                rg = sb("rg", [P, 1], stack=s2)
                yn = sb("yn", [P, GI], stack=s2)
                yt_hi = sb("yt_hi", [P, XT, P], F32R, stack=s2)
                yt_lo = sb("yt_lo", [P, XT, P], F32R, stack=s2)

        consts_ready = sem("consts_ready")
        phase_end = sem("phase_end")
        held_waits = sem("held_waits")
        x_in = [sem("x_in0"), sem("x_in1")]
        out_done = [sem("out_done0"), sem("out_done1")]
        var_ready, rstd_ready = [sem("post_var"), sem("pre_var")], [sem("post_rstd"), sem("pre_rstd")]
        y_normed, x_added = sem("y_normed"), sem("x_added")
        xn_ready, xt_done, xt_hi, xt_free = (sem(n) for n in ("xn_ready", "xt_done", "xt_hi", "xt_free"))
        wv_in, wv_ready, v_used = sem("wv_in"), sem("wv_ready"), sem("v_used")
        wo_in, wo_ready, at_done, at_hi, at_free, o_done, o_free = (
            sem(n) for n in ("wo_in", "wo_ready", "at_done", "at_hi", "at_free", "o_done", "o_free"))
        wqk_in, wqk_ready, wqk_used = sem("wqk_in"), sem("wqk_ready"), sem("wqk_used")
        ring_done, ring_free = sem("ring_done"), sem("ring_free")
        part_hi_ready, part_lo_ready = sem("part_hi_ready"), sem("part_lo_ready")
        stacked = [sem("stacked0"), sem("stacked1")]
        ones_rows = sem("ones_rows")
        mx_ready = sem("mx_ready")
        mt_ready, mt_in = sem("mt_ready"), sem("mt_in")
        st_done = [sem("st_done0"), sem("st_done1")]
        exp_done = [sem("exp_done0"), sem("exp_done1")]
        masked = [sem("masked0"), sem("masked1")]
        pv_done, ot_ready, o_zero = sem("pv_done"), sem("ot_ready"), sem("o_zero")
        F = [{n: sem(f"{n}_{i}") for n in (
            "raw_in0", "raw_in1", "lr_const", "lr_done", "weff", "w_ready", "g_done", "u_done", "sg_done",
            "hf_done", "hi_done", "h_ready", "dn_done", "dn_used", "y_zero")}
            for i in range(2)]
        dt_turned_mm, dt_turned_ready = sem("dt_turned_mm"), sem("dt_turned_ready")
        dt_w_in, dt_w_ready, dt_mm, dt_sum, dt_soft, dt_a, dt_cs, dt_exp = (
            sem(n) for n in ("dt_w_in", "dt_w_ready", "dt_mm", "dt_sum", "dt_soft", "dt_a", "dt_cs", "dt_exp"))
        m_raw_in = [sem("m_raw_in0"), sem("m_raw_in1")]
        m_hi, m_split, cpar_in = sem("m_hi"), sem("m_split"), sem("cpar_in")
        gt_ready, m_zero = sem("gt_ready"), sem("m_zero")
        proj_done, gate_done = sem("proj_done"), sem("gate_done")
        pre_ready, conv_ready, cth_ready, xbc_ready = (
            sem(n) for n in ("pre_ready", "conv_ready", "cth_ready", "xbc_ready"))
        gate_th, gate_used = sem("gate_th"), sem("gate_used")
        xtr_done, x_tm_ready = sem("xtr_done"), sem("x_tm_ready")
        bc_done, bc_ready = sem("bc_done"), sem("bc_ready")
        au_ready, d_done, decay_ready, m_ready = (sem(n) for n in ("au_ready", "d_done", "decay_ready", "m_ready"))
        pool_x = sem("pool_x")
        inter_done, inter_used, intra_done, y_ready = (
            sem(n) for n in ("inter_done", "inter_used", "intra_done", "y_ready"))
        ss_ready, rg_ready, yn_ready = sem("ss_ready"), sem("rg_ready"), sem("yn_ready")
        yt_done, yt_hi_ready, yt_ready, mo_done, mo_used = (
            sem(n) for n in ("yt_done", "yt_hi_ready", "yt_ready", "mo_done", "mo_used"))
        st_mm, state_ready, state_dec = sem("st_mm"), sem("state_ready"), sem("state_dec")

        started = [*out_done, phase_end, *exp_done, ot_ready, mt_in, gate_used, gate_done, yn_ready, yt_ready, x_tm_ready,
                   bc_ready, d_done, decay_ready, pool_x, inter_done, inter_used, intra_done, y_ready, ss_ready,
                   mo_done, mo_used, st_mm]

        block = ctx.enter_context(nc.Block())

        def held(eng, semaphore, value):
            eng.wait_ge(semaphore, value)
            eng.sem_inc(held_waits, 1)

        def leave(eng, b, phase):
            eng.drain().then_inc(phase_end, 1)

        def enter(eng, b, phase):
            held(eng, phase_end, START + b * (5 * PHASES) + 5 * phase)

        STEPS = [(s, j) for s in range(2) for j in range(CPH * (s + 1))]
        PIECES = [(h, i, s, min((i + 1) * P - s * HALF, HALF), s == i // CPH)
                  for h in range(QUAD) for i in range(TT) for s in range(i // CPH + 1)]
        NS, NP = len(STEPS), len(PIECES)
        RING = 4 * (NQ // 2) + TT + NQ * (NP + 3)
        RING_BANKS = (4, 5, 7)
        STACKED = 16 * 6 * QUAD
        AHEAD = 6

        def attention_order():
            for use in range(4):
                yield "proj", 0, use
            for i in range(5):
                yield "values_in", i
            for n in range(NP):
                if n in (3, 9, 15):
                    yield "values_in", 5 + (n - 3) // 6
                if n in (21, 27, 33, 39):
                    yield "proj", 1, (n - 21) // 6
                yield "piece", 0, n
            yield "maxima", 0
            pieces = [(t, n) for t in range(1, NQ) for n in range(NP)]
            for _ in range(AHEAD):
                yield "piece", *pieces.pop(0)
            for t in range(NQ):
                for n in range(NS):
                    for q in range(4):
                        if q < 2:
                            yield "scores", t, n, q
                        elif n > 0:
                            yield "values", t, n - 1, q - 2
                        turning = n == NS - 2 and q < 2 and t + 1 < NQ
                        if n == NS - 2 and q == 1 and t + 1 < NQ:
                            yield "maxima", t + 1
                        for _ in range(0 if turning else 2 if n in (2, 3) and q == 0 else 1):
                            if pieces:
                                yield "piece", *pieces.pop(0)
                    if n == 1 and t > 0:
                        yield "turn", t - 1, 1
                    if n == 7:
                        yield "turn", t, 0
                    if t % 2 and n < 8 and n % 2 and (t + 3) // 2 < NQ // 2:
                        yield "proj", (t + 3) // 2, n // 2
                for q in range(2):
                    yield "values", t, NS - 1, q
            yield "turn", NQ - 1, 1

        ORDER = list(attention_order())

        def m_uses(last):
            uses = []
            for c in range(TT):
                s = c // CPH
                if not (last and s == 1):
                    uses += [("proj", s * CT + ft) for ft in PROJ_AT[c % CPH]]
                uses.append(("gate", c))
            return uses

        @block.sync
        def _(sp):
            sp.wait_ge(consts_ready, 1)
            with sp.Fori(0, B) as b:
                for h in range(2):
                    own = slice(h * CPH, (h + 1) * CPH)
                    held(sp, out_done[h], START + b * 16)
                    sp.dma_start(X[:, own, :], x[b].rearrange("(t p) d -> p t d", p=P)[:, own, :]
                                 ).then_inc(x_in[h], 16)
                enter(sp, b, ATT)

                def load_qk(f):
                    if f > 0:
                        held(sp, wqk_ready, b * 8 + 2 * f)
                        held(sp, part_lo_ready, b * 16 + 4 * f)
                    sp.dma_start(wqk_raw[:], w_attn[KT + 2 * f:KT + 2 * f + 2].rearrange("n p c -> p n c")
                                 ).then_inc(wqk_in, 16)
                    sp.dma_start(qk_b[:], qk_bias[f]).then_inc(wqk_in, 16)

                def stack(t):
                    f, par = t // 2, t % 2
                    held(sp, part_hi_ready, b * 16 + 4 * f + 4)
                    held(sp, part_lo_ready, b * 16 + 4 * f + 4)
                    if t >= 4:
                        held(sp, pv_done, b * (NQ * NS) + (t - 3) * NS)
                    for h in range(QUAD):
                        src = slice(HD * (QUAD * par + h), HD * (QUAD * par + h + 1))
                        for dst, which, parts in ((stack_q[f % 2], 0, (part_hi, part_hi, part_lo)),
                                                  (stack_k[f % 2], 1, (part_hi, part_lo, part_hi))):
                            for r, part in enumerate(parts):
                                at = 64 * par + HD * r
                                sp.dma_start(dst[at:at + HD, h, :].bitcast(F32),
                                             part[src, which, :].bitcast(F32)).then_inc(stacked[par], 16)

                def put_maxima(t):
                    held(sp, mt_ready, b * NQ + t + 1)
                    for r, part in ((0, mt_hi), (1, mt_lo)):
                        at = 64 * (t % 2) + ROWS + r
                        sp.dma_start(stack_q[t // 2 % 2][at:at + 1, :, :].bitcast(F32),
                                     part[:].bitcast(F32)).then_inc(mt_in, 16)

                def ones_in(buf):
                    for row in (ROWS, ROWS + 1, 64 + ROWS, 64 + ROWS + 1):
                        sp.dma_start(stack_k[buf][row:row + 1, :, :].bitcast(F32), ones[0:QUAD * TT, :]
                                     ).then_inc(ones_rows, 16)

                load_qk(0)
                sp.dma_start(wv_raw[:], w_attn[0:KT].rearrange("n p c -> p n c")).then_inc(wv_in, 16)
                sp.dma_start(bv_sb[:], bv).then_inc(wv_in, 16)
                ones_in(0)
                stack(0)
                stack(1)
                load_qk(1)
                held(sp, v_used, b + 1)
                ones_in(1)
                put_maxima(0)
                load_qk(2)
                stack(2)
                stack(3)
                put_maxima(1)
                put_maxima(2)
                load_qk(3)
                stack(4)
                stack(5)
                put_maxima(3)
                put_maxima(4)
                stack(6)
                stack(7)
                for t in range(5, NQ):
                    put_maxima(t)
                held(sp, pv_done, b * (NQ * NS) + (NQ - 2) * NS)
                sp.dma_start(wo_raw[:], w_attn[3 * KT:4 * KT].rearrange("n p c -> p n c")).then_inc(wo_in, 16)
                sp.dma_start(bo_sb[:], bo).then_inc(wo_in, 16)
                leave(sp, b, ATT)
                enter(sp, b, PROJ)
                leave(sp, b, PROJ)
                enter(sp, b, FFN0)

                def ffn_loads(i, w, n, lowrank):
                    f = F[i]

                    def load(p, par, first):
                        t = p * 2 + par
                        if not first:
                            held(sp, f["w_ready"], (b * n + t) * 3 - 3)
                        sp.dma_start(f_raw[par][:], w[t].rearrange("m p c -> p m c")).then_inc(f[f"raw_in{par}"], 16)
                        if lowrank:
                            sp.dma_start(f_lr[par][:], lr0[t]).then_inc(f[f"raw_in{par}"], 16)

                    load(0, 0, True)
                    load(0, 1, True)
                    with sp.Fori(1, n // 2) as p:
                        for par in range(2):
                            load(p, par, False)
                    if n % 2:
                        load(n // 2, 0, False)

                sp.dma_start(f_lrc[:], lr0_const).then_inc(F[0]["lr_const"], 16)
                ffn_loads(0, w_ffn0, NF0, True)
                leave(sp, b, FFN0)
                enter(sp, b, STEPS_DT)
                for dst, src in ((wdt_raw[:], w_dt), (dtb[:], dt_bias), (alog[:], a_log), (dsk[:], d_skip)):
                    sp.dma_start(dst, src).then_inc(dt_w_in, 16)
                leave(sp, b, STEPS_DT)

                def m_load(g, at, use, first=False):
                    if not first:
                        held(sp, m_split, b * (MG * W_PER_G) + use - 1)
                    sp.dma_start(m_raw[:, at % 2, :], w_mamba[g, at]).then_inc(m_raw_in[at % 2], 16)

                sp.dma_start(cpar[:], conv_par[0]).then_inc(cpar_in, 16)
                for n in range(CT):
                    m_load(0, n, n, n < 2)

                def m_group(g, last):
                    for n in range(CT, W_PER_G):
                        m_load(g, n, g * W_PER_G + n)
                    if not last:
                        for n in range(CT - 1):
                            m_load(g + 1, n, g * W_PER_G + (W_PER_G + n))
                        held(sp, conv_ready, b * PROJ_PER_B + g * (2 * CT) + 2 * CT)
                        held(sp, m_split, b * (MG * W_PER_G) + g * W_PER_G + W_PER_G)
                        sp.dma_start(cpar[:], conv_par[g + 1]).then_inc(cpar_in, 16)
                        m_load(g + 1, CT - 1, g * W_PER_G + (W_PER_G + CT - 1))

                with sp.Fori(0, MG - 1) as g:
                    m_group(g, False)
                m_group(MG - 1, True)
                leave(sp, b, MAMBA)
                enter(sp, b, FFN1)
                ffn_loads(1, w_ffn1, NF1, False)
                leave(sp, b, FFN1)
                for h in range(2):
                    own = slice(h * CPH, (h + 1) * CPH)
                    held(sp, x_added, (b * 4 + 3) * TT + (h + 1) * CPH)
                    sp.dma_start(out[b].rearrange("(t p) d -> p t d", p=P)[:, own, :], X[:, own, :]
                                 ).then_inc(out_done[h], 16)
            for h in range(2):
                sp.wait_ge(out_done[h], START + B * 16)

        @block.tensor
        def _(pe):
            pe.wait_ge(consts_ready, 1)

            def three(dst, a_hi, a_lo, w_hi, w_lo, kt, first, last):
                pe.matmul(dst, a_hi(kt), w_hi(kt), start=first, stop=False)
                pe.matmul(dst, a_lo(kt), w_hi(kt), start=False, stop=False)
                return pe.matmul(dst, a_hi(kt), w_lo(kt), start=False, stop=last)

            def tokens(dst, i, w_hi, w_lo, cols=None):
                tok = slice(i * P, (i + 1) * P)
                for kt in range(KT):
                    r = three(dst, lambda k: xhi[:, k, tok], lambda k: xlo[:, k, tok],
                              lambda k: w_hi[:, k, :], lambda k: w_lo[:, k, :], kt, kt == 0, kt == KT - 1)
                return r

            def features(dst, w_hi, w_lo, s):
                tok = slice(s * HALF, (s + 1) * HALF)
                for kt in range(KT):
                    r = three(dst, lambda k: w_hi[:, k * P:(k + 1) * P], lambda k: w_lo[:, k * P:(k + 1) * P],
                              lambda k: xhi[:, k, tok], lambda k: xlo[:, k, tok], kt, kt == 0, kt == KT - 1)
                return r

            def norm_turn(e):
                for i in range(TT):
                    pe.wait_ge(xn_ready, e * TT + i + 1)
                    if i >= 2:
                        pe.wait_ge(xt_free, e * TT + i - 1)
                    for k in range(KT):
                        r = pe.transpose(bank[i % 2][:, k * P:(k + 1) * P], xn[:, i % 2, k * P:(k + 1) * P],
                                         ident[:])
                    r.then_inc(xt_done, 1)
                pe.wait_ge(xt_free, e * TT + TT)

            def ffn(b, i, n, lowrank):
                f = F[i]

                def factor(p, par, m, first=False):
                    t = p * 2 + par
                    if m == 0:
                        pe.wait_ge(f[f"raw_in{par}"], (b * ((n + 1 - par) // 2) + p) * 32 + 32)
                    dst = bank[4 + (3 * par + m) % 2]
                    if not (first and m < 2):
                        pe.wait_ge(f["weff"], (b * n + t) * 3 + m - 1)
                    if m < 2:
                        for k in range(KT):
                            r = pe.matmul(dst[:, k * P:(k + 1) * P],
                                          f_lrc[:, m * D + k * P:m * D + (k + 1) * P],
                                          f_lr[par][:, m * P:(m + 1) * P], start=True, stop=True,
                                          skip_group_check=True)
                    else:
                        r = pe.matmul(dst[:], f_lr[par][:, 2 * P:3 * P], f_lrc[:, 2 * D:3 * D],
                                      start=True, stop=True)
                    r.then_inc(f["lr_done"], 1)

                def gate(t, par, s, first=False):
                    if s == 0:
                        pe.wait_ge(f["w_ready"], (b * n + t) * 3 + 1)
                    if not first:
                        pe.wait_ge(f["hf_done"], (b * n + t) * 2 + s - 1)
                    features(bank[2 * s][:], f_hi[par][:, 0, :], f_lo[par][:, 0, :], s).then_inc(f["g_done"], 1)

                def up(t, par, s):
                    if s == 0:
                        pe.wait_ge(f["w_ready"], (b * n + t) * 3 + 2)
                    features(bank[2 * s + 1][:], f_hi[par][:, 1, :], f_lo[par][:, 1, :], s).then_inc(f["u_done"], 1)

                def down(t, par, i, first=False):
                    if i == 0:
                        pe.wait_ge(f["w_ready"], (b * n + t) * 3 + 3)
                    if i % CPH == 0:
                        pe.wait_ge(f["h_ready"], (b * n + t) * 2 + (i // CPH + 1))
                    for i in (i, i + 1):
                        if not (first and i < 2):
                            pe.wait_ge(f["dn_used"], (b * n + t) * TT + i - 1)
                        tok = slice(i * P, (i + 1) * P)
                        three(bank[6 + i % 2][:], lambda k: h_hi[par][:, tok], lambda k: h_lo[par][:, tok],
                              lambda k: f_hi[par][:, 2, :], lambda k: f_lo[par][:, 2, :], 0, True, True
                              ).then_inc(f["dn_done"], 1)

                def step(p, par, more2, more1, first=False):
                    t = p * 2 + par
                    for q in range(4):
                        if more2 and lowrank and q < 3:
                            factor(p + 1, par, q)
                        if more1:
                            (gate if q % 2 == 0 else up)(t + 1, 1 - par, q // 2)
                        down(t, par, 2 * q, first)

                if lowrank:
                    pe.wait_ge(f["lr_const"], b * 16 + 16)
                    for par in range(2):
                        for m in range(3):
                            factor(0, par, m, par == 0)
                for s in range(2):
                    gate(0, 0, s, True)
                    up(0, 0, s)
                step(0, 0, True, True, True)
                step(0, 1, True, True)
                with pe.Fori(1, (n - 2) // 2) as p:
                    for par in range(2):
                        step(p, par, True, True)
                for t in range((n - 2) // 2 * 2, n):
                    step(t // 2, t % 2, t + 2 < n, t + 1 < n)

            with pe.Fori(0, B) as b:
                norm_turn(b * 4)
                enter(pe, b, ATT)
                pe.wait_ge(o_zero, b + 1)
                ring = 0
                for what, *arg in ORDER:
                    if what == "proj":
                        f, use = arg
                        which = use // 2
                        if use == 0:
                            pe.wait_ge(wqk_ready, b * 8 + 2 * f + 2)
                        if ring >= 3:
                            pe.wait_ge(ring_free, b * RING + ring - 2)
                        features(bank[RING_BANKS[ring % 3]][:], wqk_hi[:, which, :], wqk_lo[:, which, :], use % 2
                                 ).then_inc(ring_done, 1)
                        ring += 1
                    elif what == "values_in":
                        i, = arg
                        if i == 0:
                            pe.wait_ge(wv_ready, b + 1)
                        pe.wait_ge(ring_free, b * RING + ring - 2)
                        tokens(bank[RING_BANKS[ring % 3]][:], i, wv_hi, wv_lo).then_inc(ring_done, 1)
                        ring += 1
                    elif what == "piece":
                        t, n = arg
                        h, i, s, cols, diag = PIECES[n]
                        base, buf = 64 * (t % 2), t // 2 % 2
                        if n == 0:
                            pe.wait_ge(stacked[t % 2], (b * (NQ // 2) + t // 2 + 1) * STACKED)
                        pe.wait_ge(ring_free, b * RING + ring - 2)
                        dst = bank[RING_BANKS[ring % 3]]
                        r = pe.matmul(dst[:, 0:cols], stack_q[buf][base:base + ROWS, h, i * P:(i + 1) * P],
                                      stack_k[buf][base:base + ROWS, h, s * HALF:s * HALF + cols],
                                      start=True, stop=True)
                        if diag:
                            r = pe.matmul(dst[:, cols - P:cols], ident_b[:], mask_qk[:], start=False, stop=True,
                                          skip_group_check=True)
                        r.then_inc(ring_done, 1)
                        ring += 1
                    elif what == "maxima":
                        t, = arg
                        pe.wait_ge(mx_ready, b * NQ + t + 1)
                        pe.wait_ge(ring_free, b * RING + ring - 2)
                        pe.transpose(bank[RING_BANKS[ring % 3]][0:QUAD * TT, 0:P], mx[:, 0, :], ident[:]
                                     ).then_inc(ring_done, 1)
                        ring += 1
                    elif what == "scores":
                        t, n, p = arg
                        s, j = STEPS[n]
                        lo = max(j * P - s * HALF, 0)
                        base, buf = 64 * (t % 2), t // 2 % 2
                        it = b * (NQ * NS) + (t * NS + n)
                        if n == 0 and p == 0 and t % 2 == 0 and t < 4:
                            pe.wait_ge(ones_rows, b * (16 * 8) + 16 * 4 * (t // 2 + 1))
                        if n == 0 and p == 0:
                            pe.wait_ge(mt_in, START + (b * NQ + t + 1) * 32)
                        pe.wait_ge(exp_done[p], START + it)
                        for h in (2 * p, 2 * p + 1):
                            dst = bank[h]
                            r = pe.matmul(dst[:, 0:HALF - lo],
                                          stack_k[buf][base:base + ROWS + 2, h, j * P:(j + 1) * P],
                                          stack_q[buf][base:base + ROWS + 2, h, s * HALF + lo:(s + 1) * HALF],
                                          start=True, stop=True)
                        r.then_inc(st_done[p], 1)
                    elif what == "values":
                        t, n, p = arg
                        s, j = STEPS[n]
                        lo = max(j * P - s * HALF, 0)
                        it = b * (NQ * NS) + (t * NS + n)
                        if j == 0 and p == 0:
                            pe.wait_ge(ot_ready, START + b * (2 * NQ) + 2 * t + s)
                        if j * P >= s * HALF:
                            pe.wait_ge(masked[p], b * (NQ * TT) + (t * TT + j + 1))
                        else:
                            pe.wait_ge(exp_done[p], START + it + 1)
                        for h in (2 * p, 2 * p + 1):
                            r = pe.matmul(bank[6][32 * h:32 * h + VW, lo:HALF], V[:, j, QUAD * t + h, :],
                                          probs[n % 2][:, h, 0:HALF - lo], start=j == 0,
                                          stop=j == CPH * (s + 1) - 1, skip_group_check=True,
                                          tile_position=(0, 32 * h))
                        if p == 1:
                            r.then_inc(pv_done, 1)
                    elif what == "turn":
                        t, s = arg
                        pe.wait_ge(ot_ready, START + b * (2 * NQ) + 2 * t + s + 1)
                        pe.wait_ge(ring_free, b * RING + ring - 2)
                        for k in range(CPH):
                            r = pe.transpose(bank[RING_BANKS[ring % 3]][:, k * P:(k + 1) * P], ot[:, k * P:(k + 1) * P], ident[:])
                        r.then_inc(ring_done, 1)
                        ring += 1
                leave(pe, b, ATT)
                enter(pe, b, PROJ)
                for i in range(TT + 1):
                    if i < TT:
                        if i >= 2:
                            pe.wait_ge(at_free, b * TT + i - 1)
                        for k in range(KT):
                            r = pe.transpose(bank[2 + i % 2][:, k * P:(k + 1) * P], Y[:, i, k * P:(k + 1) * P],
                                             ident[:])
                        r.then_inc(at_done, 1)
                    if i > 0:
                        if i == 1:
                            pe.wait_ge(wo_ready, b + 1)
                        pe.wait_ge(at_free, b * TT + i)
                        if i >= 3:
                            pe.wait_ge(o_free, b * TT + i - 2)
                        tokens(bank[(i - 1) % 2][:], i - 1, wo_hi, wo_lo).then_inc(o_done, 1)
                leave(pe, b, PROJ)
                norm_turn(b * 4 + 1)
                enter(pe, b, FFN0)
                ffn(b, 0, NF0, True)
                leave(pe, b, FFN0)
                norm_turn(b * 4 + 2)
                enter(pe, b, STEPS_DT)
                pe.wait_ge(dt_w_ready, b + 1)
                for s in range(2):
                    tok = slice(s * HALF, (s + 1) * HALF)
                    for kt in range(KT):
                        r = three(bank[5 + s][0:MH, :], lambda k: wdt_hi[:, k, :], lambda k: wdt_lo[:, k, :],
                                  lambda k: xhi[:, k, tok], lambda k: xlo[:, k, tok], kt, kt == 0, kt == KT - 1)
                    r.then_inc(dt_turned_mm, 1)
                for i in range(TT):
                    if i % CPH == 0:
                        held(pe, dt_turned_ready, b * 2 + i // CPH + 1)
                    pe.transpose(bank[4][:, i * MH:(i + 1) * MH], dt_turned[:, i * P:(i + 1) * P],
                                 ident[0:MH, 0:MH]).then_inc(dt_mm, 1)

                def decay_sums():
                    pe.wait_ge(dt_a, b + 1)
                    for k, m in enumerate((upto, after, ones)):
                        pe.matmul(bank[5 + k][:], m[:], a_all[:].rearrange("p c h -> p (c h)"), start=True, stop=True
                                  ).then_inc(dt_cs, 1)

                def project(g, s, ft):
                    pe.wait_ge(m_split, b * (MG * W_PER_G) + g * W_PER_G + (ft + 1))
                    features(bank[ft % 2][:], wx_hi[:, ft, :], wx_lo[:, ft, :], s).then_inc(proj_done, 1)

                def bank_read(g, at, uses):
                    if at < 2:
                        pe.wait_ge(pre_ready, b * PROJ_PER_B + CT + g * (2 * CT))
                        pe.wait_ge(gate_used, START + (b * MG + g) * TT)
                        return
                    kind, n = uses[at - 2]
                    if kind == "proj":
                        pe.wait_ge(pre_ready, b * PROJ_PER_B + CT + g * (2 * CT) + (n + 1))
                    else:
                        pe.wait_ge(gate_used, START + (b * MG + g) * TT + (n + 1))

                def turn_out(it):
                    pe.wait_ge(yn_ready, START + it + 1)
                    for k in range(XT):
                        r = pe.transpose(bank[2][:, k * P:(k + 1) * P], yn[:, k * P:(k + 1) * P], ident[:])
                    r.then_inc(yt_done, 1)

                def project_out(it):
                    pe.wait_ge(yt_ready, START + it + 1)
                    for k in range(XT):
                        r = three(bank[3][:], lambda q: yt_hi[:, q, :], lambda q: yt_lo[:, q, :],
                                  lambda q: wy_hi[:, q, :], lambda q: wy_lo[:, q, :], k, k == 0, k == XT - 1)
                    r.then_inc(mo_done, 1)

                def decays(it):
                    pe.wait_ge(au_ready, it + 1)
                    pe.wait_ge(decay_ready, START + it)
                    for q in range(2):
                        h4 = slice(q * HPG // 2, (q + 1) * HPG // 2)
                        dst = bank[4 + q][:].rearrange("p (h l) -> p h l", l=P)
                        pe.matmul(dst, after_r[:], au_hi[:, h4, :], start=True, stop=False)
                        r = pe.matmul(dst, after_r[:], au_lo[:, h4, :], start=False, stop=True)
                    r.then_inc(d_done, 1)

                def m_group(g, first, last):
                    uses = m_uses(last)
                    at = 0
                    for c in range(TT):
                        it = (b * MG + g) * TT + c
                        s, ck = c // CPH, slice(c % CPH * P, (c % CPH + 1) * P)
                        start = first and c == 0
                        if c % CPH == 0:
                            pe.wait_ge(xbc_ready, b * PROJ_PER_B + g * (2 * CT) + (s * CT + CT))
                        pe.wait_ge(yt_ready, START + (it if start else it - 1))
                        pe.wait_ge(x_tm_ready, START + it)
                        for k in range(XT):
                            r = pe.transpose(bank[2][:, k * P:(k + 1) * P], xbc[s][:, k, ck], ident[:])
                        r.then_inc(xtr_done, 1)
                        pe.wait_ge(mo_used, START + (it if start else it - 1))
                        pe.wait_ge(bc_ready, START + it)
                        pe.transpose(bank[3][:, 0:P], xbc[s][:, XT, ck], ident[:])
                        pe.matmul(bank[3][:, P:2 * P], xbc[s][:, XT, ck], xbc[s][:, XT + 1, ck],
                                  start=True, stop=True, skip_group_check=True).then_inc(bc_done, 1)
                        if not start:
                            decays(it)
                        turned = start
                        while uses[at][0] == "proj":
                            n = uses[at][1]
                            bank_read(g, at, uses)
                            ft = n % CT
                            if n < CT:
                                features(bank[at % 2][:], wx_hi[:, ft, :], wx_lo[:, ft, :], 1).then_inc(proj_done, 1)
                            else:
                                pe.wait_ge(m_split, b * (MG * W_PER_G) + (g + 1) * W_PER_G + (ft + 1))
                                features(bank[at % 2][:], wx_hi[:, ft, :], wx_lo[:, ft, :], 0).then_inc(proj_done, 1)
                            at += 1
                            if not turned:
                                pe.wait_ge(x_tm_ready, START + it + 1)
                                turn_out(it - 1)
                                turned = True
                        if start:
                            decays(it)
                        if not turned:
                            pe.wait_ge(x_tm_ready, START + it + 1)
                            turn_out(it - 1)
                        bank_read(g, at, uses)
                        if c == 0:
                            pe.wait_ge(m_split, b * (MG * W_PER_G) + g * W_PER_G + (CT + KT))
                        tokens(bank[at % 2][:], c, wg_hi, wg_lo).then_inc(gate_done, 1)
                        at += 1
                        pe.wait_ge(state_ready, it + 1)
                        if c == 0:
                            pe.wait_ge(inter_used, START + it)
                        pe.matmul(bank[6][:], xbc[s][:, XT + 1, ck], state[:], start=True, stop=True
                                  ).then_inc(inter_done, 1)
                        pe.wait_ge(m_ready, it + 1)
                        pe.wait_ge(pool_x, START + it + 1)
                        pe.wait_ge(ss_ready, START + it)
                        for h in range(HPG):
                            r = pe.matmul(bank[7][:, h * MP:(h + 1) * MP], decay[:, h, :], xdt[:, h * MP:(h + 1) * MP],
                                          start=True, stop=True, skip_group_check=True)
                        r.then_inc(intra_done, 1)
                        if not start:
                            if c == 1:
                                pe.wait_ge(m_split, b * (MG * W_PER_G) + g * W_PER_G + W_PER_G)
                            pe.wait_ge(bc_ready, START + it + 1)
                            project_out(it - 1)
                        if c < TT - 1:
                            pe.wait_ge(inter_used, START + it + 1)
                            pe.matmul(bank[6][:], b_tm[:], xw[:], start=True, stop=True).then_inc(st_mm, 1)

                for ft in range(CT):
                    if ft >= 2:
                        pe.wait_ge(pre_ready, b * PROJ_PER_B + ft - 1)
                    project(0, 0, ft)
                    if ft == 1:
                        decay_sums()
                        leave(pe, b, STEPS_DT)
                pe.wait_ge(dt_exp, b * 3 + 3)
                enter(pe, b, MAMBA)
                m_group(0, True, False)
                with pe.Fori(1, MG - 1) as g:
                    m_group(g, False, False)
                m_group(MG - 1, False, True)
                turn_out((b + 1) * (MG * TT) - 1)
                project_out((b + 1) * (MG * TT) - 1)
                leave(pe, b, MAMBA)
                norm_turn(b * 4 + 3)
                enter(pe, b, FFN1)
                ffn(b, 1, NF1, False)
                leave(pe, b, FFN1)

        @block.scalar
        def _(act):
            act.wait_ge(consts_ready, 1)

            def turned(src):
                return src.rearrange("p (k t) -> p k t", t=P)

            def normed_y(e):
                for i in range(TT):
                    if i % CPH == 0:
                        act.wait_ge(rstd_ready[POST], e * 2 + i // CPH + 1)
                    act.activation(Y[:, i, :], Y[:, i, :], ACT.Identity, scale=rstd[:, POST, i:i + 1],
                                   bias=shift[:, POST, i:i + 1]).then_inc(y_normed, 1)

            def normed_x(e):
                for i in range(TT + 1):
                    if i < TT:
                        if i % CPH == 0:
                            act.wait_ge(rstd_ready[PRE], e * 2 + i // CPH + 1)
                        if i >= 2:
                            act.wait_ge(xt_done, e * TT + i - 1)
                        act.activation(xn[:, i % 2, :], X[:, i, :], ACT.Identity, scale=rstd[:, PRE, i:i + 1],
                                       bias=shift[:, PRE, i:i + 1]).then_inc(xn_ready, 1)
                    if i > 0:
                        act.wait_ge(xt_done, e * TT + i)
                        act.copy(xhi[:, :, (i - 1) * P:i * P], turned(bank[(i - 1) % 2])).then_inc(xt_hi, 1)

            def ffn(b, i, n):
                f = F[i]

                def hidden(p, par, first=False):
                    for s in range(2):
                        it = (b * n + p * 2 + par) * 2 + s
                        act.wait_ge(f["g_done"], it + 1)
                        act.activation(sg[:, s, :], bank[2 * s], ACT.Silu).then_inc(f["sg_done"], 1)
                        act.wait_ge(f["hf_done"], it + 1)
                        if not first:
                            act.wait_ge(f["dn_done"], (b * n + p * 2 + par) * TT - TT)
                        act.copy(h_hi[par][:, s * HALF:(s + 1) * HALF], hf[:, s, :]).then_inc(f["hi_done"], 1)

                hidden(0, 0, True)
                hidden(0, 1, True)
                with act.Fori(1, n // 2) as p:
                    for par in range(2):
                        hidden(p, par)
                if n % 2:
                    hidden(n // 2, 0)

            with act.Fori(0, B) as b:
                normed_x(b * 4)
                enter(act, b, ATT)
                ring = 0
                for what, *arg in ORDER:
                    if what == "proj":
                        f, use = arg
                        which, s = use // 2, use % 2
                        if use == 0:
                            act.wait_ge(wqk_in, (b * (NQ // 2) + f + 1) * 32)
                        if use == 0 and f > 0:
                            act.wait_ge(stacked[0], (b * (NQ // 2) + f) * STACKED)
                            act.wait_ge(stacked[1], (b * (NQ // 2) + f) * STACKED)
                        act.wait_ge(ring_done, b * RING + ring + 1)
                        act.activation(part_hi[:, which, s * HALF:(s + 1) * HALF], bank[RING_BANKS[ring % 3]],
                                       ACT.Identity, bias=qk_b[:, which:which + 1]).then_inc(part_hi_ready, 1)
                        ring += 1
                    elif what in ("piece", "values_in", "maxima", "turn"):
                        ring += 1
                    elif what == "scores":
                        t, n, p = arg
                        s, j = STEPS[n]
                        w = HALF - max(j * P - s * HALF, 0)
                        it = b * (NQ * NS) + (t * NS + n)
                        if p == 0 and (t > 0 or n >= 2):
                            act.wait_ge(pv_done, it - 1)
                        act.wait_ge(st_done[p], it + 1)
                        act.activation(probs[n % 2][:, 2 * p:2 * p + 2, 0:w], banks[:, 2 * p:2 * p + 2, 0:w],
                                       ACT.Exp, scale=1.0 / HD ** 0.5).then_inc(exp_done[p], 1)
                leave(act, b, ATT)
                enter(act, b, PROJ)
                for i in range(TT):
                    act.wait_ge(at_done, b * TT + i + 1)
                    act.copy(xhi[:, :, i * P:(i + 1) * P], turned(bank[2 + i % 2])).then_inc(at_hi, 1)
                leave(act, b, PROJ)
                normed_y(b * 4)
                normed_x(b * 4 + 1)
                enter(act, b, FFN0)
                ffn(b, 0, NF0)
                leave(act, b, FFN0)
                normed_y(b * 4 + 1)
                normed_x(b * 4 + 2)
                enter(act, b, STEPS_DT)
                def split_hi(dst, n, g):
                    act.wait_ge(m_raw_in[n % 2], (b * (MG * W_PER_G // 2) + g * (W_PER_G // 2) + n // 2) * 16 + 16)
                    raw = m_raw[:, n % 2, :]
                    if n >= CT + KT:
                        col = CT * (MK + 1) + (n - CT - KT)
                        act.activation(raw, raw, ACT.Copy, scale=cpar[:, col:col + 1])
                        act.drain()
                    act.copy(dst, raw).then_inc(m_hi, 1)

                held(act, cpar_in, (b * MG + 1) * 16)
                for n in range(2):
                    split_hi(wx_hi[:, n, :], n, 0)
                act.wait_ge(dt_w_in, (b + 1) * 64)
                act.activation(neg_a[:], alog[:], ACT.Exp)
                act.wait_ge(dt_sum, b + 1)
                act.activation(dt_abs[:], dt_in[:], ACT.Abs)
                act.drain()
                act.activation(dt_abs[:], dt_abs[:], ACT.Exp, scale=-1.0)
                act.drain()
                act.activation(dt_sp[:], dt_abs[:], ACT.Ln, bias=ones[:, 0:1]).then_inc(dt_soft, 1)
                for n in range(2, CT):
                    split_hi(wx_hi[:, n, :], n, 0)
                for k in (EC, WE, ED):
                    act.wait_ge(dt_cs, b * 3 + k + 1)
                    act.activation(tab[:, k, :, :].rearrange("p c h -> p (c h)"), bank[5 + k], ACT.Exp
                                   ).then_inc(dt_exp, 1)
                leave(act, b, STEPS_DT)

                def before_conv(src, pi, n, s, first=False):
                    ft, par = n % CT, n % 2
                    act.drain()
                    act.wait_ge(proj_done, pi + 1)
                    if not first:
                        act.wait_ge(xbc_ready, pi - 1)
                    act.copy(pre[par][:, 0:MK - 1], carry[:, ft, :] if s else zeros[:, 0:MK - 1])
                    act.copy(pre[par][:, MK - 1:], src)
                    if not s:
                        act.copy(carry[:, ft, :], src[:, HALF - MK + 1:HALF])
                    o = ft * (MK + 1)
                    act.activation(conv[par][:], src, ACT.Identity, scale=cpar[:, o + MK - 1:o + MK],
                                   bias=cpar[:, o + MK:o + MK + 1]).then_inc(pre_ready, 1)

                def conv_tanh(pi, n, s):
                    act.wait_ge(conv_ready, pi + 1)
                    act.activation(xbc[s][:, n % CT, :], conv[n % 2][:], ACT.Tanh, scale=0.5).then_inc(cth_ready, 1)

                def turned_hi(it):
                    act.wait_ge(yt_done, it + 1)
                    act.wait_ge(mo_done, START + it)
                    act.copy(yt_hi[:], turned(bank[2])).then_inc(yt_hi_ready, 1)

                def decay_exp(it):
                    act.wait_ge(d_done, START + it + 1)
                    act.wait_ge(intra_done, START + it)
                    act.activation(decay[:].rearrange("p (a h) l -> p a (h l)", a=2), banks[:, 4:6, :], ACT.Exp
                                   ).then_inc(decay_ready, 1)

                def m_group(g, first, last):
                    uses = m_uses(last)
                    at = 0
                    p0 = b * PROJ_PER_B + g * (2 * CT) + CT

                    def more_splits(c):
                        if c == 0:
                            for k in range(2, KT):
                                split_hi(wg_hi[:, k, :], CT + k, g)
                        if c == 1:
                            for k in range(2, XT):
                                split_hi(wy_hi[:, k, :], CT + KT + k, g)

                    for c in range(TT):
                        it = (b * MG + g) * TT + c
                        start = first and c == 0
                        act.wait_ge(xtr_done, it + 1)
                        act.wait_ge(pool_x, START + it)
                        act.copy(x_tm[:], bank[2]).then_inc(x_tm_ready, 1)
                        if not start:
                            decay_exp(it)
                        is_turned = start
                        while uses[at][0] == "proj":
                            n = uses[at][1]
                            if n == CT:
                                held(act, cpar_in, (b * MG + g + 2) * 16)
                            s1 = 1 if n < CT else 0
                            before_conv(bank[at % 2], p0 + n, n, s1)
                            if not is_turned:
                                turned_hi(it - 1)
                                is_turned = True
                                more_splits(c)
                            if n % CT:
                                conv_tanh(p0 + (n - 1), n - 1, s1)
                            if n % CT == CT - 1:
                                conv_tanh(p0 + n, n, s1)
                            at += 1
                        if start:
                            decay_exp(it)
                        if not is_turned:
                            turned_hi(it - 1)
                            more_splits(c)
                        act.wait_ge(gate_done, START + it + 1)
                        act.wait_ge(yn_ready, START + it)
                        act.activation(g_th[:], bank[at % 2], ACT.Tanh, scale=0.5).then_inc(gate_th, 1)
                        at += 1
                        act.wait_ge(y_ready, START + it + 1)
                        act.activation(bank[7], yv[:], ACT.Square, accum_out=ss[:]).then_inc(ss_ready, 1)
                        if c == 0:
                            act.wait_ge(mo_done, START + it)
                            for k in range(2):
                                split_hi(wy_hi[:, k, :], CT + KT + k, g)
                        if not last:
                            if c == TT - 1:
                                for k in range(2):
                                    split_hi(wg_hi[:, k, :], CT + k, g + 1)
                            for ft in SPLIT_AT.get(c, ()):
                                act.wait_ge(proj_done, b * PROJ_PER_B + g * (2 * CT) + (CT + ft + 1))
                                split_hi(wx_hi[:, ft, :], ft, g + 1)

                for n in range(CT):
                    pi = b * PROJ_PER_B + n
                    before_conv(bank[n % 2], pi, n, 0, n < 2)
                    if n:
                        conv_tanh(pi - 1, n - 1, 0)
                conv_tanh(b * PROJ_PER_B + (CT - 1), CT - 1, 0)
                for k in range(KT):
                    split_hi(wg_hi[:, k, :], CT + k, 0)
                enter(act, b, MAMBA)
                m_group(0, True, False)
                with act.Fori(1, MG - 1) as g:
                    m_group(g, False, False)
                m_group(MG - 1, False, True)
                turned_hi((b + 1) * (MG * TT) - 1)
                leave(act, b, MAMBA)
                normed_y(b * 4 + 2)
                normed_x(b * 4 + 3)
                enter(act, b, FFN1)
                ffn(b, 1, NF1)
                leave(act, b, FFN1)
                normed_y(b * 4 + 3)

        @block.vector
        def _(dve):
            dve.wait_ge(consts_ready, 1)

            def moments(kind, src, e, b=None):
                dve.drain()
                for h in range(2):
                    tiles = range(h * CPH, (h + 1) * CPH)
                    own = slice(h * CPH, (h + 1) * CPH)
                    for i in tiles:
                        if kind == PRE and e is not None:
                            dve.wait_ge(x_added, e * TT + i + 1)
                        if kind == PRE and e is None and i % CPH == 0:
                            dve.wait_ge(x_in[h], b * 16 + 16)
                        dve.bn_stats(stats[:, kind, i, :], src[:, i, :])
                    dve.drain()
                    for i in tiles:
                        dve.bn_aggr(mv[:, kind, i, :], stats[:, kind, i, :])
                    dve.drain()
                    dve.tensor_scalar(neg_mean[:, kind, own], mv[:, kind, own, 0], -1.0, None, ALU.mult)
                    dve.tensor_scalar(var_eps[:, kind, own], mv[:, kind, own, 1], EPS, None, ALU.add)
                    dve.drain().then_inc(var_ready[kind], 1)

            def norm_lo(e):
                for i in range(TT):
                    dve.wait_ge(xt_hi, e * TT + i + 1)
                    dve.tensor_tensor(xlo[:, :, i * P:(i + 1) * P], bank[i % 2].rearrange("p (k t) -> p k t", t=P),
                                      xhi[:, :, i * P:(i + 1) * P].bitcast(F32), ALU.subtract).then_inc(xt_free, 1)

            def ffn(b, i, n, lowrank):
                f = F[i]

                def scale(p, par, m):
                    it = (b * n + p * 2 + par) * 3 + m
                    dve.wait_ge(f["lr_done"], it + 1)
                    dve.tensor_tensor(f_raw[par][:, m, :], f_raw[par][:, m, :], bank[4 + (3 * par + m) % 2],
                                      ALU.mult).then_inc(f["weff"], 1)

                def hidden(t, par, s):
                    it = (b * n + t) * 2 + s
                    dve.drain()
                    dve.wait_ge(f["sg_done"], it + 1)
                    dve.wait_ge(f["u_done"], it + 1)
                    dve.tensor_tensor(hf[:, s, :], sg[:, s, :], bank[2 * s + 1], ALU.mult).then_inc(f["hf_done"], 1)

                def hidden_lo(t, par, s):
                    dve.wait_ge(f["hi_done"], (b * n + t) * 2 + s + 1)
                    cols = slice(s * HALF, (s + 1) * HALF)
                    dve.tensor_tensor(h_lo[par][:, cols], hf[:, s, :], h_hi[par][:, cols].bitcast(F32),
                                      ALU.subtract).then_inc(f["h_ready"], 1)

                def gather(t, i):
                    for i in (i, i + 1):
                        dve.wait_ge(f["dn_done"], (b * n + t) * TT + (i + 1))
                        dve.tensor_tensor(Y[:, i, :], bank[6 + i % 2], Y[:, i, :], ALU.add).then_inc(f["dn_used"], 1)

                def step(p, par, more2, more1):
                    t = p * 2 + par
                    for q in range(4):
                        if more2 and lowrank and q < 3:
                            scale(p + 1, par, q)
                        if more1 and q % 2:
                            hidden(t + 1, 1 - par, q // 2)
                        gather(t, 2 * q)
                        if more1 and q % 2:
                            hidden_lo(t + 1, 1 - par, q // 2)

                if lowrank:
                    for par in range(2):
                        for m in range(3):
                            scale(0, par, m)
                for s in range(2):
                    hidden(0, 0, s)
                    dve.drain()
                    hidden_lo(0, 0, s)
                held(dve, f["y_zero"], b + 1)
                with dve.Fori(0, (n - 2) // 2) as p:
                    for par in range(2):
                        step(p, par, True, True)
                for t in range((n - 2) // 2 * 2, n):
                    step(t // 2, t % 2, t + 2 < n, t + 1 < n)

            with dve.Fori(0, B) as b:
                moments(PRE, X, None, b)
                norm_lo(b * 4)
                enter(dve, b, ATT)
                dve.memset(bank[6], 0.0).then_inc(o_zero, 1)
                dve.memset(V[:, :, :, HD:VW], 1.0)
                ring = 0
                for what, *arg in ORDER:
                    if what == "proj":
                        f, use = arg
                        which, cols = use // 2, slice(use % 2 * HALF, (use % 2 + 1) * HALF)
                        dve.wait_ge(part_hi_ready, b * 16 + 4 * f + use + 1)
                        dve.scalar_tensor_tensor(out=part_lo[:, which, cols], in0=bank[RING_BANKS[ring % 3]],
                                                 scalar=qk_b[:, which:which + 1],
                                                 in1=part_hi[:, which, cols].bitcast(F32),
                                                 op0=ALU.add, op1=ALU.subtract).then_inc(part_lo_ready, 1)
                        dve.drain().then_inc(ring_free, 1)
                        ring += 1
                    elif what == "values_in":
                        i, = arg
                        if i == 0:
                            dve.wait_ge(wv_in, b * 32 + 32)
                        dve.wait_ge(ring_done, b * RING + ring + 1)
                        dve.tensor_tensor(V[:, i, :, 0:HD], bank[RING_BANKS[ring % 3]].rearrange("p (h d) -> p h d", d=HD),
                                          bv_sb[:].rearrange("p (h d) -> p h d", d=HD), ALU.add
                                          ).then_inc(ring_free, 1)
                        if i == TT - 1:
                            dve.drain().then_inc(v_used, 1)
                        ring += 1
                    elif what == "piece":
                        t, n = arg
                        h, i, s, cols, _ = PIECES[n]
                        dve.wait_ge(ring_done, b * RING + ring + 1)
                        dve.tensor_reduce(mx[:, s, h * TT + i:h * TT + i + 1], bank[RING_BANKS[ring % 3]][:, 0:cols],
                                          AX.X, ALU.max).then_inc(ring_free, 1)
                        ring += 1
                    elif what == "maxima":
                        t, = arg
                        dve.drain()
                        m0, m1 = (mx[:, q, :].rearrange("p (h i) -> p h i", i=TT)[:, :, CPH:TT] for q in range(2))
                        dve.tensor_tensor(m0, m0, m1, ALU.max).then_inc(mx_ready, 1)
                        dve.wait_ge(ring_done, b * RING + ring + 1)
                        dve.wait_ge(mt_in, START + (b * NQ + t) * 32)
                        src = bank[RING_BANKS[ring % 3]][0:QUAD * TT, 0:P]
                        dve.tensor_scalar(mt_hi[:], src, -1.0, None, ALU.mult)
                        dve.drain()
                        dve.scalar_tensor_tensor(out=mt_lo[:], in0=src, scalar=-1.0, in1=mt_hi[:].bitcast(F32),
                                                 op0=ALU.mult, op1=ALU.subtract
                                                 ).then_inc(mt_ready, 1)
                        dve.drain().then_inc(ring_free, 1)
                        ring += 1
                    elif what == "values":
                        t, n, p = arg
                        s, j = STEPS[n]
                        if p == 1 and j == CPH * (s + 1) - 1:
                            dve.wait_ge(pv_done, b * (NQ * NS) + (t * NS + n) + 1)
                            dve.tensor_copy(ot[:], bank[6]).then_inc(ot_ready, 1)
                    elif what == "turn":
                        t, s = arg
                        dve.wait_ge(ring_done, b * RING + ring + 1)
                        o = bank[RING_BANKS[ring % 3]].rearrange("p (k h r) -> p k h r", k=CPH, h=QUAD)
                        dve.reciprocal(rsum[:], o[:, :, :, HD])
                        dve.drain()
                        cols = slice(t * QUAD * HD, (t + 1) * QUAD * HD)
                        dst = Y[:, s * CPH:(s + 1) * CPH, cols].rearrange("p k (h d) -> p k h d", d=HD)
                        dve.tensor_tensor(dst, o[:, :, :, 0:HD],
                                          rsum[:].unsqueeze(3).broadcast_to([P, CPH, QUAD, HD]), ALU.mult
                                          ).then_inc(ring_free, 1)
                        ring += 1
                leave(dve, b, ATT)
                enter(dve, b, PROJ)
                dve.wait_ge(wo_in, b * 32 + 32)
                for i in range(TT + 1):
                    if i < TT:
                        dve.wait_ge(at_hi, b * TT + i + 1)
                        tok = slice(i * P, (i + 1) * P)
                        dve.tensor_tensor(xlo[:, :, tok], bank[2 + i % 2].rearrange("p (k t) -> p k t", t=P),
                                          xhi[:, :, tok].bitcast(F32), ALU.subtract).then_inc(at_free, 1)
                    if i > 0:
                        dve.wait_ge(o_done, b * TT + i)
                        dve.tensor_tensor(Y[:, i - 1, :], bank[(i - 1) % 2], bo_sb[:], ALU.add).then_inc(o_free, 1)
                leave(dve, b, PROJ)
                moments(POST, Y, b * 4)
                moments(PRE, X, b * 4)
                norm_lo(b * 4 + 1)
                enter(dve, b, FFN0)
                ffn(b, 0, NF0, True)
                leave(dve, b, FFN0)
                moments(POST, Y, b * 4 + 1)
                moments(PRE, X, b * 4 + 1)
                norm_lo(b * 4 + 2)
                enter(dve, b, STEPS_DT)
                def by_token(par_tile):
                    return par_tile[:].unsqueeze(1).broadcast_to([P, TT, MH])

                dve.wait_ge(dt_w_in, (b + 1) * 64)
                dve.tensor_scalar(d_half[:], dsk[:], 0.5, None, ALU.mult)
                for s in range(2):
                    dve.wait_ge(dt_turned_mm, b * 2 + s + 1)
                    dve.tensor_copy(dt_turned[:, s * HALF:(s + 1) * HALF], bank[5 + s][0:MH, :]
                                    ).then_inc(dt_turned_ready, 1)
                dve.wait_ge(dt_mm, (b + 1) * TT)
                dve.tensor_tensor(dt_in[:], bank[4].rearrange("p (c h) -> p c h", h=MH), by_token(dtb), ALU.add
                                  ).then_inc(dt_sum, 1)
                dve.wait_ge(dt_soft, b + 1)
                dve.scalar_tensor_tensor(out=dt_sp[:], in0=dt_in[:], scalar=0.0, in1=dt_sp[:],
                                         op0=ALU.max, op1=ALU.add)
                dve.tensor_scalar(neg_a[:], neg_a[:], -1.0, None, ALU.mult)
                dve.drain()
                dve.tensor_tensor(a_all[:], dt_sp[:], by_token(neg_a), ALU.mult).then_inc(dt_a, 1)
                dve.tensor_scalar(tab[:, DTH, :, :], dt_sp[:], 0.5, None, ALU.mult)
                dve.drain()
                dve.tensor_copy(a_r[:], a_all[:])
                dve.drain()
                dve.tensor_copy(tab[:, AHI, :, :], a_r[:].bitcast(F32))
                dve.tensor_tensor(tab[:, ALO, :, :], a_all[:], a_r[:].bitcast(F32), ALU.subtract)
                dve.wait_ge(dt_exp, b * 3 + 3)
                dve.tensor_scalar(tab[:, EC, :, :], tab[:, EC, :, :], 0.5, None, ALU.mult)
                dve.scalar_tensor_tensor(out=tab[:, WE, :, :], in0=tab[:, WE, :, :], scalar=0.25, in1=dt_sp[:],
                                         op0=ALU.mult, op1=ALU.mult)
                leave(dve, b, STEPS_DT)

                def convolve(pi, n):
                    ft, par = n % CT, n % 2
                    dve.wait_ge(pre_ready, pi + 1)
                    for k in range(MK - 1):
                        o = ft * (MK + 1) + k
                        r = dve.scalar_tensor_tensor(out=conv[par][:], in0=pre[par][:, k:k + HALF],
                                                     scalar=cpar[:, o:o + 1], in1=conv[par][:],
                                                     op0=ALU.mult, op1=ALU.add)
                        if k < MK - 2:
                            dve.drain()
                    r.then_inc(conv_ready, 1)

                def twice_silu(pi, n, s):
                    dve.wait_ge(cth_ready, pi + 1)
                    dve.scalar_tensor_tensor(out=xbc[s][:, n % CT, :], in0=xbc[s][:, n % CT, :], scalar=1.0,
                                             in1=conv[n % 2][:], op0=ALU.add, op1=ALU.mult).then_inc(xbc_ready, 1)

                def masked(it, sm):
                    dve.wait_ge(bc_done, it + 1)
                    dve.wait_ge(st_mm, START + sm)
                    dve.tensor_copy(b_tm[:], bank[3][:, 0:P])
                    dve.tensor_tensor(cb[:], bank[3][:, P:2 * P], quarter[:], ALU.mult).then_inc(bc_ready, 1)
                    dve.drain()
                    dve.wait_ge(decay_ready, START + it + 1)
                    dve.tensor_tensor(decay[:], decay[:], cb[:].unsqueeze(1).broadcast_to([P, HPG, P]), ALU.mult
                                      ).then_inc(m_ready, 1)

                def turned_lo(it):
                    dve.wait_ge(yt_hi_ready, it + 1)
                    dve.tensor_tensor(yt_lo[:], bank[2].rearrange("p (k t) -> p k t", t=P), yt_hi[:].bitcast(F32),
                                      ALU.subtract).then_inc(yt_ready, 1)

                def gather(it, c):
                    dve.wait_ge(mo_done, START + it + 1)
                    dve.tensor_tensor(Y[:, c, :], bank[3], Y[:, c, :], ALU.add).then_inc(mo_used, 1)

                def by_head(t):
                    return t.rearrange("p (h d) -> p h d", d=MP)

                def tables(g, s):
                    heads = bass.ds(g * HPG, HPG)
                    for kind in range(6):
                        dve.tensor_copy(gt[:, kind, s * CPH:(s + 1) * CPH, :],
                                        tab[:, kind, s * CPH:(s + 1) * CPH, heads])
                    dve.tensor_copy(gd[:, s, :], d_half[:, heads]).then_inc(gt_ready, 1)

                def m_group(g, first, last):
                    uses = m_uses(last)
                    at = 0
                    p0 = b * PROJ_PER_B + g * (2 * CT) + CT
                    sm = (b * MG + g) * (TT - 1)
                    held(dve, inter_done, START + (b * MG + g) * TT)
                    dve.memset(state[:], 0.0).then_inc(state_ready, 1)
                    for c in range(TT):
                        it = (b * MG + g) * TT + c
                        start = first and c == 0
                        if not start:
                            masked(it, sm + c)
                        turned = start
                        while uses[at][0] == "proj":
                            n = uses[at][1]
                            s1 = 1 if n < CT else 0
                            convolve(p0 + n, n)
                            if not turned:
                                turned_lo(it - 1)
                                turned = True
                            if n % CT:
                                twice_silu(p0 + (n - 1), n - 1, s1)
                            if n % CT == CT - 1:
                                twice_silu(p0 + n, n, s1)
                            at += 1
                        if start:
                            masked(it, sm)
                        if not turned:
                            turned_lo(it - 1)
                        dve.wait_ge(gate_th, it + 1)
                        dve.scalar_tensor_tensor(out=g_th[:], in0=g_th[:], scalar=1.0, in1=bank[at % 2],
                                                 op0=ALU.add, op1=ALU.mult).then_inc(gate_used, 1)
                        at += 1
                        dve.wait_ge(inter_done, START + it + 1)
                        dve.tensor_tensor(by_head(yv[:]), by_head(bank[6]),
                                          gt[:, EC, c, :].unsqueeze(2).broadcast_to([P, HPG, MP]), ALU.mult
                                          ).then_inc(inter_used, 1)
                        dve.drain()
                        dve.wait_ge(intra_done, START + it + 1)
                        dve.tensor_tensor(yv[:], yv[:], bank[7], ALU.add)
                        dve.drain()
                        dve.wait_ge(pool_x, START + it + 1)
                        dve.tensor_tensor(yv[:], yv[:], xd[:], ALU.add).then_inc(y_ready, 1)
                        if c == 1:
                            tables(g, 1)
                        if c == TT - 2 and not last:
                            tables(g + 1, 0)
                        if not start:
                            gather(it - 1, (c - 1) % TT)
                        if c < TT - 1:
                            dve.wait_ge(st_mm, START + sm + (c + 1))
                            dve.wait_ge(state_dec, sm + (c + 1))
                            dve.tensor_tensor(state[:], state[:], bank[6], ALU.add).then_inc(state_ready, 1)
                        dve.wait_ge(rg_ready, it + 1)
                        dve.scalar_tensor_tensor(out=yn[:], in0=yv[:], scalar=rg[:], in1=g_th[:],
                                                 op0=ALU.mult, op1=ALU.mult).then_inc(yn_ready, 1)

                tables(0, 0)
                for n in range(CT):
                    pi = b * PROJ_PER_B + n
                    convolve(pi, n)
                    if n:
                        twice_silu(pi - 1, n - 1, 0)
                twice_silu(b * PROJ_PER_B + (CT - 1), CT - 1, 0)
                enter(dve, b, MAMBA)
                held(dve, m_zero, b + 1)
                m_group(0, True, False)
                with dve.Fori(1, MG - 1) as g:
                    m_group(g, False, False)
                m_group(MG - 1, False, True)
                turned_lo((b + 1) * (MG * TT) - 1)
                gather((b + 1) * (MG * TT) - 1, TT - 1)
                leave(dve, b, MAMBA)
                moments(POST, Y, b * 4 + 2)
                moments(PRE, X, b * 4 + 2)
                norm_lo(b * 4 + 3)
                enter(dve, b, FFN1)
                ffn(b, 1, NF1, False)
                leave(dve, b, FFN1)
                moments(POST, Y, b * 4 + 3)

        @block.gpsimd
        def _(pool):
            pool.memset(zeros[:], 0.0)
            pool.memset(ones[:], 1.0)
            pool.memset(half_neg[:], -0.5)
            for m, v in ((ident, 0.0), (ident_b, 0.0), (mask_qk, 0.0), (quarter, 0.25)):
                pool.memset(m[:], v)
            pool.drain()

            def select(m, src, op, p_step, x_step, fill):
                pool.affine_select(out=m[:], in_=src[:], compare_op=op, fill=fill, base=0,
                                   pattern=[[x_step, P]], channel_multiplier=p_step)

            select(ident, ident, ALU.not_equal, 1, -1, 1.0)
            select(ident_b, ident_b, ALU.not_equal, 1, -1, 1.0)
            select(mask_qk, mask_qk, ALU.is_ge, 1, -1, NEG)
            select(quarter, quarter, ALU.is_ge, -1, 1, 0.0)
            select(upto, ones, ALU.is_ge, -1, 1, 0.0)
            select(after, ones, ALU.is_gt, 1, -1, 0.0)
            pool.drain()
            pool.tensor_copy(after_r[:], after[:])
            for semaphore in started:
                pool.drain().then_inc(semaphore, START)
            pool.drain().then_inc(consts_ready, 1)

            def split(hi, lo, raw):
                pool.tensor_scalar(hi, raw, 1.0, 1.0, ALU.mult, ALU.mult)
                pool.drain()
                return pool.tensor_tensor(lo, raw, hi.bitcast(F32), ALU.subtract)

            def root(kind, e, h):
                own = slice(h * CPH, (h + 1) * CPH)
                pool.wait_ge(var_ready[kind], e * 2 + h + 1)
                pool.tensor_tensor(rstd[:, kind, own], var_eps[:, kind, own], half_neg[:, 0:CPH], ALU.pow)
                pool.drain()
                pool.tensor_tensor(shift[:, kind, own], neg_mean[:, kind, own], rstd[:, kind, own], ALU.mult
                                   ).then_inc(rstd_ready[kind], 1)

            def add_normed(e, e_next):
                root(POST, e, 0)
                root(POST, e, 1)
                for i in range(TT):
                    pool.wait_ge(y_normed, e * TT + i + 1)
                    pool.tensor_tensor(X[:, i, :], X[:, i, :], Y[:, i, :], ALU.add).then_inc(x_added, 1)
                    if e_next is not None and i == CPH + 1:
                        root(PRE, e_next, 0)
                if e_next is not None:
                    root(PRE, e_next, 1)
                pool.drain()

            def ffn(b, i, n, lowrank):
                f = F[i]
                pool.memset(Y[:], 0.0).then_inc(f["y_zero"], 1)

                def split_tile(p, par, first=False):
                    t = b * n + p * 2 + par
                    for m in range(3):
                        if lowrank:
                            held(pool, f["weff"], t * 3 + (m + 1))
                        elif m == 0:
                            held(pool, f[f"raw_in{par}"], (b * ((n + 1 - par) // 2) + p) * 16 + 16)
                        if not first:
                            if m == 0:
                                held(pool, f["u_done"], t * 2 - 2)
                            if m == 2:
                                held(pool, f["dn_done"], t * TT - TT)
                        split(f_hi[par][:, m, :], f_lo[par][:, m, :], f_raw[par][:, m, :]).then_inc(f["w_ready"], 1)

                split_tile(0, 0, True)
                split_tile(0, 1, True)
                with pool.Fori(1, n // 2) as p:
                    for par in range(2):
                        split_tile(p, par)
                if n % 2:
                    split_tile(n // 2, 0)

            with pool.Fori(0, B) as b:
                root(PRE, b * 4, 0)
                root(PRE, b * 4, 1)
                enter(pool, b, ATT)
                ring = 0
                for what, *arg in ORDER:
                    if what == "proj":
                        f, use = arg
                        ring += 1
                        if use == 3:
                            wqk_last_use = ring
                        if use > 0:
                            continue
                        held(pool, wqk_in, (b * (NQ // 2) + f + 1) * 32)
                        if f > 0:
                            held(pool, ring_done, b * RING + wqk_last_use)
                        split(wqk_hi[:], wqk_lo[:], wqk_raw[:]).then_inc(wqk_ready, 2)
                    elif what == "values_in":
                        if arg == [0]:
                            held(pool, wv_in, b * 32 + 32)
                            split(wv_hi[:], wv_lo[:], wv_raw[:]).then_inc(wv_ready, 1)
                        ring += 1
                    elif what in ("piece", "maxima", "turn"):
                        ring += 1
                    elif what == "scores":
                        t, n, p = arg
                        s, j = STEPS[n]
                        if j * P >= s * HALF:
                            held(pool, exp_done[p], START + b * (NQ * NS) + (t * NS + n) + 1)
                            own = probs[n % 2][:, 2 * p:2 * p + 2, 0:P]
                            pool.affine_select(out=own, in_=own, compare_op=ALU.is_ge, fill=0.0, base=0,
                                               pattern=[[0, 2], [1, P]], channel_multiplier=-1
                                               ).then_inc(masked[p], 1)
                        if (t, n, p) == (NQ - 1, NS // 2, 0):
                            held(pool, wo_in, b * 32 + 32)
                            split(wo_hi[:], wo_lo[:], wo_raw[:]).then_inc(wo_ready, 1)
                leave(pool, b, ATT)
                enter(pool, b, PROJ)
                leave(pool, b, PROJ)
                add_normed(b * 4, b * 4 + 1)
                enter(pool, b, FFN0)
                ffn(b, 0, NF0, True)
                leave(pool, b, FFN0)
                add_normed(b * 4 + 1, b * 4 + 2)
                enter(pool, b, STEPS_DT)
                held(pool, dt_w_in, (b + 1) * 64)
                split(wdt_hi[:], wdt_lo[:], wdt_raw[:]).then_inc(dt_w_ready, 1)
                leave(pool, b, STEPS_DT)

                pool.memset(Y[:], 0.0).then_inc(m_zero, 1)

                def split_lo(hi, lo, n, g):
                    pool.wait_ge(m_hi, b * (MG * W_PER_G) + g * W_PER_G + (n + 1))
                    pool.tensor_tensor(lo, m_raw[:, n % 2, :], hi.bitcast(F32), ALU.subtract).then_inc(m_split, 1)

                def decay_terms(c, it):
                    pool.wait_ge(d_done, START + it)
                    for dst, kind in ((au_hi, AHI), (au_lo, ALO)):
                        r = pool.tensor_tensor(dst[:], upto[:].unsqueeze(1).broadcast_to([P, HPG, P]),
                                               gt[:, kind, c, :].unsqueeze(2).broadcast_to([P, HPG, P]), ALU.mult)
                    r.then_inc(au_ready, 1)

                def by_head(t):
                    return t.rearrange("p (h d) -> p h d", d=MP)

                def per_head(t):
                    return t.unsqueeze(2).broadcast_to([P, HPG, MP])

                def m_group(g, first, last):
                    sm = (b * MG + g) * (TT - 1)
                    for c in range(TT):
                        it = (b * MG + g) * TT + c
                        pool.wait_ge(x_tm_ready, START + it + 1)
                        pool.wait_ge(intra_done, START + it)
                        pool.tensor_tensor(by_head(xdt[:]), by_head(x_tm[:]), per_head(gt[:, DTH, c, :]), ALU.mult)
                        if c < TT - 1:
                            pool.wait_ge(st_mm, START + sm + c)
                            pool.tensor_tensor(by_head(xw[:]), by_head(x_tm[:]), per_head(gt[:, WE, c, :]), ALU.mult)
                        pool.wait_ge(y_ready, START + it)
                        pool.tensor_tensor(by_head(xd[:]), by_head(x_tm[:]), per_head(gd[:, c // CPH, :]), ALU.mult
                                           ).then_inc(pool_x, 1)
                        if c == 1:
                            for k in range(2, XT):
                                split_lo(wy_hi[:, k, :], wy_lo[:, k, :], CT + KT + k, g)
                        if c == 0 and not first:
                            for k in range(2, KT):
                                split_lo(wg_hi[:, k, :], wg_lo[:, k, :], CT + k, g)
                        if c < TT - 1:
                            pool.wait_ge(state_ready, it + 1)
                            pool.wait_ge(inter_done, START + it + 1)
                            pool.tensor_tensor(by_head(state[:]), by_head(state[:]), per_head(gt[:, ED, c, :]),
                                               ALU.mult).then_inc(state_dec, 1)
                            if c == CPH - 1:
                                pool.wait_ge(gt_ready, (b * MG + g) * 2 + 2)
                            decay_terms(c + 1, it + 1)
                        elif not last:
                            pool.wait_ge(gt_ready, (b * MG + g) * 2 + 3)
                            decay_terms(0, it + 1)
                        held(pool, ss_ready, START + it + 1)
                        pool.tensor_scalar(rg[:], ss[:], 4.0 / GI, 4 * EPS, ALU.mult, ALU.add)
                        pool.drain()
                        pool.tensor_tensor(rg[:], rg[:], half_neg[:, 0:1], ALU.pow).then_inc(rg_ready, 1)
                        if c == 0:
                            for k in range(2):
                                split_lo(wy_hi[:, k, :], wy_lo[:, k, :], CT + KT + k, g)
                        if not last:
                            if c == TT - 1:
                                for k in range(2):
                                    split_lo(wg_hi[:, k, :], wg_lo[:, k, :], CT + k, g + 1)
                            for ft in SPLIT_AT.get(c, ()):
                                split_lo(wx_hi[:, ft, :], wx_lo[:, ft, :], ft, g + 1)

                for ft in range(CT):
                    split_lo(wx_hi[:, ft, :], wx_lo[:, ft, :], ft, 0)
                for k in range(KT):
                    split_lo(wg_hi[:, k, :], wg_lo[:, k, :], CT + k, 0)
                enter(pool, b, MAMBA)
                pool.wait_ge(gt_ready, b * (2 * MG) + 1)
                decay_terms(0, b * (MG * TT))
                m_group(0, True, False)
                with pool.Fori(1, MG - 1) as g:
                    m_group(g, False, False)
                m_group(MG - 1, False, True)
                leave(pool, b, MAMBA)
                add_normed(b * 4 + 2, b * 4 + 3)
                enter(pool, b, FFN1)
                ffn(b, 1, NF1, False)
                leave(pool, b, FFN1)
                add_normed(b * 4 + 3, None)


def kernel(**inputs):
    import numpy as np
    import concourse.bacc as bacc
    from concourse.bass_utils import run_bass_kernel_spmd as run

    a = {k: np.asarray(v) for k, v in inputs.items()}

    def by_out(w):
        n = w.shape[0] // P
        return w.reshape(n, P, KT, P).transpose(0, 3, 2, 1).reshape(n, P, KT * P)

    def by_in(w):
        return w.T.reshape(-1, P, w.shape[0])

    def rows(w, n):
        return np.pad(w, ((0, n - w.shape[0]), (0, 0)))

    def everywhere(v):
        return np.broadcast_to(v[None, :], (P, v.shape[0]))

    wq, wk = by_out(a["L0_attn_Wq"]), by_out(a["L0_attn_Wk"])
    qk = np.stack([wq, wk], 1).reshape(2 * KT, P, D)
    arrays = {
        "x": a["L0_attn_x"],
        "w_attn": np.concatenate([by_in(a["L0_attn_Wv"]), qk, by_in(a["L0_attn_Wo"])]),
        "qk_bias": np.stack([a["L0_attn_bq"].reshape(KT, P), a["L0_attn_bk"].reshape(KT, P)], 2),
        "bv": everywhere(a["L0_attn_bv"]),
        "bo": everywhere(a["L0_attn_bo"]),
        "w_ffn0": np.stack([by_out(a["L0_ffn_gate_w"]), by_out(a["L0_ffn_up_w"]), by_in(a["L0_ffn_down_w"])], 1),
        "lr0": np.concatenate([a["L0_ffn_gate_su"].reshape(NF0, P, RANK).transpose(0, 2, 1),
                               a["L0_ffn_up_su"].reshape(NF0, P, RANK).transpose(0, 2, 1),
                               a["L0_ffn_down_sv"].reshape(RANK, NF0, P).transpose(1, 0, 2)], 2),
        "lr0_const": np.concatenate([a["L0_ffn_gate_sv"], a["L0_ffn_up_sv"], a["L0_ffn_down_su"].T], 1),
    }
    gate_up = a["L1_ffn_w_gate_up"]
    half = gate_up.shape[0] // 2
    arrays["w_ffn1"] = np.stack([by_out(rows(gate_up[:half], NF1 * P)), by_out(rows(gate_up[half:], NF1 * P)),
                                 by_in(rows(a["L1_ffn_w_down"].T, NF1 * P).T)], 1)

    inner, gn = MH * MP, MG * MN
    proj = a["L1_attn_in_proj_w"]

    def channels(v):
        rest = v.shape[1:]
        return np.concatenate([v[:inner].reshape(MG, XT, P, *rest), v[inner:inner + gn].reshape(MG, 1, P, *rest),
                               v[inner + gn:].reshape(MG, 1, P, *rest)], 1)

    xbc_w = channels(proj[inner:2 * inner + 2 * gn])
    arrays["w_mamba"] = np.concatenate([
        by_out(xbc_w.reshape(-1, D)).reshape(MG, CT, P, D),
        proj[:inner].reshape(MG, GI, KT, P).transpose(0, 2, 3, 1),
        a["L1_attn_out_proj_w"].T.reshape(MG, XT, P, D)], 1)
    arrays["w_dt"] = proj[-MH:].T.reshape(KT, P, MH).transpose(1, 0, 2)
    taps = np.concatenate([channels(a["L1_attn_conv_weight"]), channels(a["L1_attn_conv_bias"][:, None])], 3)
    arrays["conv_par"] = np.concatenate([taps.transpose(0, 2, 1, 3).reshape(MG, P, CT * (MK + 1)),
                                         a["L1_attn_norm_weight"].reshape(MG, XT, P).transpose(0, 2, 1)], 2)
    arrays["dt_bias"] = everywhere(a["L1_attn_dt_bias"])
    arrays["a_log"] = everywhere(a["L1_attn_A_log"])
    arrays["d_skip"] = everywhere(a["L1_attn_D"])

    nc = bacc.Bacc("TRN2", target_bir_lowering=False, num_devices=1)
    feed, args = {}, {}
    for name, v in arrays.items():
        v = np.ascontiguousarray(v)
        feed[f"in_{name}"] = v
        args[name] = nc.dram_tensor(f"in_{name}", v.shape, mybir.dt.from_np(v.dtype), kind="ExternalInput").ap()
    args["out"] = nc.dram_tensor("out_y", (B, L, D), F32, kind="ExternalOutput").ap()
    build(nc, **args)
    r = run(nc, [feed], core_ids=[0])
    return r.results[0]["out_y"]
```
